# Optimizing a Trainium2 kernel written in Bass

```python
import numpy as np
import jax
import jax.numpy as jnp

def _softmax(x, axis=-1):
    return jax.nn.softmax(x, axis=axis)

def _gelu(x):
    return jax.nn.gelu(x, approximate=True)

def _silu(x):
    return jax.nn.silu(x)

def _sigmoid(x):
    return jax.nn.sigmoid(x)

def _layernorm(x, axis=-1, eps=1e-05):
    m = jnp.mean(x, axis=axis, keepdims=True)
    v = jnp.var(x, axis=axis, keepdims=True)
    return (x - m) / jnp.sqrt(v + eps)

def _scatter_add(tgt, idx, src, axis=0):
    return tgt.at[idx].add(src)

def _segment_sum(src, seg, n):
    return jax.ops.segment_sum(src, seg, n)
kernel_name = 'mk_perceiver_d4_seqx_r8_112761'

def setup_inputs(seed: int=0):
    np.random.seed(seed)
    _w = jnp.asarray

    def _rec_inputs():
        import jax
        import jax.numpy as jnp
        _rk = jax.random.key(seed)
        x = 0.002226 + 0.9996 * jax.random.normal(jax.random.fold_in(_rk, 1), (64, 64, 128), jnp.float32)
        _lenS = 64 - jax.random.randint(jax.random.fold_in(_rk, 7), (64,), 0, max(1, 64 // 4) + 1, jnp.int32)
        _lenS2 = 128 - jax.random.randint(jax.random.fold_in(_rk, 8), (64,), 0, max(1, 128 // 4) + 1, jnp.int32)
        _ctx_1024P = jax.random.normal(jax.random.fold_in(_rk, 11), (64, 16, 128), jnp.float32)
        _ctx_1024c = jax.random.dirichlet(jax.random.fold_in(_rk, 511), 0.3 * jnp.ones((16,), jnp.float32), (64, 128))
        _ctx_1024t = jnp.einsum('bsk,bkd->bsd', _ctx_1024c, _ctx_1024P)
        _ctx_1024t = _ctx_1024t * jax.lax.rsqrt(jnp.mean(jnp.square(_ctx_1024t)) + 1e-12) * 0.953939
        ctx_1024 = -0.000125008 + 0.999885 * (_ctx_1024t + 0.3 * jax.random.normal(jax.random.fold_in(_rk, 611), (64, 128, 128), jnp.float32))
        return (x, ctx_1024)
    x, ctx_1024 = _rec_inputs()

    def _L0_xattn_setup():
        import jax, jax.numpy as jnp
        import numpy as np
        DIM = 128
        HEADS = 16
        DIM_HEAD = 64
        INNER = HEADS * DIM_HEAD

        def _layernorm(x, w, b, eps=1e-05):
            mu = jnp.mean(x, axis=-1, keepdims=True)
            var = jnp.var(x, axis=-1, keepdims=True)
            return (x - mu) * jax.lax.rsqrt(var + eps) * w + b
        key = jax.random.key(seed)
        ks = jax.random.split(key, 12)
        b, n, m = (8, 512, 64)
        s = lambda fan_in: 1.0 / np.sqrt(fan_in)
        return {'x': jax.random.normal(ks[0], (b, n, DIM), jnp.float32), 'latents': jax.random.normal(ks[1], (b, m, DIM), jnp.float32), 'ln_media_w': jnp.ones((DIM,), jnp.float32), 'ln_media_b': jnp.zeros((DIM,), jnp.float32), 'ln_lat_w': jnp.ones((DIM,), jnp.float32), 'ln_lat_b': jnp.zeros((DIM,), jnp.float32), 'Wq': jax.random.normal(ks[2], (DIM, INNER), jnp.float32) * s(DIM), 'bq': jnp.zeros((INNER,), jnp.float32), 'Wkv': jax.random.normal(ks[3], (DIM, 2 * INNER), jnp.float32) * s(DIM), 'bkv': jnp.zeros((2 * INNER,), jnp.float32), 'Wout': jax.random.normal(ks[4], (INNER, DIM), jnp.float32) * s(INNER), 'bout': jnp.zeros((DIM,), jnp.float32)}
    _L0_xattn_all = _L0_xattn_setup()
    _L0_xattn_in = {k: v for k, v in _L0_xattn_all.items() if k in ('ln_media_w', 'ln_media_b', 'ln_lat_w', 'ln_lat_b', 'Wq', 'bq', 'Wkv', 'bkv', 'Wout', 'bout')}
    del _L0_xattn_all

    def _L0_attn_setup():
        import jax, jax.numpy as jnp
        import numpy as np
        DIM = 128
        DIM_INNER = 256
        B, S = (4, 512)

        def heinsen_associative_scan_log(log_coeffs, log_values):
            a_star = jnp.cumsum(log_coeffs, axis=1)
            log_h0_plus_b_star = jax.lax.cumlogsumexp(log_values - a_star, axis=1)
            return jnp.exp(a_star + log_h0_plus_b_star)
        key = jax.random.key(seed)
        k1, k2, k3 = jax.random.split(key, 3)
        x = jax.random.normal(k1, (B, S, DIM), dtype=jnp.float32)
        W_hg = jax.random.normal(k2, (DIM, 2 * DIM_INNER), dtype=jnp.float32) / np.sqrt(DIM)
        W_out = jax.random.normal(k3, (DIM_INNER, DIM), dtype=jnp.float32) / np.sqrt(DIM_INNER)
        return {'x': x, 'W_hg': W_hg, 'W_out': W_out}
    _L0_attn_all = _L0_attn_setup()
    _L0_attn_in = {k: v for k, v in _L0_attn_all.items() if k in ('W_hg', 'W_out')}
    del _L0_attn_all

    def _L0_ffn_setup():
        import jax, jax.numpy as jnp
        import numpy as np
        D_MODEL = 128
        D_OUT = 128
        RANK = 16
        NUM_TRUE = 8
        NUM_NULL = 2
        TOP_K = 2
        SCALING = 32.0 / 16.0
        key = jax.random.key(seed)
        ks = jax.random.split(key, 6)
        x = jax.random.normal(ks[0], (4, 512, D_MODEL), dtype=jnp.float32)
        base_w = jax.random.normal(ks[1], (D_OUT, D_MODEL), dtype=jnp.float32) / np.sqrt(D_MODEL)
        base_b = jax.random.normal(ks[2], (D_OUT,), dtype=jnp.float32) * 0.01
        gate_w = jax.random.normal(ks[3], (NUM_TRUE + NUM_NULL, D_MODEL), dtype=jnp.float32) / np.sqrt(D_MODEL)
        lora_A = jax.random.normal(ks[4], (NUM_TRUE, RANK, D_MODEL), dtype=jnp.float32) / np.sqrt(D_MODEL)
        lora_B = jax.random.normal(ks[5], (NUM_TRUE, D_OUT, RANK), dtype=jnp.float32) * 0.01
        return {'x': x, 'base_w': base_w, 'base_b': base_b, 'gate_w': gate_w, 'lora_A': lora_A, 'lora_B': lora_B}
    _L0_ffn_all = _L0_ffn_setup()
    _L0_ffn_in = {k: v for k, v in _L0_ffn_all.items() if k in ('base_w', 'base_b', 'gate_w', 'lora_A', 'lora_B')}
    del _L0_ffn_all

    def _L1_xattn_setup():
        import jax, jax.numpy as jnp
        import numpy as np
        D = 128
        B, SQ, SKV = (4, 256, 256)
        key = jax.random.key(seed)
        ks = jax.random.split(key, 8)
        s = 1.0 / np.sqrt(D)
        return {'x': jax.random.normal(ks[0], (B, SQ, D), jnp.float32), 'context': jax.random.normal(ks[1], (B, SKV, D), jnp.float32), 'Wq': jax.random.uniform(ks[2], (D, D), jnp.float32, -s, s), 'bq': jnp.zeros((D,), jnp.float32), 'Wk': jax.random.uniform(ks[3], (D, D), jnp.float32, -s, s), 'bk': jnp.zeros((D,), jnp.float32), 'Wv': jax.random.uniform(ks[4], (D, D), jnp.float32, -s, s), 'bv': jnp.zeros((D,), jnp.float32)}
    _L1_xattn_all = _L1_xattn_setup()
    _L1_xattn_in = {k: v for k, v in _L1_xattn_all.items() if k in ('Wq', 'bq', 'Wk', 'bk', 'Wv', 'bv')}
    del _L1_xattn_all

    def _L1_attn_setup():
        import jax, jax.numpy as jnp
        import numpy as np
        NUM_HEADS = 16
        EPS = 1e-05
        key = jax.random.key(seed)
        k1, k2, k3 = jax.random.split(key, 3)
        b, n, d = (2, 256, 128)
        x = jax.random.normal(k1, (b, n, d), dtype=jnp.float32)
        wqkv = jax.random.normal(k2, (d, 3 * d), dtype=jnp.float32) * (1.0 / np.sqrt(d))
        wo = jax.random.normal(k3, (d, d), dtype=jnp.float32) * (1.0 / np.sqrt(d))
        return {'x': x, 'wqkv': wqkv, 'wo': wo}
    _L1_attn_all = _L1_attn_setup()
    _L1_attn_in = {k: v for k, v in _L1_attn_all.items() if k in ('wqkv', 'wo')}
    del _L1_attn_all

    def _L1_ffn_setup():
        import jax, jax.numpy as jnp
        import numpy as np
        DIM = 128
        N_HEADS = 16
        N_KV_HEADS = 4
        HEAD_DIM = DIM // N_HEADS
        N_REP = N_HEADS // N_KV_HEADS
        N_EXPERTS = 4
        TOP_K = 2
        HIDDEN = 3 * DIM
        EPS = 1.1920928955078125e-07

        def _rmsnorm(x, g):
            var = jnp.mean(jnp.square(x), axis=-1, keepdims=True)
            return x * jax.lax.rsqrt(var + EPS) * g

        def _rotate_half(x):
            x1, x2 = jnp.split(x, 2, axis=-1)
            return jnp.concatenate([-x2, x1], axis=-1)

        def _rope_tables(S):
            inv_freq = 1.0 / 10000.0 ** (jnp.arange(0, HEAD_DIM, 2, dtype=jnp.float32) / HEAD_DIM)
            freqs = jnp.arange(S, dtype=jnp.float32)[:, None] * inv_freq[None, :]
            emb = jnp.concatenate([freqs, freqs], axis=-1)
            return (jnp.cos(emb), jnp.sin(emb))

        def _attention(x, wq, wk, wv, wo):
            B, S, D = x.shape
            q = (x @ wq).reshape(B, S, N_HEADS, HEAD_DIM).transpose(0, 2, 1, 3)
            k = (x @ wk).reshape(B, S, N_KV_HEADS, HEAD_DIM).transpose(0, 2, 1, 3)
            v = (x @ wv).reshape(B, S, N_KV_HEADS, HEAD_DIM).transpose(0, 2, 1, 3)
            cos, sin = _rope_tables(S)
            q = q * cos + _rotate_half(q) * sin
            k = k * cos + _rotate_half(k) * sin
            k = jnp.repeat(k, N_REP, axis=1)
            v = jnp.repeat(v, N_REP, axis=1)
            scores = jnp.einsum('bhqd,bhkd->bhqk', q, k) / jnp.sqrt(jnp.float32(HEAD_DIM))
            causal = jnp.tril(jnp.ones((S, S), dtype=bool))
            scores = jnp.where(causal, scores, -jnp.inf)
            attn = jax.nn.softmax(scores, axis=-1)
            out = jnp.einsum('bhqk,bhkd->bhqd', attn, v)
            return out.transpose(0, 2, 1, 3).reshape(B, S, D) @ wo

        def _moe(x, gate, w1, w2, w3):
            B, S, D = x.shape
            xf = x.reshape(-1, D)
            probs = jax.nn.softmax(xf @ gate, axis=-1)
            w, idx = jax.lax.top_k(probs, TOP_K)
            w = w / jnp.sum(w, axis=-1, keepdims=True)
            oh = jax.nn.one_hot(idx, N_EXPERTS, dtype=xf.dtype)
            comb = jnp.einsum('nk,nke->ne', w, oh)
            out = jnp.zeros_like(xf)
            for e in range(N_EXPERTS):
                h = jax.nn.silu(xf @ w1[e]) * (xf @ w3[e])
                out = out + comb[:, e:e + 1] * (h @ w2[e])
            return out.reshape(B, S, D)
        key = jax.random.key(seed)
        ks = jax.random.split(key, 12)
        s = 0.02
        B, S = (2, 256)
        return {'x': jax.random.normal(ks[0], (B, S, DIM), jnp.float32), 'g1': jnp.ones((DIM,), jnp.float32), 'g2': jnp.ones((DIM,), jnp.float32), 'wq': jax.random.normal(ks[1], (DIM, N_HEADS * HEAD_DIM), jnp.float32) * s, 'wk': jax.random.normal(ks[2], (DIM, N_KV_HEADS * HEAD_DIM), jnp.float32) * s, 'wv': jax.random.normal(ks[3], (DIM, N_KV_HEADS * HEAD_DIM), jnp.float32) * s, 'wo': jax.random.normal(ks[4], (N_HEADS * HEAD_DIM, DIM), jnp.float32) * s, 'gate': jax.random.normal(ks[5], (DIM, N_EXPERTS), jnp.float32) * s, 'w1': jax.random.normal(ks[6], (N_EXPERTS, DIM, HIDDEN), jnp.float32) * s, 'w2': jax.random.normal(ks[7], (N_EXPERTS, HIDDEN, DIM), jnp.float32) * s, 'w3': jax.random.normal(ks[8], (N_EXPERTS, DIM, HIDDEN), jnp.float32) * s}
    _L1_ffn_all = _L1_ffn_setup()
    _L1_ffn_in = {k: v for k, v in _L1_ffn_all.items() if k in ('g1', 'g2', 'wq', 'wk', 'wv', 'wo', 'gate', 'w1', 'w2', 'w3')}
    del _L1_ffn_all

    def _L2_xattn_setup():
        import jax, jax.numpy as jnp
        import numpy as np
        D_MODEL = 128
        D_HEAD = 64
        NHEADS = 8
        IN_DIM = D_HEAD * NHEADS
        EPS = 1e-05

        def layernorm(x, g, b):
            mu = jnp.mean(x, axis=-1, keepdims=True)
            var = jnp.var(x, axis=-1, keepdims=True)
            return (x - mu) * jax.lax.rsqrt(var + EPS) * g + b
        key = jax.random.key(seed)
        ks = jax.random.split(key, 8)
        B, M, L = (4, 1024, 64)
        x = jax.random.normal(ks[0], (B, M, D_MODEL), dtype=jnp.float32)
        latents = jax.random.normal(ks[1], (B, L, D_MODEL), dtype=jnp.float32)
        s = 1.0 / np.sqrt(D_MODEL)
        Wq = jax.random.normal(ks[2], (D_MODEL, IN_DIM), dtype=jnp.float32) * s
        Wkv = jax.random.normal(ks[3], (D_MODEL, 2 * IN_DIM), dtype=jnp.float32) * s
        Wout = jax.random.normal(ks[4], (IN_DIM, D_MODEL), dtype=jnp.float32) * (1.0 / np.sqrt(IN_DIM))
        gm = jnp.ones((D_MODEL,), jnp.float32)
        bm = jnp.zeros((D_MODEL,), jnp.float32)
        gl = jnp.ones((D_MODEL,), jnp.float32)
        bl = jnp.zeros((D_MODEL,), jnp.float32)
        return {'x': x, 'latents': latents, 'Wq': Wq, 'Wkv': Wkv, 'Wout': Wout, 'gm': gm, 'bm': bm, 'gl': gl, 'bl': bl}
    _L2_xattn_all = _L2_xattn_setup()
    _L2_xattn_in = {k: v for k, v in _L2_xattn_all.items() if k in ('Wq', 'Wkv', 'Wout', 'gm', 'bm', 'gl', 'bl')}
    del _L2_xattn_all

    def _L2_attn_setup():
        import jax, jax.numpy as jnp
        import numpy as np
        B, L, C, H, W = (4, 512, 128, 16, 64)
        D = C // H
        STRIDE = W // 2

        def _local_attention(x, w_qkv, b_qkv, w_out, b_out):
            b, l, c = x.shape
            pad = -l % W
            x = jnp.pad(x, ((0, 0), (0, pad), (0, 0)))
            lp = l + pad
            qkv = (x @ w_qkv + b_qkv).reshape(b, lp, 3, H, D).transpose(2, 0, 3, 1, 4)
            q, k, v = (qkv[0], qkv[1], qkv[2])
            nw = (lp - W) // STRIDE + 1
            idx = jnp.arange(nw)[:, None] * STRIDE + jnp.arange(W)[None, :]
            qw = q[:, :, idx, :]
            kw = k[:, :, idx, :]
            vw = v[:, :, idx, :]
            scores = jnp.einsum('bhnqd,bhnkd->bhnqk', qw, kw) / jnp.sqrt(jnp.float32(D))
            probs = jax.nn.softmax(scores, axis=-1)
            ow = jnp.einsum('bhnqk,bhnkd->bhnqd', probs, vw)
            o = ow.transpose(0, 2, 3, 1, 4).reshape(b, nw * W, c)
            o = o @ w_out + b_out
            return o[:, :l, :]
        key = jax.random.key(seed)
        k0, k1, k2 = jax.random.split(key, 3)
        s = 0.02
        return {'x': jax.random.normal(k0, (B, L, C), jnp.float32), 'w_qkv': jax.random.normal(k1, (C, 3 * C), jnp.float32) * s, 'b_qkv': jnp.zeros((3 * C,), jnp.float32), 'w_out': jax.random.normal(k2, (C, C), jnp.float32) * s, 'b_out': jnp.zeros((C,), jnp.float32)}
    _L2_attn_all = _L2_attn_setup()
    _L2_attn_in = {k: v for k, v in _L2_attn_all.items() if k in ('w_qkv', 'b_qkv', 'w_out', 'b_out')}
    del _L2_attn_all

    def _L2_ffn_setup():
        import jax, jax.numpy as jnp
        import numpy as np
        key = jax.random.key(seed)
        ks = jax.random.split(key, 5)
        B, T, D, E = (4, 256, 128, 8)
        inputs = jax.random.normal(ks[0], (B, T, D), dtype=jnp.float32)
        Wr = jax.random.normal(ks[1], (D, E), dtype=jnp.float32) * 0.02
        br = jnp.zeros((E,), dtype=jnp.float32)
        W1 = jax.random.normal(ks[2], (E, D, D), dtype=jnp.float32) * 0.02
        b1 = jnp.zeros((E, D), dtype=jnp.float32)
        W2 = jax.random.normal(ks[3], (E, D, D), dtype=jnp.float32) * 0.02
        b2 = jnp.zeros((E, D), dtype=jnp.float32)
        return {'inputs': inputs, 'Wr': Wr, 'br': br, 'W1': W1, 'b1': b1, 'W2': W2, 'b2': b2}
    _L2_ffn_all = _L2_ffn_setup()
    _L2_ffn_in = {k: v for k, v in _L2_ffn_all.items() if k in ('Wr', 'br', 'W1', 'b1', 'W2', 'b2')}
    del _L2_ffn_all

    def _L3_xattn_setup():
        import jax, jax.numpy as jnp
        import numpy as np
        D1, D2, D3 = (128, 128, 128)
        key = jax.random.key(seed)
        k1, k2, kw, kb = jax.random.split(key, 4)
        x1 = jax.random.normal(k1, (8, 256, D1), dtype=jnp.float32)
        x2 = jax.random.normal(k2, (8, 256, D2), dtype=jnp.float32)
        bound = 1.0 / np.sqrt(D1 + D2)
        W = jax.random.uniform(kw, (D3, D1 + D2), minval=-bound, maxval=bound, dtype=jnp.float32)
        b = jax.random.uniform(kb, (D3,), minval=-bound, maxval=bound, dtype=jnp.float32)
        return {'x1': x1, 'x2': x2, 'W': W, 'b': b}
    _L3_xattn_all = _L3_xattn_setup()
    _L3_xattn_in = {k: v for k, v in _L3_xattn_all.items() if k in ('W', 'b')}
    del _L3_xattn_all

    def _L3_attn_setup():
        import jax, jax.numpy as jnp
        from jax import lax
        import numpy as np
        B, S, D = (4, 256, 128)
        D_INNER, D_STATE, D_CONV = (256, 16, 4)

        def silu(v):
            return v * jax.nn.sigmoid(v)
        key = jax.random.key(seed)
        ks = jax.random.split(key, 7)
        return {'x': jax.random.normal(ks[0], (B, S, D), jnp.float32), 'w_in': jax.random.normal(ks[1], (D, 2 * D_INNER), jnp.float32) * 0.02, 'conv_w': jax.random.normal(ks[2], (D_INNER, 1, D_CONV), jnp.float32) * 0.1, 'conv_b': jax.random.normal(ks[3], (D_INNER,), jnp.float32) * 0.01, 'w_B': jax.random.normal(ks[4], (D_INNER, D_STATE), jnp.float32) * 0.02, 'w_C': jax.random.normal(ks[5], (D_STATE, D_INNER), jnp.float32) * 0.02, 'w_out': jax.random.normal(ks[6], (D_INNER, D), jnp.float32) * 0.02}
    _L3_attn_all = _L3_attn_setup()
    _L3_attn_in = {k: v for k, v in _L3_attn_all.items() if k in ('w_in', 'conv_w', 'conv_b', 'w_B', 'w_C', 'w_out')}
    del _L3_attn_all

    def _L3_ffn_setup():
        import jax, jax.numpy as jnp
        import numpy as np
        H = 128
        I = 128
        E = 8
        key = jax.random.key(seed)
        ks = jax.random.split(key, 8)
        s = 0.02
        x = jax.random.normal(ks[0], (4, 256, H), dtype=jnp.float32)
        Wg = jax.random.normal(ks[1], (H, E), dtype=jnp.float32) * s
        bg = jnp.zeros((E,), dtype=jnp.float32)
        W1 = jax.random.normal(ks[2], (E, H, I), dtype=jnp.float32) * s
        b1 = jnp.zeros((E, I), dtype=jnp.float32)
        W2 = jax.random.normal(ks[3], (E, I, H), dtype=jnp.float32) * s
        b2 = jnp.zeros((E, H), dtype=jnp.float32)
        return {'x': x, 'Wg': Wg, 'bg': bg, 'W1': W1, 'b1': b1, 'W2': W2, 'b2': b2}
    _L3_ffn_all = _L3_ffn_setup()
    _L3_ffn_in = {k: v for k, v in _L3_ffn_all.items() if k in ('Wg', 'bg', 'W1', 'b1', 'W2', 'b2')}
    del _L3_ffn_all
    return {'x': x, 'ctx_1024': ctx_1024, 'L0_xattn_ln_media_w': _L0_xattn_in['ln_media_w'], 'L0_xattn_ln_media_b': _L0_xattn_in['ln_media_b'], 'L0_xattn_ln_lat_w': _L0_xattn_in['ln_lat_w'], 'L0_xattn_ln_lat_b': _L0_xattn_in['ln_lat_b'], 'L0_xattn_Wq': _L0_xattn_in['Wq'], 'L0_xattn_bq': _L0_xattn_in['bq'], 'L0_xattn_Wkv': _L0_xattn_in['Wkv'], 'L0_xattn_bkv': _L0_xattn_in['bkv'], 'L0_xattn_Wout': _L0_xattn_in['Wout'], 'L0_xattn_bout': _L0_xattn_in['bout'], 'L0_attn_W_hg': _L0_attn_in['W_hg'], 'L0_attn_W_out': _L0_attn_in['W_out'], 'L0_ffn_base_w': _L0_ffn_in['base_w'], 'L0_ffn_base_b': _L0_ffn_in['base_b'], 'L0_ffn_gate_w': _L0_ffn_in['gate_w'], 'L0_ffn_lora_A': _L0_ffn_in['lora_A'], 'L0_ffn_lora_B': _L0_ffn_in['lora_B'], 'L1_xattn_Wq': _L1_xattn_in['Wq'], 'L1_xattn_bq': _L1_xattn_in['bq'], 'L1_xattn_Wk': _L1_xattn_in['Wk'], 'L1_xattn_bk': _L1_xattn_in['bk'], 'L1_xattn_Wv': _L1_xattn_in['Wv'], 'L1_xattn_bv': _L1_xattn_in['bv'], 'L1_attn_wqkv': _L1_attn_in['wqkv'], 'L1_attn_wo': _L1_attn_in['wo'], 'L1_ffn_g1': _L1_ffn_in['g1'], 'L1_ffn_g2': _L1_ffn_in['g2'], 'L1_ffn_wq': _L1_ffn_in['wq'], 'L1_ffn_wk': _L1_ffn_in['wk'], 'L1_ffn_wv': _L1_ffn_in['wv'], 'L1_ffn_wo': _L1_ffn_in['wo'], 'L1_ffn_gate': _L1_ffn_in['gate'], 'L1_ffn_w1': _L1_ffn_in['w1'], 'L1_ffn_w2': _L1_ffn_in['w2'], 'L1_ffn_w3': _L1_ffn_in['w3'], 'L2_xattn_Wq': _L2_xattn_in['Wq'], 'L2_xattn_Wkv': _L2_xattn_in['Wkv'], 'L2_xattn_Wout': _L2_xattn_in['Wout'], 'L2_xattn_gm': _L2_xattn_in['gm'], 'L2_xattn_bm': _L2_xattn_in['bm'], 'L2_xattn_gl': _L2_xattn_in['gl'], 'L2_xattn_bl': _L2_xattn_in['bl'], 'L2_attn_w_qkv': _L2_attn_in['w_qkv'], 'L2_attn_b_qkv': _L2_attn_in['b_qkv'], 'L2_attn_w_out': _L2_attn_in['w_out'], 'L2_attn_b_out': _L2_attn_in['b_out'], 'L2_ffn_Wr': _L2_ffn_in['Wr'], 'L2_ffn_br': _L2_ffn_in['br'], 'L2_ffn_W1': _L2_ffn_in['W1'], 'L2_ffn_b1': _L2_ffn_in['b1'], 'L2_ffn_W2': _L2_ffn_in['W2'], 'L2_ffn_b2': _L2_ffn_in['b2'], 'L3_xattn_W': _L3_xattn_in['W'], 'L3_xattn_b': _L3_xattn_in['b'], 'L3_attn_w_in': _L3_attn_in['w_in'], 'L3_attn_conv_w': _L3_attn_in['conv_w'], 'L3_attn_conv_b': _L3_attn_in['conv_b'], 'L3_attn_w_B': _L3_attn_in['w_B'], 'L3_attn_w_C': _L3_attn_in['w_C'], 'L3_attn_w_out': _L3_attn_in['w_out'], 'L3_ffn_Wg': _L3_ffn_in['Wg'], 'L3_ffn_bg': _L3_ffn_in['bg'], 'L3_ffn_W1': _L3_ffn_in['W1'], 'L3_ffn_b1': _L3_ffn_in['b1'], 'L3_ffn_W2': _L3_ffn_in['W2'], 'L3_ffn_b2': _L3_ffn_in['b2']}

def reference(x, ctx_1024, L0_xattn_ln_media_w, L0_xattn_ln_media_b, L0_xattn_ln_lat_w, L0_xattn_ln_lat_b, L0_xattn_Wq, L0_xattn_bq, L0_xattn_Wkv, L0_xattn_bkv, L0_xattn_Wout, L0_xattn_bout, L0_attn_W_hg, L0_attn_W_out, L0_ffn_base_w, L0_ffn_base_b, L0_ffn_gate_w, L0_ffn_lora_A, L0_ffn_lora_B, L1_xattn_Wq, L1_xattn_bq, L1_xattn_Wk, L1_xattn_bk, L1_xattn_Wv, L1_xattn_bv, L1_attn_wqkv, L1_attn_wo, L1_ffn_g1, L1_ffn_g2, L1_ffn_wq, L1_ffn_wk, L1_ffn_wv, L1_ffn_wo, L1_ffn_gate, L1_ffn_w1, L1_ffn_w2, L1_ffn_w3, L2_xattn_Wq, L2_xattn_Wkv, L2_xattn_Wout, L2_xattn_gm, L2_xattn_bm, L2_xattn_gl, L2_xattn_bl, L2_attn_w_qkv, L2_attn_b_qkv, L2_attn_w_out, L2_attn_b_out, L2_ffn_Wr, L2_ffn_br, L2_ffn_W1, L2_ffn_b1, L2_ffn_W2, L2_ffn_b2, L3_xattn_W, L3_xattn_b, L3_attn_w_in, L3_attn_conv_w, L3_attn_conv_b, L3_attn_w_B, L3_attn_w_C, L3_attn_w_out, L3_ffn_Wg, L3_ffn_bg, L3_ffn_W1, L3_ffn_b1, L3_ffn_W2, L3_ffn_b2):
    import jax
    import jax.numpy as jnp

    def _L0_xattn_ref(x, latents, ln_media_w, ln_media_b, ln_lat_w, ln_lat_b, Wq, bq, Wkv, bkv, Wout, bout):
        import jax, jax.numpy as jnp
        import numpy as np
        DIM = 128
        HEADS = 16
        DIM_HEAD = 64
        INNER = HEADS * DIM_HEAD

        def _layernorm(x, w, b, eps=1e-05):
            mu = jnp.mean(x, axis=-1, keepdims=True)
            var = jnp.var(x, axis=-1, keepdims=True)
            return (x - mu) * jax.lax.rsqrt(var + eps) * w + b
        scale = DIM_HEAD ** (-0.5)
        x = _layernorm(x, ln_media_w, ln_media_b)
        lat = _layernorm(latents, ln_lat_w, ln_lat_b)
        q = lat @ Wq + bq
        kv_in = jnp.concatenate([x, lat], axis=1)
        kv = kv_in @ Wkv + bkv
        k, v = jnp.split(kv, 2, axis=-1)
        split = lambda t: t.reshape(t.shape[0], t.shape[1], HEADS, DIM_HEAD).transpose(0, 2, 1, 3)
        q, k, v = (split(q), split(k), split(v))
        sim = jnp.einsum('bhid,bhjd->bhij', q * scale, k)
        sim = sim - jax.lax.stop_gradient(jnp.max(sim, axis=-1, keepdims=True))
        attn = jax.nn.softmax(sim, axis=-1)
        out = jnp.einsum('bhij,bhjd->bhid', attn, v)
        out = out.transpose(0, 2, 1, 3).reshape(out.shape[0], out.shape[2], INNER)
        return out @ Wout + bout

    def _L0_attn_ref(x, W_hg, W_out):
        import jax, jax.numpy as jnp
        import numpy as np
        DIM = 128
        DIM_INNER = 256
        B, S = (4, 512)

        def heinsen_associative_scan_log(log_coeffs, log_values):
            a_star = jnp.cumsum(log_coeffs, axis=1)
            log_h0_plus_b_star = jax.lax.cumlogsumexp(log_values - a_star, axis=1)
            return jnp.exp(a_star + log_h0_plus_b_star)
        hg = jnp.einsum('bsd,de->bse', x, W_hg)
        hidden, gate = jnp.split(hg, 2, axis=-1)
        log_z = jax.nn.log_sigmoid(gate)
        log_coeffs = -jax.nn.softplus(gate)
        hidden_log = jnp.log(jax.nn.relu(hidden) + 0.5)
        log_values = hidden_log + log_z
        h = heinsen_associative_scan_log(log_coeffs, log_values)
        out = jnp.einsum('bse,ed->bsd', h, W_out)
        return out

    def _L0_ffn_ref(x, base_w, base_b, gate_w, lora_A, lora_B):
        import jax, jax.numpy as jnp
        import numpy as np
        D_MODEL = 128
        D_OUT = 128
        RANK = 16
        NUM_TRUE = 8
        NUM_NULL = 2
        TOP_K = 2
        SCALING = 32.0 / 16.0
        xf = x.reshape(-1, x.shape[-1])
        logits = jnp.einsum('td,ed->te', xf, gate_w)
        probs = jax.nn.softmax(logits, axis=-1)
        weights, selected = jax.lax.top_k(probs, TOP_K)
        true_mask = (selected < NUM_TRUE).astype(weights.dtype)
        tw = weights * true_mask
        denom = tw.sum(axis=-1, keepdims=True)
        denom = jnp.where(denom > 0, denom, jnp.ones_like(denom))
        nw = tw / denom
        onehot = jax.nn.one_hot(selected, NUM_TRUE, dtype=nw.dtype)
        ew = jnp.einsum('tk,tke->te', nw, onehot)
        z = jnp.einsum('td,erd->ter', xf, lora_A)
        moe = jnp.einsum('ter,te,eor->to', z, ew, lora_B) * SCALING
        base = jnp.einsum('td,od->to', xf, base_w) + base_b
        out = (base + moe).reshape(x.shape[:-1] + (D_OUT,))
        return out

    def _L1_xattn_ref(x, context, Wq, bq, Wk, bk, Wv, bv):
        import jax, jax.numpy as jnp
        import numpy as np
        D = 128
        B, SQ, SKV = (4, 256, 256)
        Q = x @ Wq + bq
        K = context @ Wk + bk
        V = context @ Wv + bv
        scale = 1.0 / np.sqrt(D).astype(np.float32)
        scores = jnp.einsum('bqd,bkd->bqk', Q, K) * scale
        attn = jax.nn.softmax(scores, axis=-1)
        out = jnp.einsum('bqk,bkd->bqd', attn, V)
        return out

    def _L1_attn_ref(x, wqkv, wo):
        import jax, jax.numpy as jnp
        import numpy as np
        NUM_HEADS = 16
        EPS = 1e-05
        b, n, d = x.shape
        h = NUM_HEADS
        hd = d // h
        qkv = x @ wqkv
        q, k, v = jnp.split(qkv, 3, axis=-1)
        q = jax.nn.relu(q)
        k = jax.nn.relu(k)
        split_heads = lambda t: t.reshape(b, n, h, hd).transpose(0, 2, 1, 3)
        q, k, v = (split_heads(q), split_heads(k), split_heads(v))
        kv = jnp.cumsum(k[..., :, None] * v[..., None, :], axis=2)
        num = jnp.einsum('bhnd,bhnde->bhne', q, kv)
        k_sum = jnp.cumsum(k, axis=2)
        den = jnp.einsum('bhnd,bhnd->bhn', q, k_sum)[..., None] + EPS
        y = num / den
        y = y.transpose(0, 2, 1, 3).reshape(b, n, d)
        return y @ wo

    def _L1_ffn_ref(x, g1, g2, wq, wk, wv, wo, gate, w1, w2, w3):
        import jax, jax.numpy as jnp
        import numpy as np
        DIM = 128
        N_HEADS = 16
        N_KV_HEADS = 4
        HEAD_DIM = DIM // N_HEADS
        N_REP = N_HEADS // N_KV_HEADS
        N_EXPERTS = 4
        TOP_K = 2
        HIDDEN = 3 * DIM
        EPS = 1.1920928955078125e-07

        def _rmsnorm(x, g):
            var = jnp.mean(jnp.square(x), axis=-1, keepdims=True)
            return x * jax.lax.rsqrt(var + EPS) * g

        def _rotate_half(x):
            x1, x2 = jnp.split(x, 2, axis=-1)
            return jnp.concatenate([-x2, x1], axis=-1)

        def _rope_tables(S):
            inv_freq = 1.0 / 10000.0 ** (jnp.arange(0, HEAD_DIM, 2, dtype=jnp.float32) / HEAD_DIM)
            freqs = jnp.arange(S, dtype=jnp.float32)[:, None] * inv_freq[None, :]
            emb = jnp.concatenate([freqs, freqs], axis=-1)
            return (jnp.cos(emb), jnp.sin(emb))

        def _attention(x, wq, wk, wv, wo):
            B, S, D = x.shape
            q = (x @ wq).reshape(B, S, N_HEADS, HEAD_DIM).transpose(0, 2, 1, 3)
            k = (x @ wk).reshape(B, S, N_KV_HEADS, HEAD_DIM).transpose(0, 2, 1, 3)
            v = (x @ wv).reshape(B, S, N_KV_HEADS, HEAD_DIM).transpose(0, 2, 1, 3)
            cos, sin = _rope_tables(S)
            q = q * cos + _rotate_half(q) * sin
            k = k * cos + _rotate_half(k) * sin
            k = jnp.repeat(k, N_REP, axis=1)
            v = jnp.repeat(v, N_REP, axis=1)
            scores = jnp.einsum('bhqd,bhkd->bhqk', q, k) / jnp.sqrt(jnp.float32(HEAD_DIM))
            causal = jnp.tril(jnp.ones((S, S), dtype=bool))
            scores = jnp.where(causal, scores, -jnp.inf)
            attn = jax.nn.softmax(scores, axis=-1)
            out = jnp.einsum('bhqk,bhkd->bhqd', attn, v)
            return out.transpose(0, 2, 1, 3).reshape(B, S, D) @ wo

        def _moe(x, gate, w1, w2, w3):
            B, S, D = x.shape
            xf = x.reshape(-1, D)
            probs = jax.nn.softmax(xf @ gate, axis=-1)
            w, idx = jax.lax.top_k(probs, TOP_K)
            w = w / jnp.sum(w, axis=-1, keepdims=True)
            oh = jax.nn.one_hot(idx, N_EXPERTS, dtype=xf.dtype)
            comb = jnp.einsum('nk,nke->ne', w, oh)
            out = jnp.zeros_like(xf)
            for e in range(N_EXPERTS):
                h = jax.nn.silu(xf @ w1[e]) * (xf @ w3[e])
                out = out + comb[:, e:e + 1] * (h @ w2[e])
            return out.reshape(B, S, D)
        x = x + _attention(_rmsnorm(x, g1), wq, wk, wv, wo)
        x = x + _moe(_rmsnorm(x, g2), gate, w1, w2, w3)
        return x

    def _L2_xattn_ref(x, latents, Wq, Wkv, Wout, gm, bm, gl, bl):
        import jax, jax.numpy as jnp
        import numpy as np
        D_MODEL = 128
        D_HEAD = 64
        NHEADS = 8
        IN_DIM = D_HEAD * NHEADS
        EPS = 1e-05

        def layernorm(x, g, b):
            mu = jnp.mean(x, axis=-1, keepdims=True)
            var = jnp.var(x, axis=-1, keepdims=True)
            return (x - mu) * jax.lax.rsqrt(var + EPS) * g + b
        scale = D_HEAD ** (-0.5)
        xn = layernorm(x, gm, bm)
        ln = layernorm(latents, gl, bl)
        q = ln @ Wq
        kv_input = jnp.concatenate([xn, ln], axis=-2)
        kv = kv_input @ Wkv
        k, v = jnp.split(kv, 2, axis=-1)

        def heads(t):
            B, S, _ = t.shape
            return t.reshape(B, S, NHEADS, D_HEAD).transpose(0, 2, 1, 3)
        q, k, v = (heads(q), heads(k), heads(v))
        q = q / scale
        sim = jnp.einsum('bhid,bhjd->bhij', q, k)
        sim = sim - jax.lax.stop_gradient(jnp.max(sim, axis=-1, keepdims=True))
        attn = jax.nn.softmax(sim, axis=-1)
        out = jnp.einsum('bhij,bhjd->bhid', attn, v)
        B, H, L, dh = out.shape
        out = out.transpose(0, 2, 1, 3).reshape(B, L, H * dh)
        return out @ Wout

    def _L2_attn_ref(x, w_qkv, b_qkv, w_out, b_out):
        import jax, jax.numpy as jnp
        import numpy as np
        B, L, C, H, W = (4, 512, 128, 16, 64)
        D = C // H
        STRIDE = W // 2

        def _local_attention(x, w_qkv, b_qkv, w_out, b_out):
            b, l, c = x.shape
            pad = -l % W
            x = jnp.pad(x, ((0, 0), (0, pad), (0, 0)))
            lp = l + pad
            qkv = (x @ w_qkv + b_qkv).reshape(b, lp, 3, H, D).transpose(2, 0, 3, 1, 4)
            q, k, v = (qkv[0], qkv[1], qkv[2])
            nw = (lp - W) // STRIDE + 1
            idx = jnp.arange(nw)[:, None] * STRIDE + jnp.arange(W)[None, :]
            qw = q[:, :, idx, :]
            kw = k[:, :, idx, :]
            vw = v[:, :, idx, :]
            scores = jnp.einsum('bhnqd,bhnkd->bhnqk', qw, kw) / jnp.sqrt(jnp.float32(D))
            probs = jax.nn.softmax(scores, axis=-1)
            ow = jnp.einsum('bhnqk,bhnkd->bhnqd', probs, vw)
            o = ow.transpose(0, 2, 3, 1, 4).reshape(b, nw * W, c)
            o = o @ w_out + b_out
            return o[:, :l, :]
        return _local_attention(x, w_qkv, b_qkv, w_out, b_out)

    def _L2_ffn_ref(inputs, Wr, br, W1, b1, W2, b2):
        import jax, jax.numpy as jnp
        import numpy as np
        B, T, D = inputs.shape
        E = Wr.shape[1]
        x = inputs.reshape(B * T, D)
        N = x.shape[0]
        C = N // E
        logits = x @ Wr + br
        probs = jax.nn.softmax(logits, axis=-1)
        gate = jnp.max(probs, axis=-1, keepdims=True)
        idx = jnp.argmax(probs, axis=-1)
        mask = jax.nn.one_hot(idx, E, dtype=jnp.float32)
        pos = (jnp.cumsum(mask, axis=0) * mask).astype(jnp.int32)
        mask = mask * (pos < C).astype(jnp.float32)
        mask_flat = jnp.sum(mask, axis=-1, keepdims=True)
        gate = gate * mask_flat
        combine = (gate * mask_flat * jax.nn.one_hot(idx, E, dtype=jnp.float32))[..., None] * jax.nn.one_hot(pos, C, dtype=jnp.float32)
        dispatch = combine
        expert_in = jnp.einsum('nd,nec->ecd', x, dispatch)
        h = jax.nn.relu(jnp.einsum('ecd,edf->ecf', expert_in, W1) + b1[:, None, :])
        eo = jnp.einsum('ecf,efd->ecd', h, W2) + b2[:, None, :]
        out = jnp.einsum('ecd,nec->nd', eo, combine)
        return out.reshape(B, T, D)

    def _L3_xattn_ref(x1, x2, W, b):
        import jax, jax.numpy as jnp
        import numpy as np
        D1, D2, D3 = (128, 128, 128)
        d1 = x1.shape[-1]
        W1 = W[:, :d1]
        W2 = W[:, d1:]
        part1 = jnp.einsum('bld,ed->ble', x1, W1)
        part2 = jnp.einsum('bld,ed->be', x2, W2) / x2.shape[1]
        return part1 + part2[:, None, :] + b

    def _L3_attn_ref(x, w_in, conv_w, conv_b, w_B, w_C, w_out):
        import jax, jax.numpy as jnp
        from jax import lax
        import numpy as np
        B, S, D = (4, 256, 128)
        D_INNER, D_STATE, D_CONV = (256, 16, 4)

        def silu(v):
            return v * jax.nn.sigmoid(v)
        d_inner = conv_w.shape[0]
        d_conv = conv_w.shape[2]
        xz = x @ w_in
        xp, z = jnp.split(xz, 2, axis=-1)
        xc = lax.conv_general_dilated(xp.transpose(0, 2, 1), conv_w, window_strides=(1,), padding=[(d_conv - 1, 0)], dimension_numbers=('NCH', 'OIH', 'NCH'), feature_group_count=d_inner)
        xc = (xc + conv_b[None, :, None]).transpose(0, 2, 1)
        xc = silu(xc)
        h0 = jnp.zeros((xc.shape[0], w_B.shape[1]), xc.dtype)

        def step(h, xt):
            h = h * 0.9 + 0.1 * (xt @ w_B)
            return (h, h @ w_C)
        _, ys = lax.scan(step, h0, xc.transpose(1, 0, 2))
        y = ys.transpose(1, 0, 2) * silu(z)
        return y @ w_out

    def _L3_ffn_ref(x, Wg, bg, W1, b1, W2, b2):
        import jax, jax.numpy as jnp
        import numpy as np
        H = 128
        I = 128
        E = 8
        B, S, Hd = x.shape
        xf = x.reshape(-1, Hd)
        logits = xf @ Wg + bg
        gates = jax.nn.softmax(logits, axis=-1)
        idx = jnp.argmax(gates, axis=-1)
        h = jax.nn.gelu(jnp.einsum('th,ehi->tei', xf, W1) + b1, approximate=False)
        y = jnp.einsum('tei,eih->teh', h, W2) + b2
        out = jnp.take_along_axis(y, idx[:, None, None], axis=1)[:, 0, :]
        return out.reshape(B, S, Hd)
    x = x + _L0_xattn_ref(ctx_1024, _layernorm(x, axis=-1), L0_xattn_ln_media_w, L0_xattn_ln_media_b, L0_xattn_ln_lat_w, L0_xattn_ln_lat_b, L0_xattn_Wq, L0_xattn_bq, L0_xattn_Wkv, L0_xattn_bkv, L0_xattn_Wout, L0_xattn_bout)
    x = x + _L0_attn_ref(_layernorm(x, axis=-1), L0_attn_W_hg, L0_attn_W_out)
    x = x + _L0_ffn_ref(_layernorm(x, axis=-1), L0_ffn_base_w, L0_ffn_base_b, L0_ffn_gate_w, L0_ffn_lora_A, L0_ffn_lora_B)
    x = x + _L1_xattn_ref(_layernorm(x, axis=-1), ctx_1024, L1_xattn_Wq, L1_xattn_bq, L1_xattn_Wk, L1_xattn_bk, L1_xattn_Wv, L1_xattn_bv)
    x = x + _L1_attn_ref(_layernorm(x, axis=-1), L1_attn_wqkv, L1_attn_wo)
    x = x + _L1_ffn_ref(_layernorm(x, axis=-1), L1_ffn_g1, L1_ffn_g2, L1_ffn_wq, L1_ffn_wk, L1_ffn_wv, L1_ffn_wo, L1_ffn_gate, L1_ffn_w1, L1_ffn_w2, L1_ffn_w3)
    x = x + _L2_xattn_ref(ctx_1024, _layernorm(x, axis=-1), L2_xattn_Wq, L2_xattn_Wkv, L2_xattn_Wout, L2_xattn_gm, L2_xattn_bm, L2_xattn_gl, L2_xattn_bl)
    x = x + _L2_attn_ref(_layernorm(x, axis=-1), L2_attn_w_qkv, L2_attn_b_qkv, L2_attn_w_out, L2_attn_b_out)
    x = x + _L2_ffn_ref(_layernorm(x, axis=-1), L2_ffn_Wr, L2_ffn_br, L2_ffn_W1, L2_ffn_b1, L2_ffn_W2, L2_ffn_b2)
    x = x + _L3_xattn_ref(_layernorm(x, axis=-1), ctx_1024, L3_xattn_W, L3_xattn_b)
    x = x + _L3_attn_ref(_layernorm(x, axis=-1), L3_attn_w_in, L3_attn_conv_w, L3_attn_conv_b, L3_attn_w_B, L3_attn_w_C, L3_attn_w_out)
    x = x + _L3_ffn_ref(_layernorm(x, axis=-1), L3_ffn_Wg, L3_ffn_bg, L3_ffn_W1, L3_ffn_b1, L3_ffn_W2, L3_ffn_b2)
    return x

_drawn_inputs = setup_inputs


def setup_inputs(seed=0):
    import zlib

    import numpy as np

    out = dict(_drawn_inputs(seed))
    spreads = {'L0_xattn_ln_media_w': (1.0, 0.2),
     'L0_xattn_ln_media_b': (0.0, 0.1),
     'L0_xattn_ln_lat_w': (1.0, 0.2),
     'L0_xattn_ln_lat_b': (0.0, 0.1),
     'L0_xattn_bq': (0.0, 0.1),
     'L0_xattn_bkv': (0.0, 0.1),
     'L0_xattn_bout': (0.0, 0.1),
     'L1_xattn_bq': (0.0, 0.577),
     'L1_xattn_bk': (0.0, 2.0),
     'L1_xattn_bv': (0.0, 0.1),
     'L1_ffn_g1': (1.0, 0.6),
     'L1_ffn_g2': (1.0, 0.6),
     'L2_xattn_gm': (1.0, 0.2),
     'L2_xattn_bm': (0.0, 0.1),
     'L2_xattn_gl': (1.0, 0.2),
     'L2_xattn_bl': (0.0, 0.1),
     'L2_attn_b_qkv': (0.0, 0.8),
     'L2_attn_b_out': (0.0, 0.344),
     'L2_ffn_br': (0.0, 0.8),
     'L2_ffn_b1': (0.0, 0.8),
     'L2_ffn_b2': (0.0, 0.8),
     'L3_ffn_bg': (0.0, 0.365),
     'L3_ffn_b1': (0.0, 0.8),
     'L3_ffn_b2': (0.0, 0.8)}
    factors = {'L0_ffn_base_b': 3.114,
     'L1_ffn_wq': 8.0,
     'L1_ffn_wk': 8.0,
     'L1_ffn_gate': 8.0,
     'L1_ffn_w1': 8.0,
     'L1_ffn_w2': 8.0,
     'L1_ffn_w3': 8.0,
     'L2_attn_w_qkv': 4.577,
     'L2_attn_w_out': 3.718,
     'L2_ffn_Wr': 8.0,
     'L2_ffn_W1': 8.0,
     'L2_ffn_W2': 8.0,
     'L3_xattn_b': 4.77,
     'L3_attn_w_in': 8.0,
     'L3_attn_conv_w': 8.0,
     'L3_attn_conv_b': 21.775,
     'L3_attn_w_B': 8.0,
     'L3_attn_w_C': 8.0,
     'L3_attn_w_out': 8.0,
     'L3_ffn_W1': 6.888,
     'L3_ffn_W2': 6.353}
    for name, (base, spread) in spreads.items():
        noise = np.random.default_rng([zlib.crc32(name.encode()), seed]).standard_normal(out[name].shape)
        drawn = base * np.exp(spread * noise) if base else spread * noise
        out[name] = jnp.asarray(drawn.astype(out[name].dtype))
    for name, factor in factors.items():
        out[name] = (out[name] * factor).astype(out[name].dtype)
    return out
```

```python
import numpy as np
from contextlib import ExitStack

import concourse.bass as bass
from concourse import mybir

D = 128
BATCH, SEQ, CTX = 64, 64, 128
SLOTS = 2
GB = 8
GT = GB * SEQ
GC = GB * CTX
TILES = GT // 128
PASSES = BATCH // (GB * SLOTS)
BANK = 512
KEYS = CTX + SEQ
H0, H2, DH = 16, 8, 64
NH, HD = 16, 8
INNER = 256
LORA_E, LORA_R = 8, 16
MOE1_E, MOE1_C = 4, 3
EXPERTS = 8
CAPACITY = BATCH * SEQ // EXPERTS
STATE = 16
NEG = -1.0e30

FOLD = [("q0T", 1024), ("k0T", 1024), ("v0T", 1024), ("o0", 1024), ("q2T", 512), ("k2T", 512), ("v2T", 512), ("o2", 512)]
COLUMNS = [("lmw", 1), ("lmb", 1), ("llw", 1), ("llb", 1), ("bout0", 1), ("bq0", 8), ("bv0", 8), ("base_b", 1),
           ("bq1", 1), ("bk1", 1), ("bv1", 1), ("g1", 1), ("g2", 1), ("gm", 1), ("bm", 1), ("gl", 1), ("bl", 1),
           ("bqkv", 3), ("bo2", 1), ("moe2_b1", 8), ("b3", 1), ("conv_w", 8), ("conv_b", 2), ("moe3_b1", 8),
           ("br", 8), ("bg", 8)]
WEIGHTS = [("hg", 512), ("rnn_out", 256), ("base", 128), ("gate0", 10), ("loraA", 128), ("loraB", 128),
           ("q1", 128), ("k1", 128), ("v1", 128), ("lin_q", 128), ("lin_k", 128), ("lin_v", 128), ("lin_o", 128),
           ("rq", 128), ("rqp", 128), ("rk", 128), ("rkp", 128), ("rv", 128), ("ro", 128), ("gate1", 4),
           ("w1", 1536), ("w3", 1536), ("w2", 1536),
           ("loc_q", 128), ("loc_k", 128), ("loc_v", 128), ("loc_o", 128),
           ("moe2_r", 8), ("moe2_w1", 1024), ("moe2_w2", 1024), ("moe2_b2", 128),
           ("x3a", 128), ("x3b", 128), ("ssm_in", 512), ("ssm_B", 32), ("ssm_C", 256), ("ssm_out", 256),
           ("moe3_r", 8), ("moe3_w1", 1024), ("moe3_w2", 1024), ("moe3_b2", 128)]
CONSTS = [("ident", 128), ("center", 128), ("mean", 128), ("hmask", NH), ("cos", SEQ), ("sin", SEQ),
          ("causal_add", SEQ), ("causal_T", SEQ), ("upto", 128), ("iota", 16), ("lora_sel", 128),
          ("decay", GT), ("ones_row", 128)]


def offsets(table):
    at, out = 0, {}
    for name, n in table:
        out[name] = (at, n)
        at += n
    return out, at


FOLD_AT, FOLD_N = offsets(FOLD)
COL_AT, COL_N = offsets(COLUMNS)
W_AT, W_N = offsets(WEIGHTS)
C_AT, C_N = offsets(CONSTS)


def build(nc, x, ctxin, fold, cols, weights, consts, out):
    f32, bf16, u32 = mybir.dt.float32, mybir.dt.bfloat16, mybir.dt.uint32
    ALU, ACT, AX = mybir.AluOpType, mybir.ActivationFunctionType, mybir.AxisListType

    stack = ExitStack()
    with stack:
        def sb(name, cols_, dt=f32):
            return stack.enter_context(nc.sbuf_tensor(name, [128, cols_], dt))

        def sem(name):
            return stack.enter_context(nc.semaphore(name))

        cst = sb("cst", C_N)
        col = sb("col", COL_N)
        wts = sb("wts", W_N)
        score0 = sb("score0", H0 * D)
        value0 = sb("value0", H0 * D)
        score2 = sb("score2", H2 * D)
        value2 = sb("value2", H2 * D)
        qbias0 = sb("qbias0", H0)
        obias0 = sb("obias0", 1)
        ident_b = sb("ident_b", 128, bf16)
        causal_b = sb("causal_b", SEQ, bf16)
        upto_b = sb("upto_b", 128, bf16)
        ones_b = sb("ones_b", 128, bf16)
        pick_b = sb("pick_b", EXPERTS * 128, bf16)
        eps5 = sb("eps5", 1)
        eps7 = sb("eps7", 1)
        count = sb("count", EXPERTS)

        def C(name):
            at, n = C_AT[name]
            return cst[:, at:at + n]

        def W(name):
            at, n = W_AT[name]
            return wts[:, at:at + n]

        def V(name, k=0):
            at = COL_AT[name][0] + k
            return col[:, at:at + 1]

        def per_slot(name, n, dt=f32):
            return [sb(f"{name}_{s}", n, dt) for s in range(SLOTS)]

        X = per_slot("X", GT)
        Z = per_slot("Z", GT)
        A = per_slot("A", GT)
        ctxT = per_slot("ctxT", GC)
        ctxz = per_slot("ctxz", GC)
        kvT = per_slot("kvT", GB * KEYS)
        T = per_slot("T", 4 * GT)
        big = per_slot("big", 4096)
        P = per_slot("P", 2048)
        Vbd = per_slot("Vbd", GB * 8 * 18)
        small = per_slot("small", 448)
        idx = per_slot("idx", TILES * 8, u32)
        ohb = per_slot("ohb", TILES * 8, bf16)
        mTb = per_slot("mTb", GT, bf16)

        ps = [stack.enter_context(nc.psum_tensor(f"ps_{s}", [128, 4 * BANK], f32)) for s in range(SLOTS)]

        def bank(s, k, n=1, p0=0, p1=128):
            return ps[s][p0:p1, k * BANK:(k + n) * BANK]

        def tmp(s, k, n=1):
            return T[s][:, k * GT:(k + n) * GT]

        def seqs(ap):
            return ap.rearrange("p (b t) -> p b t", t=SEQ)

        def by_head(s, h):
            return big[s][:, :].rearrange("p (b h t) -> p b h t", h=8, t=SEQ)[:, :, h, :]

        def block_of(h, n):
            return (h % 2) * (n // 2) + h // 2

        def qb(h):
            return qbias0[:, block_of(h, H0):block_of(h, H0) + 1]

        def over(ap, axis, shape):
            return ap.unsqueeze(axis).to_broadcast(shape)

        L, M8, IXF, OH, OH1, U, CW, G8, DN = 32, 96, 128, 160, 224, 288, 352, 384, 416

        def route(s, at, e):
            return small[s][:, at:at + 64].rearrange("p (t e) -> p t e", e=16)[:, :, 0:e]

        def comb(s, at):
            return small[s][:, at:at + 32].rearrange("p (t e) -> p t e", e=8)

        def over_e(s, at, k, e):
            return comb(s, at)[:, :, k:k + 1].to_broadcast([128, TILES, e])

        def padded(s):
            return big[s][:, 0:2 * GB * (SEQ + 3)].rearrange("p (n t) -> p n t", t=SEQ + 3)

        LN_EXP = "natural_log_exp_and_others"
        X1_SCALE = float(D) ** -0.5

        w_fold, w_col, w_cst, w_main = sem("w_fold"), sem("w_col"), sem("w_cst"), [sem(f"w_main{k}") for k in range(4)]
        prep = sem("prep")
        folded, fold_out = sem("folded"), sem("fold_out")
        NAMES = ["x_loaded0", "x_loaded1", "ctx_loaded0", "ctx_loaded1", "stored",
                 "centered", "squared", "var", "log_var", "rstd", "normed", "rms_sq", "rms_var", "rms_rstd", "rms_done",
                 "kv_ready", "kvn_ps", "kvn_ready", "kvl_ready",
                 "qp_ps", "qp_act", "qp_dve", "scores", "maxed", "exped", "rsum", "p_ready", "pT_ps", "pT_act", "pT_dve",
                 "mixed", "mix_out", "heads_ps",
                 "rnn_in", "rnn_tanh", "rnn_pool", "rnn_h", "rnn_out",
                 "logits", "shifted", "u_exp", "comb", "combT_ps", "combT", "lora_z_ps", "lora_z", "lora_b", "lora_zs", "lora_out",
                 "x1_proj", "x1_q", "x1_k", "x1_s", "x1_v", "x1_max", "x1_exp", "x1_sum", "x1_p", "x1_pT", "x1_pT_sb", "x1_o",
                 "n_proj", "n_q", "n_k", "v_ps", "v_sb", "bd_ready", "bd_used", "n_s", "n_sub", "n_exp",
                 "n_pT", "n_pT_act", "n_pT_dve", "n_o", "n_y", "n_yT", "n_yT_sb", "n_out",
                 "rope_dve", "rope", "y_ready", "final",
                 "m1_bc", "m1_x", "m1_h", "m1_t", "m1_g", "m1_out",
                 "cum_ps", "g_bc", "g_sb", "xg", "m2_h", "m2_relu", "m2_m", "m2_out", "m2_mT_b",
                 "onehot", "m2_mask", "m2_act", "x1_v_sb", "rms_log", "pool_chain", "ssm_pad", "x3_sum", "x3_ps", "ssm_in", "ssm_xp", "ssm_conv", "ssm_t", "ssm_x", "ssm_u", "ssm_h", "ssm_y",
                 "ssm_zt", "ssm_g", "ssm_out", "chain", "x_added"]
        g = {n: sem(n) for n in NAMES}
        x_loaded, ctx_loaded = (g["x_loaded0"], g["x_loaded1"]), (g["ctx_loaded0"], g["ctx_loaded1"])
        clear = range(g["x_loaded0"].num, g["x_added"].num + 1)
        assert len(clear) == len(NAMES)

        def nth(n, s):
            return n * SLOTS + s + 1

        with nc.Block() as block:
            @block.sync
            def _(sp):
                sp.dma_start(big[0][:, :], fold[:, 0:4096]).then_inc(w_fold, 16)
                sp.dma_start(big[1][:, 0:2048], fold[:, 4096:6144]).then_inc(w_fold, 16)
                sp.dma_start(col[:, :], cols[:, :]).then_inc(w_col, 16)
                sp.dma_start(cst[:, :], consts[:, :]).then_inc(w_cst, 16)
                cut = [0, W_AT["lin_q"][0], W_AT["w1"][0], W_AT["loc_q"][0], W_N]
                for k in range(4):
                    sp.dma_start(wts[:, cut[k]:cut[k + 1]], weights[:, cut[k]:cut[k + 1]]).then_inc(w_main[k], 16)

            @block.gpsimd
            def _(pool):
                pool.memset(count[:, :], 0.0).then_inc(prep, 1)
                for s in range(SLOTS):
                    pool.wait_ge(prep, 3 * s + 1)
                    pool.memset(Vbd[s][:, :], 0.0).then_inc(prep, 1)
                    pool.wait_ge(prep, 3 * s + 2)
                    vb = Vbd[s][:, :].rearrange("p (n c) -> p n c", c=18)
                    pool.memset(vb[0:64, :, 8:9], 1.0).then_inc(prep, 1)
                    pool.wait_ge(prep, 3 * s + 3)
                    pool.memset(vb[64:128, :, 17:18], 1.0).then_inc(prep, 1)

            def rows(s, name, j, hh):
                at = FOLD_AT[name][0] - (4096 if s else 0)
                return big[s][64 * hh:64 * hh + 64, at + 128 * j:at + 128 * j + 128]

            @block.tensor
            def _(pe):
                pe.wait_ge(w_fold, 32)
                pe.wait_ge(w_col, 16)
                for h in range(H0):
                    j, hh, at = h // 2, h % 2, 128 * block_of(h, H0)
                    pe.matmul(ps[0][:, at:at + 128], rows(0, "q0T", j, hh), rows(0, "k0T", j, hh), start=True, stop=True)
                    m = pe.matmul(ps[1][:, at:at + 128], rows(0, "v0T", j, hh), rows(0, "o0", j, hh), start=True, stop=True)
                m.then_inc(folded, 1)
                pe.wait_ge(fold_out, 2)
                for h in range(H2):
                    j, hh, at = h // 2, h % 2, 128 * block_of(h, H2)
                    pe.matmul(ps[0][:, at:at + 128], rows(1, "q2T", j, hh), rows(1, "k2T", j, hh), start=True, stop=True)
                    m = pe.matmul(ps[1][:, at:at + 128], rows(1, "v2T", j, hh), rows(1, "o2", j, hh), start=True, stop=True)
                for h in range(H0):
                    j, hh = h // 2, h % 2
                    at, to = COL_AT["bq0"][0] + j, (2 + hh) * BANK + j
                    pe.matmul(ps[0][:, to:to + 1], rows(0, "k0T", j, hh), col[64 * hh:64 * hh + 64, at:at + 1],
                              start=True, stop=True)
                for j in range(H0 // 2):
                    at = FOLD_AT["o0"][0] + 128 * j
                    m = pe.matmul(ps[1][:, 2 * BANK:2 * BANK + 1], big[0][:, at:at + 128], V("bv0", j), start=(j == 0), stop=(j == 7))
                m.then_inc(folded, 1)

            @block.scalar
            def _(act):
                act.wait_ge(folded, 1)
                act.activation(score0[:, :], ps[0][:, :], ACT.Copy).then_inc(fold_out, 1)
                act.wait_ge(folded, 2)
                act.activation(score2[:, :], ps[0][:, 0:1024], ACT.Copy).then_inc(fold_out, 1)
                for hh in range(2):
                    act.activation(qbias0[:, 8 * hh:8 * hh + 8], ps[0][:, (2 + hh) * BANK:(2 + hh) * BANK + 8], ACT.Copy,
                                   scale=0.125).then_inc(fold_out, 1)

            @block.vector
            def _(dve):
                dve.wait_ge(w_cst, 16)
                dve.tensor_copy(ident_b[:, :], C("ident"))
                dve.tensor_copy(causal_b[:, :], C("causal_add"))
                dve.tensor_copy(upto_b[:, :], C("upto"))
                dve.tensor_copy(pick_b[:, :].rearrange("p (e m) -> p e m", m=128),
                                over(C("ident")[:, 0:EXPERTS], 2, [128, EXPERTS, 128]))
                dve.memset(ones_b[:, :], 1.0)
                dve.memset(eps5[:, :], 1e-5)
                dve.memset(eps7[:, :], 1.1920928955078125e-07)
                dve.wait_ge(folded, 1)
                dve.tensor_copy(value0[:, :], ps[1][:, :]).then_inc(fold_out, 1)
                dve.wait_ge(folded, 2)
                dve.tensor_copy(value2[:, :], ps[1][:, 0:1024])
                dve.tensor_tensor(obias0[:, :], ps[1][:, 2 * BANK:2 * BANK + 1], V("bout0"), ALU.add)

        LAST = 12
        LN = dict(ctx0=0, ctx1=1, x0=2, lat0=3, rnn=4, lora=5, x1=6, lin=7, moe1=8, x2=9, lat2=10, loc=11, moe2=12, x3=13,
                  ssm=14, moe3=15)

        with nc.Fori(0, PASSES) as i:
            with nc.Block() as block:
                @block.sync
                def _(sp):
                    for s in range(SLOTS):
                        at = i * (SLOTS * GT) + s * GT
                        atc = i * (SLOTS * GC) + s * GC
                        sp.dma_start(ctxT[s][:, :], ctxin[:, bass.ds(atc, GC)]).then_inc(ctx_loaded[s], 16)
                        sp.dma_start(X[s][:, :], x[:, bass.ds(at, GT)]).then_inc(x_loaded[s], 16)
                    for s in range(SLOTS):
                        at = i * (SLOTS * GT) + s * GT
                        sp.wait_ge(g["x_added"], nth(LAST, s))
                        sp.dma_start(out[:, bass.ds(at, GT)], X[s][:, :]).then_inc(g["stored"], 16)
                    sp.wait_ge(g["stored"], 16 * SLOTS)

                @block.tensor
                def _(pe):
                    def added(n, s):
                        if n >= 0:
                            pe.wait_ge(g["x_added"], nth(n, s))

                    def norm(name, src, ready):
                        n = LN[name]
                        for s in range(SLOTS):
                            ready(s)
                            pe.matmul(bank(s, 0), C("center"), src(s), start=True, stop=True).then_inc(g["centered"], 1)
                        for s in range(SLOTS):
                            pe.wait_ge(g["squared"], nth(n, s))
                            pe.matmul(bank(s, 1), C("mean"), tmp(s, 0), start=True, stop=True).then_inc(g["var"], 1)

                    def normed(name, s):
                        pe.wait_ge(g["normed"], nth(LN[name], s))

                    def kv_tokens(n):
                        for s in range(SLOTS):
                            pe.wait_ge(g["kv_ready"], nth(n, s))
                            for b in range(GB):
                                pe.transpose(ps[s][:, 128 * b:128 * b + 128], kvT[s][:, KEYS * b:KEYS * b + CTX], C("ident"))
                                m = pe.transpose(ps[s][0:64, 2 * BANK + 128 * b:2 * BANK + 128 * b + 128],
                                                 kvT[s][:, KEYS * b + CTX:KEYS * b + KEYS], C("ident"))
                            m.then_inc(g["kvn_ps"], 1)

                    def heads(gi, n, score, value, nh, h0):
                        for r in range(2):
                            for s in range(SLOTS):
                                if r == 0 and h0 == 0:
                                    pe.wait_ge(g["kvn_ready"], nth(n, s))
                                    pe.wait_ge(g["kvl_ready"], nth(n, s))
                                elif r == 0:
                                    added(gi - 1, s)
                                else:
                                    pe.wait_ge(g["qp_act"], nth(2 * gi, s))
                                    pe.wait_ge(g["qp_dve"], nth(2 * gi, s))
                                lat = kvT[s][:, :].rearrange("p (b k) -> p b k", k=KEYS)[:, :, CTX:KEYS]
                                for k in range(4):
                                    h = h0 + 4 * r + k
                                    m = pe.matmul(bank(s, k), score[:, 128 * block_of(h, nh):128 * block_of(h, nh) + 128], lat, start=True, stop=True)
                                m.then_inc(g["qp_ps"], 1)
                        for b in range(GB):
                            u = gi * GB + b
                            for s in range(SLOTS):
                                if b == 0:
                                    pe.wait_ge(g["qp_act"], nth(2 * gi + 1, s))
                                    pe.wait_ge(g["qp_dve"], nth(2 * gi + 1, s))
                                else:
                                    pe.wait_ge(g["mix_out"], nth(u - 1, s))
                                for p in range(4):
                                    at = (p // 2) * BANK + (p % 2) * KEYS
                                    m = pe.matmul(ps[s][:, at:at + KEYS], big[s][:, BANK * b + 128 * p:BANK * b + 128 * p + 128],
                                                  kvT[s][:, KEYS * b:KEYS * b + KEYS], start=True, stop=True)
                                m.then_inc(g["scores"], 1)
                            for s in range(SLOTS):
                                pe.wait_ge(g["p_ready"], nth(u, s))
                                for p in range(4):
                                    pe.transpose(ps[s][:, 2 * BANK + 128 * p:2 * BANK + 128 * p + 128],
                                                 P[s][:, KEYS * p:KEYS * p + CTX], C("ident"))
                                    m = pe.transpose(ps[s][0:64, 3 * BANK + 128 * p:3 * BANK + 128 * p + 128],
                                                     P[s][:, KEYS * p + CTX:KEYS * p + KEYS], C("ident"))
                                m.then_inc(g["pT_ps"], 1)
                            for s in range(SLOTS):
                                pe.wait_ge(g["pT_act"], nth(u, s))
                                pe.wait_ge(g["pT_dve"], nth(u, s))
                                pe.matmul(bank(s, 0), T[s][:, 128 * b:128 * b + 128], P[s][:, 1024:1536], start=True, stop=False)
                                pe.matmul(bank(s, 0), T[s][0:64, GC + 128 * b:GC + 128 * b + 128], P[s][0:64, 1536:2048],
                                          start=False, stop=True).then_inc(g["mixed"], 1)
                        for s in range(SLOTS):
                            pe.wait_ge(g["mix_out"], nth(gi * GB + GB - 1, s))
                            for k in range(8):
                                m = pe.matmul(bank(s, 1), value[:, 128 * block_of(h0 + k, nh):128 * block_of(h0 + k, nh) + 128],
                                              by_head(s, k), start=(k == 0), stop=(k == 7))
                            m.then_inc(g["heads_ps"], 1)

                    pe.wait_ge(w_cst, 16)
                    for k in range(4):
                        pe.wait_ge(w_main[k], 16)
                    norm("ctx0", lambda s: ctxT[s][:, 0:GT], lambda s: pe.wait_ge(ctx_loaded[s], 16))
                    norm("ctx1", lambda s: ctxT[s][:, GT:GC], lambda s: normed("ctx0", s))
                    norm("x0", lambda s: X[s][:, :], lambda s: (normed("ctx1", s), pe.wait_ge(x_loaded[s], 16)))
                    norm("lat0", lambda s: Z[s][:, :], lambda s: normed("x0", s))
                    kv_tokens(0)
                    heads(0, 0, score0, value0, H0, 0)
                    heads(1, 0, score0, value0, H0, 8)

                    norm("rnn", lambda s: X[s][:, :], lambda s: added(1, s))
                    for s in range(SLOTS):
                        normed("rnn", s)
                        for k in range(4):
                            m = pe.matmul(bank(s, k), W("hg")[:, 128 * k:128 * k + 128], Z[s][:, :], start=True, stop=True)
                        m.then_inc(g["rnn_in"], 1)
                    for s in range(SLOTS):
                        pe.wait_ge(g["rnn_h"], nth(0, s))
                        for k in range(2):
                            m = pe.matmul(bank(s, 0), W("rnn_out")[:, 128 * k:128 * k + 128],
                                          big[s][:, 2048 + GT * k:2048 + GT * k + GT], start=(k == 0), stop=(k == 1))
                        m.then_inc(g["rnn_out"], 1)

                    def logits(n, src, w, e, bias=None):
                        for s in range(SLOTS):
                            for t in range(TILES):
                                to = ps[s][:, 16 * t:16 * t + e]
                                if bias:
                                    pe.matmul(to, C("ones_row")[0:1, :], bias, start=True, stop=False)
                                m = pe.matmul(to, src(s)[:, 128 * t:128 * t + 128], w, start=not bias, stop=True)
                            m.then_inc(g["logits"], 1)

                    def turn(n, pairs):
                        for s in range(SLOTS):
                            pe.wait_ge(g["comb"], nth(n, s))
                            for at, k in pairs:
                                for t in range(TILES):
                                    m = pe.transpose(ps[s][0:8, k * BANK + 128 * t:k * BANK + 128 * t + 128],
                                                     small[s][:, at + 8 * t:at + 8 * t + 8], C("ident"))
                            m.then_inc(g["combT_ps"], 1)

                    norm("lora", lambda s: X[s][:, :], lambda s: added(2, s))
                    for s in range(SLOTS):
                        normed("lora", s)
                    logits(0, lambda s: Z[s], W("gate0"), 10)
                    for s in range(SLOTS):
                        pe.matmul(bank(s, 1), W("loraA"), Z[s][:, :], start=True, stop=True).then_inc(g["lora_z_ps"], 1)
                        pe.matmul(bank(s, 2), W("base"), Z[s][:, :], start=True, stop=False)
                    turn(0, [(352, 3)])
                    for s in range(SLOTS):
                        pe.wait_ge(g["combT"], nth(0, s))
                        pe.wait_ge(g["lora_z"], nth(0, s))
                        pe.matmul(bank(s, 1), C("lora_sel")[0:8, :], tmp(s, 3)[0:8, :], start=True, stop=True).then_inc(g["lora_b"], 1)
                    for s in range(SLOTS):
                        pe.wait_ge(g["lora_zs"], nth(0, s))
                        pe.matmul(bank(s, 2), W("loraB"), tmp(s, 1), start=False, stop=True).then_inc(g["lora_out"], 1)

                    norm("x1", lambda s: X[s][:, :], lambda s: added(3, s))
                    for s in range(SLOTS):
                        normed("x1", s)
                        pe.matmul(bank(s, 0), W("q1"), Z[s][:, :], start=True, stop=True)
                        pe.matmul(bank(s, 1), W("k1"), ctxT[s][:, 0:GT], start=True, stop=True)
                        pe.matmul(bank(s, 2), W("k1"), ctxT[s][:, GT:GC], start=True, stop=True).then_inc(g["x1_proj"], 1)
                    for s in range(SLOTS):
                        pe.wait_ge(g["x1_q"], nth(0, s))
                        pe.wait_ge(g["x1_k"], nth(0, s))
                        for b in range(GB):
                            p0 = SEQ * (b % 2)
                            m = pe.matmul(ps[s][p0:p0 + SEQ, 128 * (b // 2):128 * (b // 2) + 128], A[s][:, SEQ * b:SEQ * b + SEQ],
                                          kvT[s][:, CTX * b:CTX * b + CTX], start=True, stop=True)
                        m.then_inc(g["x1_s"], 1)
                        for b in range(GB):
                            m = pe.matmul(ps[s][:, BANK + 128 * b:BANK + 128 * b + 128], ctxT[s][:, CTX * b:CTX * b + CTX],
                                          W("v1"), start=True, stop=True)
                        m.then_inc(g["x1_v"], 1)
                    for s in range(SLOTS):
                        pe.wait_ge(g["x1_p"], nth(0, s))
                        for t in range(TILES):
                            m = pe.transpose(ps[s][:, 3 * BANK + 128 * t:3 * BANK + 128 * t + 128], P[s][:, 128 * t:128 * t + 128],
                                             C("ident"))
                        m.then_inc(g["x1_pT"], 1)
                    for s in range(SLOTS):
                        pe.wait_ge(g["x1_pT_sb"], nth(0, s))
                        pe.wait_ge(g["x1_v_sb"], nth(0, s))
                        for b in range(GB):
                            m = pe.matmul(ps[s][:, SEQ * b:SEQ * b + SEQ], big[s][:, CTX * b:CTX * b + CTX],
                                          P[s][:, 512 + SEQ * b:512 + SEQ * b + SEQ], start=True, stop=True)
                        m.then_inc(g["x1_o"], 1)

                    def values(s, k, src, w):
                        wv = w.rearrange("p (j c d) -> p j c d", c=2, d=HD)
                        for b in range(GB):
                            for hh in range(2):
                                m = pe.matmul(ps[s][64 * hh:64 * hh + 64, k * BANK + 64 * b:k * BANK + 64 * b + 64],
                                              src[:, SEQ * b:SEQ * b + SEQ], wv[:, :, hh, :], start=True, stop=True)
                        m.then_inc(g["v_ps"], 1)

                    def project(m_, w):
                        for s in range(SLOTS):
                            for t in range(TILES):
                                m = pe.transpose(ps[s][:, BANK + 128 * t:BANK + 128 * t + 128], kvT[s][:, 128 * t:128 * t + 128],
                                                 C("ident"))
                            m.then_inc(g["n_yT"], 1)
                        for s in range(SLOTS):
                            pe.wait_ge(g["n_yT_sb"], nth(m_, s))
                            pe.matmul(bank(s, 2), w, kvT[s][:, GT:2 * GT], start=True, stop=True).then_inc(g["n_out"], 1)

                    def softmax_heads(u0, v0, causal):
                        for t in range(TILES):
                            u, v = u0 + t, v0 + t
                            for s in range(SLOTS):
                                pe.wait_ge(g["bd_ready"], nth(u, s))
                                if t:
                                    pe.wait_ge(g["n_y"], nth(u - 1, s))
                                for half in range(2 if causal else 0):
                                    pe.matmul(bank(s, half), ident_b[:, :], over(causal_b[:, :], 1, [128, 8, SEQ]), start=True, stop=False)
                                for half in range(2):
                                    for bb in range(2):
                                        b, at = 2 * t + bb, 2048 * (t % 2) + 1024 * bb + 512 * half
                                        m = pe.matmul(bank(s, half, 1, 64 * bb, 64 * bb + 64), tmp(s, 0)[:, SEQ * b:SEQ * b + SEQ],
                                                      big[s][:, at:at + 512], start=not causal, stop=True)
                                m.then_inc(g["n_s"], 1)
                            for s in range(SLOTS):
                                pe.wait_ge(g["n_exp"], nth(v, s))
                                for j in range(8):
                                    m = pe.transpose(ps[s][:, 2 * BANK + 128 * j:2 * BANK + 128 * j + 128],
                                                     P[s][:, 128 * j:128 * j + 128], C("ident"))
                                m.then_inc(g["n_pT"], 1)
                            for s in range(SLOTS):
                                pe.wait_ge(g["n_pT_act"], nth(v, s))
                                pe.wait_ge(g["n_pT_dve"], nth(v, s))
                                for bb in range(2):
                                    b = 2 * t + bb
                                    for j in range(8):
                                        m = pe.matmul(ps[s][64 * bb:64 * bb + 64, 18 * j:18 * j + 18],
                                                      P[s][:, 1024 + 128 * j + 64 * bb:1024 + 128 * j + 64 * bb + 64],
                                                      Vbd[s][:, 18 * (8 * b + j):18 * (8 * b + j) + 18], start=True, stop=True)
                                m.then_inc(g["n_o"], 1)
                        for s in range(SLOTS):
                            pe.wait_ge(g["n_y"], nth(u0 + TILES - 1, s))

                    norm("lin", lambda s: X[s][:, :], lambda s: added(4, s))
                    for s in range(SLOTS):
                        normed("lin", s)
                        pe.matmul(bank(s, 0), W("lin_q"), Z[s][:, :], start=True, stop=True)
                        pe.matmul(bank(s, 1), W("lin_k"), Z[s][:, :], start=True, stop=True).then_inc(g["n_proj"], 1)
                        values(s, 2, Z[s], W("lin_v"))
                    for r in range(2):
                        for s in range(SLOTS):
                            pe.wait_ge(g["bd_ready"], nth(r, s))
                            if r == 0:
                                pe.wait_ge(g["n_k"], nth(0, s))
                                pe.wait_ge(g["v_sb"], nth(0, s))
                            else:
                                pe.wait_ge(g["n_y"], nth(0, s))
                            for bb in range(4):
                                b = 4 * r + bb
                                q = big[s][:, 1024 * bb:1024 * bb + 1024].rearrange("p (j c t) -> p j c t", c=2, t=SEQ)
                                for hh in range(2):
                                    m = pe.matmul(bank(s, bb, 1, 64 * hh, 64 * hh + 64), tmp(s, 2)[:, SEQ * b:SEQ * b + SEQ],
                                                  q[:, :, hh, :], start=True, stop=True)
                            m.then_inc(g["n_s"], 1)
                        for s in range(SLOTS):
                            pe.wait_ge(g["n_sub"], nth(r, s))
                            for bb in range(4):
                                p0 = 64 * (bb % 2)
                                for j in range(8):
                                    at, b = (bb // 2) * 144 + 18 * j, 4 * r + bb
                                    m = pe.matmul(ps[s][p0:p0 + 64, at:at + 18], P[s][:, 64 * (8 * bb + j):64 * (8 * bb + j) + 64],
                                                  Vbd[s][:, 18 * (8 * b + j):18 * (8 * b + j) + 18], start=True, stop=True)
                            m.then_inc(g["n_o"], 1)
                    for s in range(SLOTS):
                        pe.wait_ge(g["n_y"], nth(1, s))
                    project(0, W("lin_o"))

                    def rms(n, ready):
                        for s in range(SLOTS):
                            ready(s)
                            pe.wait_ge(g["rms_sq"], nth(n, s))
                            pe.matmul(bank(s, 1), C("mean"), tmp(s, 0), start=True, stop=True).then_inc(g["rms_var"], 1)

                    norm("moe1", lambda s: X[s][:, :], lambda s: added(5, s))
                    rms(0, lambda s: normed("moe1", s))
                    for s in range(SLOTS):
                        pe.wait_ge(g["rms_done"], nth(0, s))
                        for k, name in enumerate(("rq", "rqp", "rk", "rkp")):
                            m = pe.matmul(bank(s, k), W(name), A[s][:, :], start=True, stop=True)
                        m.then_inc(g["n_proj"], 1)
                    for s in range(SLOTS):
                        pe.wait_ge(g["rope_dve"], nth(0, s))
                        values(s, 0, A[s], W("rv"))
                    for s in range(SLOTS):
                        pe.wait_ge(g["v_sb"], nth(1, s))
                    softmax_heads(2, 0, True)
                    project(1, W("ro"))
                    rms(1, lambda s: None)
                    for s in range(SLOTS):
                        pe.wait_ge(g["rms_done"], nth(1, s))
                    logits(1, lambda s: A[s], W("gate1"), MOE1_E)
                    turn(1, [(352, 3)])
                    for e in range(MOE1_E):
                        for s in range(SLOTS):
                            if e == 0:
                                pe.wait_ge(g["combT"], nth(1, s))
                            else:
                                pe.wait_ge(g["m1_x"], nth(e - 1, s))
                            pe.matmul(bank(s, 3), C("ident")[0:8, e:e + 1].to_broadcast([8, 128]), tmp(s, 3)[0:8, :],
                                      start=True, stop=True).then_inc(g["m1_bc"], 1)
                        for c in range(MOE1_C):
                            k = e * MOE1_C + c
                            at = 128 * k
                            for s in range(SLOTS):
                                if c == 0:
                                    pe.wait_ge(g["m1_x"], nth(e, s))
                                pe.matmul(bank(s, 0), W("w1")[:, at:at + 128], A[s][:, :], start=True, stop=True)
                                pe.matmul(bank(s, 1), W("w3")[:, at:at + 128], tmp(s, e % 2), start=True, stop=True).then_inc(g["m1_h"], 1)
                            for s in range(SLOTS):
                                pe.wait_ge(g["m1_g"], nth(k, s))
                                m = pe.matmul(bank(s, 2), W("w2")[:, at:at + 128], P[s][:, 1024 + 512 * (k % 2):1536 + 512 * (k % 2)],
                                              start=(k == 0), stop=(k == 11))
                                if k == 11:
                                    m.then_inc(g["m1_out"], 1)

                    norm("x2", lambda s: X[s][:, :], lambda s: added(6, s))
                    norm("lat2", lambda s: Z[s][:, :], lambda s: normed("x2", s))
                    kv_tokens(1)
                    heads(2, 1, score2, value2, H2, 0)

                    norm("loc", lambda s: X[s][:, :], lambda s: added(7, s))
                    for s in range(SLOTS):
                        normed("loc", s)
                        pe.matmul(bank(s, 0), W("loc_q"), Z[s][:, :], start=True, stop=True)
                        pe.matmul(bank(s, 1), W("loc_k"), Z[s][:, :], start=True, stop=True).then_inc(g["n_proj"], 1)
                        values(s, 2, Z[s], W("loc_v"))
                    for s in range(SLOTS):
                        pe.wait_ge(g["n_q"], nth(1, s))
                        pe.wait_ge(g["n_k"], nth(1, s))
                        pe.wait_ge(g["v_sb"], nth(2, s))
                    softmax_heads(6, 4, False)
                    project(2, W("loc_o"))

                    def top1_experts(layer, w1, w2, b2):
                        for s in range(SLOTS):
                            pe.matmul(bank(s, 2), b2[0:8, :], tmp(s, 3)[0:8, :], start=True, stop=False)
                        for e in range(EXPERTS):
                            n = layer * EXPERTS + e
                            for s in range(SLOTS):
                                if e:
                                    pe.wait_ge(g["m2_m"], nth(n - 1, s))
                                src = A[s][:, :] if layer == 0 else Z[s][:, :]
                                pe.matmul(bank(s, 0), w1[:, 128 * e:128 * e + 128], src, start=True, stop=True).then_inc(g["m2_h"], 1)
                                pe.matmul(bank(s, 1), pick_b[0:8, 128 * e:128 * e + 128], mTb[s][0:8, :], start=True, stop=True)\
                                    .then_inc(g["m2_mask"], 1)
                            for s in range(SLOTS):
                                pe.wait_ge(g["m2_m"], nth(n, s))
                                m = pe.matmul(bank(s, 2), w2[:, 128 * e:128 * e + 128], P[s][:, 1024 + 512 * (e % 2):1536 + 512 * (e % 2)],
                                              start=False, stop=(e == EXPERTS - 1))
                                if e == EXPERTS - 1:
                                    m.then_inc(g["m2_out"], 1)

                    norm("moe2", lambda s: X[s][:, :], lambda s: added(8, s))
                    for s in range(SLOTS):
                        normed("moe2", s)
                    at = COL_AT["br"][0]
                    logits(2, lambda s: Z[s], W("moe2_r"), 8, col[0:1, at:at + 8])
                    for s in range(SLOTS):
                        pe.wait_ge(g["onehot"], nth(0, s))
                        for t in range(TILES):
                            for t2 in range(t):
                                pe.matmul(ps[s][:, BANK + 8 * t:BANK + 8 * t + 8], ones_b[:, :], ohb[s][:, 8 * t2:8 * t2 + 8],
                                          start=(t2 == 0), stop=False)
                            pe.matmul(ps[s][:, BANK + 8 * t:BANK + 8 * t + 8], upto_b[:, :], ohb[s][:, 8 * t:8 * t + 8],
                                      start=(t == 0), stop=True)
                        for t in range(TILES):
                            m = pe.matmul(ps[s][:, BANK + 32:BANK + 40], ones_b[:, :], ohb[s][:, 8 * t:8 * t + 8],
                                          start=(t == 0), stop=(t == TILES - 1))
                        m.then_inc(g["cum_ps"], 1)
                    turn(2, [(352, 3), (384, 2)])
                    for s in range(SLOTS):
                        pe.wait_ge(g["combT"], nth(2, s))
                        pe.matmul(bank(s, 0), C("ones_row")[0:8, :], tmp(s, 2)[0:8, :], start=True, stop=True).then_inc(g["g_bc"], 1)
                    for s in range(SLOTS):
                        pe.wait_ge(g["xg"], nth(0, s))
                    top1_experts(0, W("moe2_w1"), W("moe2_w2"), W("moe2_b2"))

                    norm("x3", lambda s: X[s][:, :], lambda s: added(9, s))
                    for s in range(SLOTS):
                        normed("x3", s)
                        pe.wait_ge(g["x3_sum"], nth(0, s))
                        pe.matmul(bank(s, 0), W("x3a"), Z[s][:, :], start=True, stop=True)
                        pe.matmul(ps[s][:, BANK:BANK + GB], W("x3b"), small[s][:, 0:8], start=True, stop=True).then_inc(g["x3_ps"], 1)

                    norm("ssm", lambda s: X[s][:, :], lambda s: added(10, s))
                    for s in range(SLOTS):
                        normed("ssm", s)
                        for k in range(4):
                            m = pe.matmul(bank(s, k), W("ssm_in")[:, 128 * k:128 * k + 128], Z[s][:, :], start=True, stop=True)
                        m.then_inc(g["ssm_in"], 1)
                    for s in range(SLOTS):
                        pe.wait_ge(g["ssm_x"], nth(0, s))
                        for k in range(2):
                            m = pe.matmul(bank(s, 0, 1, 0, STATE), W("ssm_B")[:, STATE * k:STATE * k + STATE],
                                          P[s][:, 1024 + GT * k:1024 + GT * k + GT], start=(k == 0), stop=(k == 1))
                        m.then_inc(g["ssm_u"], 1)
                    for s in range(SLOTS):
                        pe.wait_ge(g["ssm_h"], nth(0, s))
                        for k in range(2):
                            m = pe.matmul(bank(s, k), W("ssm_C")[0:STATE, 128 * k:128 * k + 128], tmp(s, 1)[0:STATE, :],
                                          start=True, stop=True)
                        m.then_inc(g["ssm_y"], 1)
                    for s in range(SLOTS):
                        pe.wait_ge(g["ssm_g"], nth(0, s))
                        for k in range(2):
                            m = pe.matmul(bank(s, 2), W("ssm_out")[:, 128 * k:128 * k + 128], P[s][:, GT * k:GT * k + GT],
                                          start=(k == 0), stop=(k == 1))
                        m.then_inc(g["ssm_out"], 1)

                    norm("moe3", lambda s: X[s][:, :], lambda s: added(11, s))
                    for s in range(SLOTS):
                        normed("moe3", s)
                    at = COL_AT["bg"][0]
                    logits(3, lambda s: Z[s], W("moe3_r"), 8, col[0:1, at:at + 8])
                    turn(3, [(352, 3)])
                    for s in range(SLOTS):
                        pe.wait_ge(g["combT"], nth(3, s))
                    top1_experts(1, W("moe3_w1"), W("moe3_w2"), W("moe3_b2"))

                @block.scalar
                def _(act):
                    def norm(name):
                        n = LN[name]
                        for s in range(SLOTS):
                            act.wait_ge(g["centered"], nth(n, s))
                            act.activation(tmp(s, 0), bank(s, 0), ACT.Square).then_inc(g["squared"], 1)
                        for s in range(SLOTS):
                            act.wait_ge(g["var"], nth(n, s))
                            act.activation(tmp(s, 0), bank(s, 1), ACT.Ln, bias=eps5[:, 0:1]).then_inc(g["log_var"], 1)
                        for s in range(SLOTS):
                            act.wait_ge(g["log_var"], nth(n, s))
                            act.activation(tmp(s, 1), tmp(s, 0), ACT.Exp, scale=-0.5).then_inc(g["rstd"], 1)

                    def kv_tokens(n):
                        for s in range(SLOTS):
                            act.wait_ge(g["kvn_ps"], nth(n, s))
                            act.activation(T[s][:, 0:GC], bank(s, 0, 2), ACT.Copy).then_inc(g["kvn_ready"], 1)

                    def heads(gi, scale, bias, h0):
                        for r in range(2):
                            for s in range(SLOTS):
                                act.wait_ge(g["qp_ps"], nth(2 * gi + r, s))
                                for k in (2, 3):
                                    h = 4 * r + k
                                    m = act.activation(by_head(s, h), seqs(bank(s, k)), ACT.Identity,
                                                       bias=qb(h0 + h) if bias else 0.0, scale=scale)
                                m.then_inc(g["qp_act"], 1)
                        for b in range(GB):
                            u = gi * GB + b
                            for s in range(SLOTS):
                                act.wait_ge(g["maxed"], nth(u, s))
                                for p in range(4):
                                    at = (p // 2) * BANK + (p % 2) * KEYS
                                    m = act.activation(P[s][:, KEYS * p:KEYS * p + KEYS], ps[s][:, at:at + KEYS], ACT.Exp,
                                                       bias=small[s][:, p:p + 1], accum_out=small[s][:, 8 + p:9 + p])
                                m.then_inc(g["exped"], 1)
                            for s in range(SLOTS):
                                act.wait_ge(g["pT_ps"], nth(u, s))
                                act.activation(P[s][:, 1024:1536], bank(s, 2), ACT.Copy).then_inc(g["pT_act"], 1)

                    act.preload_act_table_set(LN_EXP)
                    norm("ctx0")
                    norm("ctx1")
                    norm("x0")
                    norm("lat0")
                    kv_tokens(0)
                    heads(0, 0.125, True, 0)
                    heads(1, 0.125, True, 8)

                    norm("rnn")
                    for s in range(SLOTS):
                        act.wait_ge(g["rnn_in"], nth(0, s))
                        act.activation(tmp(s, 0, 2), bank(s, 2, 2), ACT.Tanh, scale=0.5).then_inc(g["rnn_tanh"], 1)
                    act.preload_act_table_set(LN_EXP)

                    def exp_logits(n, e):
                        for s in range(SLOTS):
                            act.wait_ge(g["shifted"], nth(n, s))
                            act.activation(route(s, U, e), route(s, U, e), ACT.Exp).then_inc(g["u_exp"], 1)

                    def turned(n, copies):
                        for s in range(SLOTS):
                            act.wait_ge(g["combT_ps"], nth(n, s))
                            for dst, k in copies:
                                m = act.activation(dst(s), bank(s, k, 1, 0, 8), ACT.Copy)
                            m.then_inc(g["combT"], 1)

                    norm("lora")
                    for s in range(SLOTS):
                        act.wait_ge(g["lora_z_ps"], nth(0, s))
                        act.activation(tmp(s, 0), bank(s, 1), ACT.Copy, scale=2.0).then_inc(g["lora_z"], 1)
                    exp_logits(0, 10)
                    turned(0, [(lambda s: tmp(s, 3)[0:8, :], 3)])

                    norm("x1")
                    for s in range(SLOTS):
                        act.wait_ge(g["x1_proj"], nth(0, s))
                        act.activation(kvT[s][:, 0:GC], bank(s, 1, 2), ACT.Identity, bias=V("bk1")).then_inc(g["x1_k"], 1)
                    for s in range(SLOTS):
                        act.wait_ge(g["x1_v"], nth(0, s))
                        act.activation(big[s][:, 0:GC], bank(s, 1, 2), ACT.Copy).then_inc(g["x1_v_sb"], 1)
                    for s in range(SLOTS):
                        act.wait_ge(g["x1_max"], nth(0, s))
                        for t in range(TILES):
                            m = act.activation(P[s][:, 128 * t:128 * t + 128], ps[s][:, 128 * t:128 * t + 128], ACT.Exp,
                                               bias=small[s][:, 16 + t:17 + t], scale=X1_SCALE, accum_out=small[s][:, 20 + t:21 + t])
                        m.then_inc(g["x1_exp"], 1)

                    def values(m_, k):
                        for s in range(SLOTS):
                            act.wait_ge(g["v_ps"], nth(m_, s))
                            vb = Vbd[s][:, :].rearrange("p (n c) -> p n c", c=18)
                            for hh in range(2):
                                p0 = 64 * hh
                                m = act.activation(vb[p0:p0 + 64, :, 9 * hh:9 * hh + 8],
                                                   bank(s, k, 1, p0, p0 + 64).rearrange("p (n d) -> p n d", d=HD), ACT.Copy)
                            m.then_inc(g["v_sb"], 1)

                    def project(m_, bias):
                        for s in range(SLOTS):
                            act.wait_ge(g["n_yT"], nth(m_, s))
                            act.activation(kvT[s][:, GT:2 * GT], bank(s, 1), ACT.Identity, bias=bias).then_inc(g["n_yT_sb"], 1)

                    def softmax_heads(v0):
                        for v in range(v0, v0 + TILES):
                            for s in range(SLOTS):
                                act.wait_ge(g["n_sub"], nth(v + 2, s))
                                act.activation(P[s][:, 0:1024], P[s][:, 0:1024], ACT.Exp, scale=HD ** -0.5).then_inc(g["n_exp"], 1)
                            for s in range(SLOTS):
                                act.wait_ge(g["n_pT"], nth(v, s))
                                act.activation(P[s][:, 1024:1536], bank(s, 2), ACT.Copy).then_inc(g["n_pT_act"], 1)

                    norm("lin")
                    for s in range(SLOTS):
                        act.wait_ge(g["n_proj"], nth(0, s))
                        act.activation(tmp(s, 2), bank(s, 1), ACT.Relu).then_inc(g["n_k"], 1)
                    values(0, 2)
                    project(0, 0.0)

                    def rms(n, ready):
                        for s in range(SLOTS):
                            ready(s)
                            act.activation(tmp(s, 0), Z[s][:, :], ACT.Square).then_inc(g["rms_sq"], 1)
                        for s in range(SLOTS):
                            act.wait_ge(g["rms_var"], nth(n, s))
                            act.activation(tmp(s, 0), bank(s, 1), ACT.Ln, bias=eps7[:, 0:1]).then_inc(g["rms_log"], 1)
                        for s in range(SLOTS):
                            act.wait_ge(g["rms_log"], nth(n, s))
                            act.activation(tmp(s, 1), tmp(s, 0), ACT.Exp, scale=-0.5).then_inc(g["rms_rstd"], 1)

                    norm("moe1")
                    rms(0, lambda s: act.wait_ge(g["normed"], nth(LN["moe1"], s)))
                    values(1, 0)
                    softmax_heads(0)
                    project(1, 0.0)
                    rms(1, lambda s: act.wait_ge(g["y_ready"], nth(0, s)))
                    exp_logits(1, MOE1_E)
                    turned(1, [(lambda s: tmp(s, 3)[0:8, :], 3)])
                    for k in range(MOE1_E * MOE1_C):
                        for s in range(SLOTS):
                            act.wait_ge(g["m1_h"], nth(k, s))
                            act.activation(P[s][:, 0:512], bank(s, 0), ACT.Tanh, scale=0.5).then_inc(g["m1_t"], 1)
                    act.preload_act_table_set(LN_EXP)

                    norm("x2")
                    norm("lat2")
                    kv_tokens(1)
                    heads(2, 8.0, False, 0)

                    norm("loc")
                    for s in range(SLOTS):
                        act.wait_ge(g["n_proj"], nth(2, s))
                        act.activation(tmp(s, 2), bank(s, 1), ACT.Identity, bias=V("bqkv", 1)).then_inc(g["n_k"], 1)
                    values(2, 2)
                    softmax_heads(4)
                    project(2, V("bqkv", 2))

                    def top1_experts(layer, func, b1):
                        for e in range(EXPERTS):
                            n = layer * EXPERTS + e
                            for s in range(SLOTS):
                                act.wait_ge(g["m2_h"], nth(n, s))
                                act.activation(P[s][:, 512 * (e % 2):512 * (e % 2) + 512], bank(s, 0), func, bias=V(b1, e))\
                                    .then_inc(g["m2_act"], 1)

                    norm("moe2")
                    exp_logits(2, EXPERTS)
                    turned(2, [(lambda s: tmp(s, 3)[0:8, :], 3), (lambda s: mTb[s][0:8, :], 3), (lambda s: tmp(s, 2)[0:8, :], 2)])
                    for s in range(SLOTS):
                        act.wait_ge(g["g_bc"], nth(0, s))
                        act.activation(tmp(s, 0), bank(s, 0), ACT.Copy).then_inc(g["g_sb"], 1)
                    top1_experts(0, ACT.Relu, "moe2_b1")

                    norm("x3")

                    norm("ssm")
                    for s in range(SLOTS):
                        act.wait_ge(g["ssm_in"], nth(0, s))
                        act.wait_ge(g["ssm_pad"], nth(0, s))
                        act.activation(padded(s)[:, :, 3:67], bank(s, 0, 2).rearrange("p (n t) -> p n t", t=SEQ), ACT.Copy)\
                           .then_inc(g["ssm_xp"], 1)
                        act.activation(tmp(s, 2, 2), bank(s, 2, 2), ACT.Tanh, scale=0.5).then_inc(g["ssm_zt"], 1)
                    for s in range(SLOTS):
                        act.wait_ge(g["ssm_conv"], nth(0, s))
                        act.activation(P[s][:, 0:1024], big[s][:, 2048:3072], ACT.Tanh, scale=0.5).then_inc(g["ssm_t"], 1)
                    act.preload_act_table_set(LN_EXP)

                    norm("moe3")
                    turned(3, [(lambda s: tmp(s, 3)[0:8, :], 3), (lambda s: mTb[s][0:8, :], 3)])
                    top1_experts(1, ACT.Gelu, "moe3_b1")

                @block.vector
                def _(dve):
                    links = [0]

                    def link(ins):
                        links[0] += 1
                        ins.then_inc(g["chain"], 1)
                        dve.wait_ge(g["chain"], links[0])

                    def norm(name, dst, eps=1e-5):
                        n = LN[name]
                        for s in range(SLOTS):
                            dve.wait_ge(g["rstd"], nth(n, s))
                            dve.tensor_tensor(dst(s), bank(s, 0), tmp(s, 1), ALU.mult).then_inc(g["normed"], 1)

                    def kv(n, name, wm, bm, wl, bl):
                        for s in range(SLOTS):
                            view = kvT[s][:, :].rearrange("p (b k) -> p b k", k=KEYS)
                            dve.tensor_scalar(view[:, :, 0:CTX], ctxz[s][:, :].rearrange("p (b k) -> p b k", k=CTX),
                                              V(wm), V(bm), ALU.mult, ALU.add)
                            dve.wait_ge(g["normed"], nth(LN[name], s))
                            dve.tensor_scalar(view[:, :, CTX:KEYS], seqs(A[s][:, :]), V(wl), V(bl), ALU.mult, ALU.add)\
                               .then_inc(g["kv_ready"], 1)
                        for s in range(SLOTS):
                            dve.wait_ge(g["kvn_ps"], nth(n, s))
                            dve.tensor_copy(T[s][0:64, GC:2 * GC], bank(s, 2, 2, 0, 64)).then_inc(g["kvl_ready"], 1)

                    def heads(gi, scale, bias, h0):
                        for r in range(2):
                            for s in range(SLOTS):
                                dve.wait_ge(g["qp_ps"], nth(2 * gi + r, s))
                                for k in (0, 1):
                                    h = 4 * r + k
                                    if bias:
                                        m = dve.tensor_scalar(by_head(s, h), seqs(bank(s, k)), scale,
                                                              qb(h0 + h), ALU.mult, ALU.add)
                                    else:
                                        m = dve.tensor_scalar(by_head(s, h), seqs(bank(s, k)), scale, None, ALU.mult)
                                m.then_inc(g["qp_dve"], 1)
                        for b in range(GB):
                            u = gi * GB + b
                            for s in range(SLOTS):
                                dve.wait_ge(g["scores"], nth(u, s))
                                view = bank(s, 0, 2).rearrange("p (a k) -> p a k", k=BANK)[:, :, 0:2 * KEYS]
                                dve.tensor_reduce(small[s][:, 0:4].rearrange("p (a c) -> p a c", c=2),
                                                  view.rearrange("p a (c k) -> p a c k", k=KEYS), AX.X, ALU.max,
                                                  negate=True).then_inc(g["maxed"], 1)
                            for s in range(SLOTS):
                                dve.wait_ge(g["exped"], nth(u, s))
                                dve.reciprocal(small[s][:, 12:16], small[s][:, 8:12]).then_inc(g["rsum"], 1)
                            for s in range(SLOTS):
                                dve.wait_ge(g["pT_ps"], nth(u, s))
                                dve.tensor_copy(P[s][0:64, 1536:2048], bank(s, 3, 1, 0, 64)).then_inc(g["pT_dve"], 1)
                            for s in range(SLOTS):
                                dve.wait_ge(g["mixed"], nth(u, s))
                                dve.tensor_copy(big[s][:, BANK * b:BANK * b + BANK], bank(s, 0)).then_inc(g["mix_out"], 1)
                        for s in range(SLOTS):
                            dve.wait_ge(g["heads_ps"], nth(gi, s))
                            if gi == 0:
                                dve.scalar_tensor_tensor(X[s][:, :], bank(s, 1), obias0[:, 0:1], X[s][:, :], ALU.add, ALU.add)\
                                   .then_inc(g["x_added"], 1)
                            else:
                                dve.tensor_tensor(X[s][:, :], bank(s, 1), X[s][:, :], ALU.add).then_inc(g["x_added"], 1)

                    norm("ctx0", lambda s: ctxz[s][:, 0:GT])
                    norm("ctx1", lambda s: ctxz[s][:, GT:GC])
                    norm("x0", lambda s: Z[s][:, :])
                    norm("lat0", lambda s: A[s][:, :])
                    kv(0, "lat0", "lmw", "lmb", "llw", "llb")
                    heads(0, 0.125, True, 0)
                    heads(1, 0.125, True, 8)

                    def add_to_x(done, n, k, bias=None):
                        for s in range(SLOTS):
                            dve.wait_ge(done, nth(n, s))
                            if bias is None:
                                dve.tensor_tensor(X[s][:, :], bank(s, k), X[s][:, :], ALU.add).then_inc(g["x_added"], 1)
                            else:
                                dve.scalar_tensor_tensor(X[s][:, :], bank(s, k), bias, X[s][:, :], ALU.add, ALU.add).then_inc(g["x_added"], 1)

                    def to_z(s):
                        return Z[s][:, :]

                    norm("rnn", to_z)
                    for s in range(SLOTS):
                        dve.wait_ge(g["rnn_in"], nth(0, s))
                        m = dve.tensor_scalar(big[s][:, 0:1024], bank(s, 0, 2), 0.0, 0.5, ALU.max, ALU.add)
                    link(m)
                    for s in range(SLOTS):
                        dve.wait_ge(g["rnn_pool"], nth(0, s))
                        m = dve.tensor_tensor(big[s][:, 1024:2048], big[s][:, 0:1024], tmp(s, 0, 2), ALU.mult)
                    link(m)
                    for s in range(SLOTS):
                        for k in range(2):
                            m = dve.tensor_tensor_scan(big[s][:, 2048 + GT * k:2048 + GT * k + GT], tmp(s, 2 + k),
                                                       big[s][:, 1024 + GT * k:1024 + GT * k + GT], 0.0, ALU.mult, ALU.add)
                        m.then_inc(g["rnn_h"], 1)
                    add_to_x(g["rnn_out"], 0, 0)

                    def each(op):
                        for s in range(SLOTS):
                            m = op(s)
                        link(m)

                    def router(n, e, top):
                        wide = max(e, 8)
                        if wide > e:
                            each(lambda s: dve.memset(route(s, L, wide), NEG))
                        for s in range(SLOTS):
                            dve.wait_ge(g["logits"], nth(n, s))
                        each(lambda s: dve.tensor_copy(route(s, L, e), ps[s][:, 0:64].rearrange("p (t e) -> p t e", e=16)[:, :, 0:e]))
                        for s in range(SLOTS):
                            for t in range(TILES):
                                m = dve.max(small[s][:, M8 + 8 * t:M8 + 8 * t + 8], small[s][:, L + 16 * t:L + 16 * t + wide])
                        link(m)
                        if n != 3:
                            for s in range(SLOTS):
                                dve.tensor_tensor(route(s, U, e), route(s, L, e), over_e(s, M8, 0, e), ALU.subtract).then_inc(g["shifted"], 1)
                        for s in range(SLOTS):
                            for t in range(TILES):
                                m = dve.max_index(idx[s][:, 8 * t:8 * t + 8], small[s][:, M8 + 8 * t:M8 + 8 * t + 8],
                                                  small[s][:, L + 16 * t:L + 16 * t + wide])
                        link(m)
                        each(lambda s: dve.tensor_copy(small[s][:, IXF:IXF + 32], idx[s][:, :]))
                        iota = over(C("iota")[:, 0:e], 1, [128, TILES, e])
                        each(lambda s: dve.tensor_tensor(route(s, OH, e), iota, over_e(s, IXF, 0, e), ALU.is_equal))
                        if top == 2:
                            each(lambda s: dve.tensor_tensor(route(s, OH1, e), iota, over_e(s, IXF, 1, e), ALU.is_equal))
                            each(lambda s: dve.tensor_tensor(route(s, OH, e), route(s, OH, e), route(s, OH1, e), ALU.add))

                    def top2_weights(n, e):
                        for s in range(SLOTS):
                            dve.wait_ge(g["u_exp"], nth(n, s))
                        if e < 8:
                            each(lambda s: dve.memset(comb(s, CW), 0.0))
                        k = min(e, 8)
                        each(lambda s: dve.tensor_tensor(comb(s, CW)[:, :, 0:k], route(s, U, k), route(s, OH, k), ALU.mult))
                        each(lambda s: dve.tensor_reduce(small[s][:, DN:DN + 4], comb(s, CW), AX.X, ALU.add))
                        if e > 8:
                            each(lambda s: dve.tensor_scalar(small[s][:, DN + 4:DN + 8], small[s][:, DN:DN + 4], 0.0, None, ALU.is_equal))
                            each(lambda s: dve.tensor_tensor(small[s][:, DN:DN + 4], small[s][:, DN:DN + 4], small[s][:, DN + 4:DN + 8], ALU.add))
                        each(lambda s: dve.reciprocal(small[s][:, DN + 8:DN + 12], small[s][:, DN:DN + 4]))
                        for s in range(SLOTS):
                            dve.tensor_tensor(comb(s, CW), comb(s, CW), over(small[s][:, DN + 8:DN + 12], 2, [128, TILES, 8]), ALU.mult)\
                               .then_inc(g["comb"], 1)

                    norm("lora", to_z)
                    router(0, 10, 2)
                    top2_weights(0, 10)
                    for s in range(SLOTS):
                        dve.wait_ge(g["lora_b"], nth(0, s))
                        dve.tensor_tensor(tmp(s, 1), tmp(s, 0), bank(s, 1), ALU.mult).then_inc(g["lora_zs"], 1)
                    add_to_x(g["lora_out"], 0, 2, V("base_b"))

                    norm("x1", to_z)
                    for s in range(SLOTS):
                        dve.wait_ge(g["x1_proj"], nth(0, s))
                        dve.tensor_scalar(A[s][:, :], bank(s, 0), V("bq1"), None, ALU.add).then_inc(g["x1_q"], 1)
                    for s in range(SLOTS):
                        dve.wait_ge(g["x1_s"], nth(0, s))
                        m = dve.tensor_reduce(small[s][:, 12:16], bank(s, 0).rearrange("p (t k) -> p t k", k=CTX), AX.X, ALU.max,
                                              negate=True)
                    link(m)
                    for s in range(SLOTS):
                        dve.tensor_scalar(small[s][:, 16:20], small[s][:, 12:16], X1_SCALE, None, ALU.mult).then_inc(g["x1_max"], 1)
                    for s in range(SLOTS):
                        dve.wait_ge(g["x1_exp"], nth(0, s))
                        dve.reciprocal(small[s][:, 24:28], small[s][:, 20:24]).then_inc(g["x1_sum"], 1)
                    for s in range(SLOTS):
                        dve.wait_ge(g["x1_pT"], nth(0, s))
                        dve.tensor_copy(P[s][:, 512:1024], bank(s, 3)).then_inc(g["x1_pT_sb"], 1)
                    add_to_x(g["x1_o"], 0, 0, V("bv1"))

                    def head_out(u, at, tiles, eps):
                        n = tiles * NH
                        for s in range(SLOTS):
                            dve.wait_ge(g["n_o"], nth(u, s))
                            both = ps[s][:, 0:9 * n].rearrange("p (h c) -> p h c", c=9)
                            rec = small[s][:, 16:16 + n].unsqueeze(2)
                            if eps:
                                link(dve.tensor_scalar(rec, both[:, :, 8:9], eps, None, ALU.add))
                                link(dve.reciprocal(rec, rec))
                            else:
                                link(dve.reciprocal(rec, both[:, :, 8:9]))
                            dve.tensor_tensor(kvT[s][:, at:at + HD * n].rearrange("p (h d) -> p h d", d=HD), both[:, :, 0:8],
                                              over(small[s][:, 16:16 + n], 2, [128, n, HD]), ALU.mult).then_inc(g["n_y"], 1)

                    def softmax_heads(u0, v0):
                        for t in range(TILES):
                            u, v = u0 + t, v0 + t
                            for s in range(SLOTS):
                                dve.wait_ge(g["n_s"], nth(u, s))
                                sc = bank(s, 0, 2).rearrange("p (h k) -> p h k", k=SEQ)
                                link(dve.tensor_reduce(small[s][:, 0:16], sc, AX.X, ALU.max))
                                dve.tensor_tensor(P[s][:, 0:1024].rearrange("p (h k) -> p h k", k=SEQ), sc,
                                                  over(small[s][:, 0:16], 2, [128, NH, SEQ]), ALU.subtract).then_inc(g["n_sub"], 1)
                            for s in range(SLOTS):
                                dve.wait_ge(g["n_pT"], nth(v, s))
                                dve.tensor_copy(P[s][:, 1536:2048], bank(s, 3)).then_inc(g["n_pT_dve"], 1)
                            head_out(u, 128 * t, 1, 0.0)

                    norm("lin", to_z)
                    for s in range(SLOTS):
                        dve.wait_ge(g["n_proj"], nth(0, s))
                        dve.tensor_scalar(A[s][:, :], bank(s, 0), 0.0, None, ALU.max).then_inc(g["n_q"], 1)
                    for r in range(2):
                        for s in range(SLOTS):
                            dve.wait_ge(g["n_s"], nth(r, s))
                            dve.tensor_tensor(P[s][:, :].rearrange("p (n t) -> p n t", t=SEQ),
                                              ps[s][:, :].rearrange("p (n t) -> p n t", t=SEQ),
                                              over(C("causal_T"), 1, [128, 32, SEQ]), ALU.mult).then_inc(g["n_sub"], 1)
                        head_out(r, 256 * r, 2, 1e-5)
                    add_to_x(g["n_out"], 0, 2)

                    def rms(n, gain):
                        for s in range(SLOTS):
                            dve.wait_ge(g["rms_rstd"], nth(n, s))
                            dve.scalar_tensor_tensor(A[s][:, :], Z[s][:, :], gain, tmp(s, 1), ALU.mult, ALU.mult).then_inc(g["rms_done"], 1)

                    norm("moe1", to_z)
                    rms(0, V("g1"))
                    for s in range(SLOTS):
                        dve.wait_ge(g["n_proj"], nth(1, s))
                        for k in range(4):
                            m = dve.tensor_tensor(seqs(tmp(s, k)), seqs(bank(s, k)),
                                                  over(C("sin" if k % 2 else "cos"), 1, [128, GB, SEQ]), ALU.mult)
                        m.then_inc(g["rope_dve"], 1)
                    softmax_heads(2, 0)
                    for s in range(SLOTS):
                        dve.wait_ge(g["n_out"], nth(1, s))
                        dve.tensor_tensor(Z[s][:, :], bank(s, 2), Z[s][:, :], ALU.add).then_inc(g["y_ready"], 1)
                    rms(1, V("g2"))
                    router(1, MOE1_E, 2)
                    top2_weights(1, MOE1_E)
                    for e in range(MOE1_E):
                        for s in range(SLOTS):
                            dve.wait_ge(g["m1_bc"], nth(e, s))
                            dve.tensor_tensor(tmp(s, e % 2), A[s][:, :], bank(s, 3), ALU.mult).then_inc(g["m1_x"], 1)
                        for c in range(MOE1_C):
                            k = e * MOE1_C + c
                            for s in range(SLOTS):
                                dve.wait_ge(g["m1_t"], nth(k, s))
                                m = dve.scalar_tensor_tensor(P[s][:, 512:1024], P[s][:, 0:512], 1.0, bank(s, 0), ALU.add, ALU.mult)
                            link(m)
                            for s in range(SLOTS):
                                dve.scalar_tensor_tensor(P[s][:, 1024 + 512 * (k % 2):1536 + 512 * (k % 2)], P[s][:, 512:1024], 0.5,
                                                         bank(s, 1), ALU.mult, ALU.mult).then_inc(g["m1_g"], 1)
                    for s in range(SLOTS):
                        dve.wait_ge(g["m1_out"], nth(0, s))
                        m = dve.tensor_tensor(Z[s][:, :], bank(s, 2), Z[s][:, :], ALU.add)
                    link(m)
                    for s in range(SLOTS):
                        dve.tensor_tensor(X[s][:, :], Z[s][:, :], X[s][:, :], ALU.add).then_inc(g["x_added"], 1)

                    norm("x2", to_z)
                    norm("lat2", lambda s: A[s][:, :])
                    kv(1, "lat2", "gm", "bm", "gl", "bl")
                    heads(2, 8.0, False, 0)

                    norm("loc", to_z)
                    for s in range(SLOTS):
                        dve.wait_ge(g["n_proj"], nth(2, s))
                        dve.tensor_scalar(tmp(s, 0), bank(s, 0), V("bqkv", 0), None, ALU.add).then_inc(g["n_q"], 1)
                    softmax_heads(6, 4)
                    add_to_x(g["n_out"], 2, 2, V("bo2"))

                    def top1_experts(layer):
                        for e in range(EXPERTS):
                            n = layer * EXPERTS + e
                            for s in range(SLOTS):
                                dve.wait_ge(g["m2_act"], nth(n, s))
                                dve.wait_ge(g["m2_mask"], nth(n, s))
                                dve.tensor_tensor(P[s][:, 1024 + 512 * (e % 2):1536 + 512 * (e % 2)],
                                                  P[s][:, 512 * (e % 2):512 * (e % 2) + 512], bank(s, 1), ALU.mult).then_inc(g["m2_m"], 1)

                    norm("moe2", to_z)
                    router(2, EXPERTS, 1)
                    for s in range(SLOTS):
                        dve.tensor_copy(ohb[s][:, :].rearrange("p (t e) -> p t e", e=8), route(s, OH, 8)).then_inc(g["onehot"], 1)
                    for s in range(SLOTS):
                        dve.wait_ge(g["u_exp"], nth(2, s))
                    each(lambda s: dve.tensor_reduce(small[s][:, DN:DN + 4], route(s, U, 8), AX.X, ALU.add))
                    each(lambda s: dve.reciprocal(small[s][:, DN + 8:DN + 12], small[s][:, DN:DN + 4]))
                    for s in range(SLOTS):
                        dve.wait_ge(g["cum_ps"], nth(0, s))
                        link(dve.tensor_tensor(comb(s, G8), ps[s][:, BANK:BANK + 32].rearrange("p (t e) -> p t e", e=8),
                                               over(count[:, :], 1, [128, TILES, 8]), ALU.add))
                        link(dve.tensor_tensor(count[:, :], count[:, :], ps[s][:, BANK + 32:BANK + 40], ALU.add))
                        link(dve.scalar_tensor_tensor(comb(s, CW), comb(s, G8), float(CAPACITY), route(s, OH, 8), ALU.is_lt, ALU.mult))
                        dve.tensor_tensor(comb(s, G8), comb(s, CW), over(small[s][:, DN + 8:DN + 12], 2, [128, TILES, 8]), ALU.mult)\
                           .then_inc(g["comb"], 1)
                    for s in range(SLOTS):
                        dve.wait_ge(g["g_sb"], nth(0, s))
                        dve.tensor_tensor(A[s][:, :], Z[s][:, :], tmp(s, 0), ALU.mult).then_inc(g["xg"], 1)
                    top1_experts(0)
                    for s in range(SLOTS):
                        dve.wait_ge(g["m2_out"], nth(0, s))
                        m = dve.tensor_tensor(A[s][:, :], tmp(s, 0), bank(s, 2), ALU.mult)
                    link(m)
                    for s in range(SLOTS):
                        dve.tensor_tensor(X[s][:, :], X[s][:, :], A[s][:, :], ALU.add).then_inc(g["x_added"], 1)

                    for s in range(SLOTS):
                        dve.tensor_reduce(small[s][:, 0:8], ctxT[s][:, :].rearrange("p (b k) -> p b k", k=CTX), AX.X, ALU.add)\
                           .then_inc(g["x3_sum"], 1)
                    norm("x3", to_z)
                    for s in range(SLOTS):
                        dve.wait_ge(g["x3_ps"], nth(0, s))
                        dve.tensor_scalar(small[s][:, 8:16], ps[s][:, BANK:BANK + GB], 1.0 / CTX, V("b3"), ALU.mult, ALU.add)
                        m = dve.tensor_tensor(X[s][:, :], X[s][:, :], bank(s, 0), ALU.add)
                    link(m)
                    for s in range(SLOTS):
                        dve.tensor_tensor(seqs(X[s][:, :]), seqs(X[s][:, :]), over(small[s][:, 8:16], 2, [128, GB, SEQ]), ALU.add)\
                           .then_inc(g["x_added"], 1)

                    norm("ssm", to_z)
                    for s in range(SLOTS):
                        dve.wait_ge(g["ssm_xp"], nth(0, s))
                    cacc = lambda s, k: seqs(big[s][:, 2048 + GT * k:2048 + GT * k + GT])
                    for k in range(2):
                        each(lambda s: dve.tensor_scalar(cacc(s, k), padded(s)[:, GB * k:GB * k + GB, 3:67], V("conv_w", 4 * k + 3),
                                                         V("conv_b", k), ALU.mult, ALU.add))
                        for tap in range(3):
                            for s in range(SLOTS):
                                m = dve.scalar_tensor_tensor(cacc(s, k), padded(s)[:, GB * k:GB * k + GB, tap:tap + SEQ],
                                                             V("conv_w", 4 * k + tap), cacc(s, k), ALU.mult, ALU.add)
                                if k == 1 and tap == 2:
                                    m.then_inc(g["ssm_conv"], 1)
                            if not (k == 1 and tap == 2):
                                link(m)
                    for s in range(SLOTS):
                        dve.wait_ge(g["ssm_t"], nth(0, s))
                        dve.scalar_tensor_tensor(P[s][:, 1024:2048], P[s][:, 0:1024], 1.0, big[s][:, 2048:3072], ALU.add, ALU.mult)\
                           .then_inc(g["ssm_x"], 1)
                    for s in range(SLOTS):
                        dve.wait_ge(g["ssm_u"], nth(0, s))
                        m = dve.tensor_scalar(tmp(s, 0)[0:STATE, :], bank(s, 0, 1, 0, STATE), 0.05, None, ALU.mult)
                    link(m)
                    for s in range(SLOTS):
                        dve.tensor_tensor_scan(tmp(s, 1)[0:STATE, :], C("decay")[0:STATE, :], tmp(s, 0)[0:STATE, :], 0.0,
                                               ALU.mult, ALU.add).then_inc(g["ssm_h"], 1)
                    for s in range(SLOTS):
                        dve.wait_ge(g["ssm_zt"], nth(0, s))
                        m = dve.scalar_tensor_tensor(tmp(s, 2, 2), tmp(s, 2, 2), 1.0, bank(s, 2, 2), ALU.add, ALU.mult)
                    link(m)
                    for s in range(SLOTS):
                        dve.wait_ge(g["ssm_y"], nth(0, s))
                        dve.scalar_tensor_tensor(P[s][:, 0:1024], tmp(s, 2, 2), 0.5, bank(s, 0, 2), ALU.mult, ALU.mult)\
                           .then_inc(g["ssm_g"], 1)
                    add_to_x(g["ssm_out"], 0, 2)

                    norm("moe3", to_z)
                    router(3, EXPERTS, 1)
                    for s in range(SLOTS):
                        dve.tensor_copy(comb(s, CW), route(s, OH, 8)).then_inc(g["comb"], 1)
                    top1_experts(1)
                    add_to_x(g["m2_out"], 1, 2)

                @block.gpsimd
                def _(pool):
                    def heads(gi):
                        for b in range(GB):
                            u = gi * GB + b
                            for s in range(SLOTS):
                                pool.wait_ge(g["rsum"], nth(u, s))
                                view = P[s][:, 0:4 * KEYS].rearrange("p (a k) -> p a k", k=KEYS)
                                pool.tensor_tensor(view, view, over(small[s][:, 12:16], 2, [128, 4, KEYS]), ALU.mult)\
                                    .then_inc(g["p_ready"], 1)

                    heads(0)
                    heads(1)

                    links = [0]

                    def link(ins):
                        links[0] += 1
                        ins.then_inc(g["pool_chain"], 1)
                        pool.wait_ge(g["pool_chain"], links[0])

                    for s in range(SLOTS):
                        pool.wait_ge(g["rnn_tanh"], nth(0, s))
                        link(pool.tensor_scalar(tmp(s, 2, 2), tmp(s, 0, 2), -0.5, 0.5, ALU.mult, ALU.add))
                        link(pool.memset(tmp(s, 2, 2).rearrange("p (n t) -> p n t", t=SEQ)[:, :, 0:1], 0.0))
                        pool.tensor_scalar(tmp(s, 0, 2), tmp(s, 0, 2), 0.5, 0.5, ALU.mult, ALU.add).then_inc(g["rnn_pool"], 1)

                    for s in range(SLOTS):
                        pool.wait_ge(g["x1_sum"], nth(0, s))
                        view = P[s][:, 0:512].rearrange("p (t k) -> p t k", k=CTX)
                        pool.tensor_tensor(view, view, over(small[s][:, 24:28], 2, [128, TILES, CTX]), ALU.mult).then_inc(g["x1_p"], 1)

                    def spread(s, b, src, at):
                        return pool.tensor_tensor(big[s][:, at:at + 1024].rearrange("p (h t) -> p h t", t=SEQ),
                                                  over(src[:, SEQ * b:SEQ * b + SEQ], 1, [128, NH, SEQ]),
                                                  over(C("hmask"), 2, [128, NH, SEQ]), ALU.mult)

                    for r in range(2):
                        for s in range(SLOTS):
                            if r == 0:
                                pool.wait_ge(g["n_q"], nth(0, s))
                            else:
                                pool.wait_ge(g["n_s"], nth(0, s))
                            for bb in range(4):
                                m = spread(s, 4 * r + bb, A[s], 1024 * bb)
                            m.then_inc(g["bd_ready"], 1)

                    def keys(u0, k):
                        for t in range(TILES):
                            for s in range(SLOTS):
                                if t >= 2:
                                    pool.wait_ge(g["n_s"], nth(u0 + t - 2, s))
                                for bb in range(2):
                                    m = spread(s, 2 * t + bb, tmp(s, 2), 2048 * (t % 2) + 1024 * bb)
                                m.then_inc(g["bd_ready"], 1)

                    for s in range(SLOTS):
                        pool.wait_ge(g["rope_dve"], nth(0, s))
                        pool.tensor_tensor(tmp(s, 0), tmp(s, 0), tmp(s, 1), ALU.add)
                        link(pool.tensor_tensor(tmp(s, 2), tmp(s, 2), tmp(s, 3), ALU.add))
                    keys(2, 1)

                    heads(2)

                    for s in range(SLOTS):
                        pool.wait_ge(g["n_k"], nth(1, s))
                    keys(6, 2)

                    for s in range(SLOTS):
                        pool.wait_ge(g["normed"], nth(LN["ssm"], s))
                        pool.memset(padded(s)[:, :, 0:3], 0.0).then_inc(g["ssm_pad"], 1)

            nc.all_engine_barrier(sems_to_clear=clear)


def pack(i):
    def heads_T(w):
        return w.T.reshape(-1, 128, 128).transpose(1, 0, 2).reshape(128, -1)

    def rows_of(w, n):
        return w.reshape(n, 128, -1).transpose(1, 0, 2).reshape(128, -1)

    def at(p, a):
        out = np.zeros((128, a.shape[-1]), np.float32)
        out[:p] = a
        return out

    def per_partition(v, n):
        return v.reshape(n, 128).T

    half = HD // 2
    swap = np.arange(D).reshape(-1, HD)
    swap = np.concatenate([swap[:, half:], swap[:, :half]], axis=1).ravel()
    kv_rep = np.arange(32).reshape(4, 1, HD).repeat(4, axis=1).ravel()
    wkv0, wkv2, wqkv = i["L0_xattn_Wkv"], i["L2_xattn_Wkv"], i["L1_attn_wqkv"]
    lq, bqkv = i["L2_attn_w_qkv"], i["L2_attn_b_qkv"]
    wk_rep = i["L1_ffn_wk"][:, kv_rep]
    fold = dict(q0T=heads_T(i["L0_xattn_Wq"]), k0T=heads_T(wkv0[:, :1024]), v0T=heads_T(wkv0[:, 1024:]),
                o0=rows_of(i["L0_xattn_Wout"], 8), q2T=heads_T(i["L2_xattn_Wq"]), k2T=heads_T(wkv2[:, :512]),
                v2T=heads_T(wkv2[:, 512:]), o2=rows_of(i["L2_xattn_Wout"], 4))
    one = lambda n: i[n].reshape(128, 1)
    cols = dict(lmw=one("L0_xattn_ln_media_w"), lmb=one("L0_xattn_ln_media_b"), llw=one("L0_xattn_ln_lat_w"),
                llb=one("L0_xattn_ln_lat_b"), bout0=one("L0_xattn_bout"), bq0=per_partition(i["L0_xattn_bq"], 8),
                bv0=per_partition(i["L0_xattn_bkv"][1024:], 8), base_b=one("L0_ffn_base_b"), bq1=one("L1_xattn_bq"),
                bk1=one("L1_xattn_bk"), bv1=one("L1_xattn_bv"), g1=one("L1_ffn_g1"), g2=one("L1_ffn_g2"),
                gm=one("L2_xattn_gm"), bm=one("L2_xattn_bm"), gl=one("L2_xattn_gl"), bl=one("L2_xattn_bl"),
                bqkv=per_partition(bqkv, 3), bo2=one("L2_attn_b_out"), moe2_b1=i["L2_ffn_b1"].T, b3=one("L3_xattn_b"),
                conv_w=i["L3_attn_conv_w"].reshape(2, 128, 4).transpose(1, 0, 2).reshape(128, 8),
                conv_b=per_partition(i["L3_attn_conv_b"], 2), moe3_b1=i["L3_ffn_b1"].T,
                br=at(1, i["L2_ffn_br"]), bg=at(1, i["L3_ffn_bg"]))
    experts = lambda w: w.transpose(1, 0, 2).reshape(128, -1)
    wts = dict(hg=i["L0_attn_W_hg"], rnn_out=rows_of(i["L0_attn_W_out"], 2), base=i["L0_ffn_base_w"].T,
               gate0=i["L0_ffn_gate_w"].T, loraA=i["L0_ffn_lora_A"].reshape(128, 128).T,
               loraB=i["L0_ffn_lora_B"].transpose(0, 2, 1).reshape(128, 128),
               q1=i["L1_xattn_Wq"], k1=i["L1_xattn_Wk"], v1=i["L1_xattn_Wv"],
               lin_q=wqkv[:, :128], lin_k=wqkv[:, 128:256], lin_v=wqkv[:, 256:], lin_o=i["L1_attn_wo"],
               rq=i["L1_ffn_wq"], rqp=i["L1_ffn_wq"][:, swap], rk=wk_rep, rkp=wk_rep[:, swap],
               rv=i["L1_ffn_wv"][:, kv_rep], ro=i["L1_ffn_wo"], gate1=i["L1_ffn_gate"],
               w1=experts(i["L1_ffn_w1"]), w3=experts(i["L1_ffn_w3"]), w2=rows_of(i["L1_ffn_w2"].reshape(-1, 128), 12),
               loc_q=lq[:, :128], loc_k=lq[:, 128:256], loc_v=lq[:, 256:], loc_o=i["L2_attn_w_out"],
               moe2_r=i["L2_ffn_Wr"], moe2_w1=experts(i["L2_ffn_W1"]), moe2_w2=experts(i["L2_ffn_W2"]),
               moe2_b2=at(8, i["L2_ffn_b2"]), x3a=i["L3_xattn_W"][:, :128].T, x3b=i["L3_xattn_W"][:, 128:].T,
               ssm_in=i["L3_attn_w_in"], ssm_B=rows_of(i["L3_attn_w_B"], 2), ssm_C=at(16, i["L3_attn_w_C"]),
               ssm_out=rows_of(i["L3_attn_w_out"], 2), moe3_r=i["L3_ffn_Wg"], moe3_w1=experts(i["L3_ffn_W1"]),
               moe3_w2=experts(i["L3_ffn_W2"]), moe3_b2=at(8, i["L3_ffn_b2"]))
    return [np.concatenate([parts[n] for n, _ in table], axis=1)
            for table, parts in ((FOLD, fold), (COLUMNS, cols), (WEIGHTS, wts))]


def shape_constants():
    p = np.arange(128)
    half = HD // 2
    inv = (np.float32(1.0) / np.float32(10000.0) ** (np.arange(0, HD, 2, dtype=np.float32) / np.float32(HD))).astype(np.float32)
    angle = np.arange(SEQ, dtype=np.float32)[None, :] * inv[p % half][:, None]
    sign = np.where(p % HD < half, -1.0, 1.0)[:, None]
    q, k = p[:, None] % SEQ, np.arange(SEQ)[None, :]
    decay = np.full((128, GT), 0.9)
    decay[:, ::SEQ] = 0.0
    c = dict(ident=np.eye(128), center=np.eye(128) - 1.0 / 128, mean=np.full((128, 128), 1.0 / 128),
             hmask=(p[:, None] // HD == np.arange(NH)[None, :]), cos=np.cos(angle), sin=np.sin(angle) * sign,
             causal_add=np.where(k <= q, 0.0, NEG), causal_T=(k >= q), upto=(p[:, None] <= p[None, :]),
             iota=np.broadcast_to(np.arange(16), (128, 16)), lora_sel=(p[:, None] == p[None, :] // LORA_R),
             decay=decay, ones_row=np.ones((128, 128)))
    return np.concatenate([np.asarray(c[n], np.float32) for n, _ in CONSTS], axis=1)


def kernel(**inputs):
    import concourse.bacc as bacc
    from concourse.bass_utils import run_bass_kernel_spmd

    i = {k: np.asarray(v) for k, v in inputs.items()}
    fold, cols, wts = pack(i)
    arrays = {"x_dram": i["x"].reshape(BATCH * SEQ, D).T, "ctx_dram": i["ctx_1024"].reshape(BATCH * CTX, D).T,
              "fold_dram": fold, "cols_dram": cols, "weights_dram": wts, "consts_dram": shape_constants()}
    arrays = {k: np.ascontiguousarray(v) for k, v in arrays.items()}
    nc = bacc.Bacc("TRN2", target_bir_lowering=False, num_devices=1)
    f32 = mybir.dt.float32
    args = [nc.dram_tensor(k, v.shape, f32, kind="ExternalInput").ap() for k, v in arrays.items()]
    out = nc.dram_tensor("out_dram", (D, BATCH * SEQ), f32, kind="ExternalOutput").ap()
    build(nc, *args, out)
    r = run_bass_kernel_spmd(nc, [arrays], core_ids=[0])
    return np.ascontiguousarray(r.results[0]["out_dram"].T).reshape(BATCH, SEQ, D)
```

```python
import numpy as np
from contextlib import ExitStack

import concourse.bass as bass
from concourse import mybir

D = 128
BATCH, SEQ, CTX = 64, 64, 128
SLOTS = 2
GB = 8
GT = GB * SEQ
GC = GB * CTX
TILES = GT // 128
PASSES = BATCH // (GB * SLOTS)
BANK = 512
KEYS = CTX + SEQ
H0, H2, DH = 16, 8, 64
NH, HD = 16, 8
INNER = 256
LORA_E, LORA_R = 8, 16
MOE1_E, MOE1_C = 4, 3
MOE1_K = MOE1_E * MOE1_C
H3 = (0, 1, 3)
EXPERTS = 8
CAPACITY = BATCH * SEQ // EXPERTS
STATE = 16
NEG = -1.0e30

FOLD = [("q0T", 1024), ("k0T", 1024), ("v0T", 1024), ("o0", 1024), ("q2T", 512), ("k2T", 512), ("v2T", 512), ("o2", 512)]
COLUMNS = [("lmw", 1), ("lmb", 1), ("llw", 1), ("llb", 1), ("bout0", 1), ("bq0", 8), ("bv0", 8), ("base_b", 1),
           ("bq1", 1), ("bk1", 1), ("bv1", 1), ("g1", 1), ("g2", 1), ("gm", 1), ("bm", 1), ("gl", 1), ("bl", 1),
           ("bqkv", 3), ("bo2", 1), ("moe2_b1", 8), ("b3", 1), ("conv_w", 8), ("conv_b", 2), ("moe3_b1", 8),
           ("br", 8), ("bg", 8)]
WEIGHTS = [("hg", 512), ("rnn_out", 256), ("base", 128), ("gate0", 10), ("loraA", 128), ("loraB", 128),
           ("q1", 128), ("k1", 128), ("v1", 128), ("lin_q", 128), ("lin_k", 128), ("lin_v", 128), ("lin_o", 128),
           ("rq", 128), ("rqp", 128), ("rk", 128), ("rkp", 128), ("rv", 128), ("ro", 128), ("gate1", 4),
           ("w1", 1536), ("w3", 1536), ("w2", 1536),
           ("loc_q", 128), ("loc_k", 128), ("loc_v", 128), ("loc_o", 128),
           ("moe2_r", 8), ("moe2_w1", 1024), ("moe2_w2", 1024), ("moe2_b2", 128),
           ("x3a", 128), ("x3b", 128), ("ssm_in", 512), ("ssm_B", 32), ("ssm_C", 256), ("ssm_out", 256),
           ("moe3_r", 8), ("moe3_w1", 1024), ("moe3_w2", 1024), ("moe3_b2", 128)]
CONSTS = [("ident", 128), ("center", 128), ("mean", 128), ("hmask", NH), ("cos", SEQ), ("sin", SEQ),
          ("causal_add", SEQ), ("causal_T", SEQ), ("upto", 128), ("iota", 16), ("lora_sel", 128),
          ("decay", GT), ("ones_row", 128)]


def offsets(table):
    at, out = 0, {}
    for name, n in table:
        out[name] = (at, n)
        at += n
    return out, at


FOLD_AT, FOLD_N = offsets(FOLD)
COL_AT, COL_N = offsets(COLUMNS)
W_AT, W_N = offsets(WEIGHTS)
C_AT, C_N = offsets(CONSTS)


def build(nc, x, ctxin, fold, cols, weights, consts, out):
    f32, bf16, u32 = mybir.dt.float32, mybir.dt.bfloat16, mybir.dt.uint32
    ALU, ACT, AX = mybir.AluOpType, mybir.ActivationFunctionType, mybir.AxisListType

    stack = ExitStack()
    with stack:
        def sb(name, cols_, dt=f32):
            return stack.enter_context(nc.sbuf_tensor(name, [128, cols_], dt))

        def sem(name):
            return stack.enter_context(nc.semaphore(name))

        cst = sb("cst", C_N)
        col = sb("col", COL_N)
        wts = sb("wts", W_N)
        score0 = sb("score0", H0 * D)
        value0 = sb("value0", H0 * D)
        score2 = sb("score2", H2 * D)
        value2 = sb("value2", H2 * D)
        qbias0 = sb("qbias0", H0)
        obias0 = sb("obias0", 1)
        ident_b = sb("ident_b", 128, bf16)
        causal_b = sb("causal_b", SEQ, bf16)
        upto_b = sb("upto_b", 128, bf16)
        ones_b = sb("ones_b", 128, bf16)
        pick_b = sb("pick_b", EXPERTS * 128, bf16)
        eps5 = sb("eps5", 1)
        eps7 = sb("eps7", 1)
        count = sb("count", EXPERTS)

        def C(name):
            at, n = C_AT[name]
            return cst[:, at:at + n]

        def W(name):
            at, n = W_AT[name]
            return wts[:, at:at + n]

        def V(name, k=0):
            at = COL_AT[name][0] + k
            return col[:, at:at + 1]

        def per_slot(name, n, dt=f32):
            return [sb(f"{name}_{s}", n, dt) for s in range(SLOTS)]

        X = per_slot("X", GT)
        Z = per_slot("Z", GT)
        A = per_slot("A", GT)
        ctxT = per_slot("ctxT", GC)
        ctxz = per_slot("ctxz", GC)
        kvT = per_slot("kvT", GB * KEYS)
        T = per_slot("T", 4 * GT)
        big = per_slot("big", 4096)
        P = per_slot("P", 2048)
        Vbd = per_slot("Vbd", GB * 8 * 18)
        small = per_slot("small", 448)
        idx = per_slot("idx", TILES * 8, u32)
        ohb = per_slot("ohb", TILES * 8, bf16)
        mTb = per_slot("mTb", GT, bf16)

        ps = [stack.enter_context(nc.psum_tensor(f"ps_{s}", [128, 4 * BANK], f32)) for s in range(SLOTS)]

        def bank(s, k, n=1, p0=0, p1=128):
            return ps[s][p0:p1, k * BANK:(k + n) * BANK]

        def tmp(s, k, n=1):
            return T[s][:, k * GT:(k + n) * GT]

        def seqs(ap):
            return ap.rearrange("p (b t) -> p b t", t=SEQ)

        def by_head(s, h):
            return big[s][:, :].rearrange("p (b h t) -> p b h t", h=8, t=SEQ)[:, :, h, :]

        def block_of(h, n):
            return (h % 2) * (n // 2) + h // 2

        def qb(h):
            return qbias0[:, block_of(h, H0):block_of(h, H0) + 1]

        def over(ap, axis, shape):
            return ap.unsqueeze(axis).to_broadcast(shape)

        L, M8, IXF, OH, OH1, U, CW, G8, DN = 32, 96, 128, 160, 224, 288, 352, 384, 416

        def route(s, at, e):
            return small[s][:, at:at + 64].rearrange("p (t e) -> p t e", e=16)[:, :, 0:e]

        def comb(s, at):
            return small[s][:, at:at + 32].rearrange("p (t e) -> p t e", e=8)

        def over_e(s, at, k, e):
            return comb(s, at)[:, :, k:k + 1].to_broadcast([128, TILES, e])

        def padded(s):
            return big[s][:, 0:2 * GB * (SEQ + 3)].rearrange("p (n t) -> p n t", t=SEQ + 3)

        LN_EXP = "natural_log_exp_and_others"
        X1_SCALE = float(D) ** -0.5

        w_fold, w_col, w_cst, w_main = sem("w_fold"), sem("w_col"), sem("w_cst"), [sem(f"w_main{k}") for k in range(4)]
        prep = sem("prep")
        folded, fold_out = sem("folded"), sem("fold_out")
        ctx_loaded, x_free = (sem("ctx_loaded0"), sem("ctx_loaded1")), sem("x_free")
        NAMES = ["x_loaded0", "x_loaded1",
                 "centered", "squared", "var", "log_var", "rstd", "normed", "rms_sq", "rms_var", "rms_rstd", "rms_done",
                 "kv_ready", "kvn_ps", "kvn_ready", "kvl_ready",
                 "qp_ps", "qp_act", "qp_dve", "scores", "maxed", "exped", "rsum", "p_ready", "pT_ps", "pT_act", "pT_dve",
                 "mixed", "mix_out", "heads_ps",
                 "rnn_gate", "rnn_in", "rnn_tanh", "rnn_keep0", "rnn_keep1", "rnn_h", "rnn_out",
                 "logits", "shifted", "u_exp", "comb", "combT_ps", "combT", "lora_z_ps", "lora_z", "lora_b", "lora_zs", "lora_out",
                 "x1_proj", "x1_q", "x1_k", "x1_s", "x1_v", "x1_max", "x1_exp", "x1_sum", "x1_p", "x1_pT", "x1_pT_sb", "x1_o",
                 "n_proj", "n_q", "n_k", "v_ps", "v_sb", "bd_ready", "bd_used", "n_s", "n_sub", "n_exp",
                 "n_pT", "n_pT_act", "n_pT_dve", "n_o", "n_y", "n_yT", "n_yT_sb", "n_out",
                 "rope_dve", "rope", "y_ready", "final",
                 "m1_bc", "m1_x", "m1_a", "m1_b", "m1_t", "m1_g", "m1_out",
                 "cum_ps", "g_bc", "g_sb", "xg", "m2_h", "m2_relu", "m2_m", "m2_out", "m2_mT_b",
                 "onehot", "m2_mask", "m2_act", "x1_v_sb", "rms_log", "pool_chain", "kv_pad", "ssm_pad", "x3_sum", "x3_ps", "ssm_in", "ssm_xp", "ssm_tap", "ssm_conv", "ssm_t", "ssm_x", "ssm_u", "ssm_h", "ssm_y",
                 "ssm_zt", "ssm_g", "ssm_out", "chain", "x_added"]
        g = {n: sem(n) for n in NAMES}
        x_loaded = (g["x_loaded0"], g["x_loaded1"])
        clear = range(g["x_loaded0"].num, g["x_added"].num + 1)
        assert len(clear) == len(NAMES)

        def nth(n, s):
            return n * SLOTS + s + 1

        def nth_half(n, s, hf):
            return 2 * (n * SLOTS + s) + hf + 1

        with nc.Block() as block:
            @block.sync
            def _(sp):
                sp.dma_start(big[0][:, :], fold[:, 0:4096]).then_inc(w_fold, 16)
                sp.dma_start(big[1][:, 0:2048], fold[:, 4096:6144]).then_inc(w_fold, 16)
                sp.dma_start(col[:, :], cols[:, :]).then_inc(w_col, 16)
                sp.dma_start(cst[:, :], consts[:, :]).then_inc(w_cst, 16)
                cut = [0, W_AT["lin_q"][0], W_AT["w1"][0], W_AT["loc_q"][0], W_N]
                for s in range(SLOTS):
                    sp.dma_start(ctxT[s][:, :], ctxin[:, s * GC:s * GC + GC]).then_inc(ctx_loaded[s], 16)
                for k in range(4):
                    sp.dma_start(wts[:, cut[k]:cut[k + 1]], weights[:, cut[k]:cut[k + 1]]).then_inc(w_main[k], 16)

            @block.gpsimd
            def _(pool):
                pool.memset(count[:, :], 0.0).then_inc(prep, 1)
                pool.memset(eps7[:, :], 1.1920928955078125e-07).then_inc(x_free, 16)
                for s in range(SLOTS):
                    pool.wait_ge(prep, 3 * s + 1)
                    pool.memset(Vbd[s][:, :], 0.0).then_inc(prep, 1)
                    pool.wait_ge(prep, 3 * s + 2)
                    vb = Vbd[s][:, :].rearrange("p (n c) -> p n c", c=18)
                    pool.memset(vb[0:64, :, 8:9], 1.0).then_inc(prep, 1)
                    pool.wait_ge(prep, 3 * s + 3)
                    pool.memset(vb[64:128, :, 17:18], 1.0).then_inc(prep, 1)

            def rows(s, name, j, hh):
                at = FOLD_AT[name][0] - (4096 if s else 0)
                return big[s][64 * hh:64 * hh + 64, at + 128 * j:at + 128 * j + 128]

            @block.tensor
            def _(pe):
                pe.wait_ge(w_fold, 32)
                pe.wait_ge(w_col, 16)
                for h in range(H0):
                    j, hh, at = h // 2, h % 2, 128 * block_of(h, H0)
                    pe.matmul(ps[0][:, at:at + 128], rows(0, "q0T", j, hh), rows(0, "k0T", j, hh), start=True, stop=True)
                    m = pe.matmul(ps[1][:, at:at + 128], rows(0, "v0T", j, hh), rows(0, "o0", j, hh), start=True, stop=True)
                m.then_inc(folded, 1)
                pe.wait_ge(fold_out, 2)
                for h in range(H2):
                    j, hh, at = h // 2, h % 2, 128 * block_of(h, H2)
                    pe.matmul(ps[0][:, at:at + 128], rows(1, "q2T", j, hh), rows(1, "k2T", j, hh), start=True, stop=True)
                    m = pe.matmul(ps[1][:, at:at + 128], rows(1, "v2T", j, hh), rows(1, "o2", j, hh), start=True, stop=True)
                for h in range(H0):
                    j, hh = h // 2, h % 2
                    at, to = COL_AT["bq0"][0] + j, (2 + hh) * BANK + j
                    pe.matmul(ps[0][:, to:to + 1], rows(0, "k0T", j, hh), col[64 * hh:64 * hh + 64, at:at + 1],
                              start=True, stop=True)
                for j in range(H0 // 2):
                    at = FOLD_AT["o0"][0] + 128 * j
                    m = pe.matmul(ps[1][:, 2 * BANK:2 * BANK + 1], big[0][:, at:at + 128], V("bv0", j), start=(j == 0), stop=(j == 7))
                m.then_inc(folded, 1)

            @block.scalar
            def _(act):
                act.wait_ge(folded, 1)
                act.activation(score0[:, :], ps[0][:, :], ACT.Copy).then_inc(fold_out, 1)
                act.wait_ge(folded, 2)
                act.activation(score2[:, :], ps[0][:, 0:1024], ACT.Copy).then_inc(fold_out, 1)
                for hh in range(2):
                    act.activation(qbias0[:, 8 * hh:8 * hh + 8], ps[0][:, (2 + hh) * BANK:(2 + hh) * BANK + 8], ACT.Copy,
                                   scale=0.125).then_inc(fold_out, 1)

            @block.vector
            def _(dve):
                dve.wait_ge(w_cst, 16)
                dve.tensor_copy(ident_b[:, :], C("ident"))
                dve.tensor_copy(causal_b[:, :], C("causal_add"))
                dve.tensor_copy(upto_b[:, :], C("upto"))
                dve.tensor_copy(pick_b[:, :].rearrange("p (e m) -> p e m", m=128),
                                over(C("ident")[:, 0:EXPERTS], 2, [128, EXPERTS, 128]))
                dve.memset(ones_b[:, :], 1.0)
                dve.memset(eps5[:, :], 1e-5)
                dve.wait_ge(folded, 1)
                dve.tensor_copy(value0[:, :], ps[1][:, :]).then_inc(fold_out, 1)
                dve.wait_ge(folded, 2)
                dve.tensor_copy(value2[:, :], ps[1][:, 0:1024])
                dve.tensor_tensor(obias0[:, :], ps[1][:, 2 * BANK:2 * BANK + 1], V("bout0"), ALU.add)

        LAST = 12
        LN = dict(ctx0=0, ctx1=1, x0=2, lat0=3, rnn=4, lora=5, x1=6, lin=7, moe1=8, x2=9, lat2=10, loc=11, moe2=12, x3=13,
                  ssm=14, moe3=15)

        with nc.Fori(0, PASSES) as i:
            with nc.Block() as block:
                @block.sync
                def _(sp):
                    for s in range(SLOTS):
                        at = i * (SLOTS * GT) + s * GT
                        sp.wait_ge(x_free, 16 * SLOTS * i + 16)
                        sp.dma_start(X[s][:, :], x[:, bass.ds(at, GT)]).then_inc(x_loaded[s], 16)
                    for s in range(SLOTS):
                        atc = (i + 1) * (SLOTS * GC) + s * GC
                        sp.wait_ge(g["x3_sum"], nth(0, s))
                        sp.dma_start(ctxT[s][:, :], ctxin[:, bass.ds(atc, GC)]).then_inc(ctx_loaded[s], 16)
                    for s in range(SLOTS):
                        at = i * (SLOTS * GT) + s * GT
                        sp.wait_ge(g["x_added"], nth(LAST, s))
                        sp.dma_start(out[:, bass.ds(at, GT)], X[s][:, :]).then_inc(x_free, 16)

                @block.tensor
                def _(pe):
                    def added(n, s):
                        if n >= 0:
                            pe.wait_ge(g["x_added"], nth(n, s))

                    def norm(name, src, ready):
                        n = LN[name]
                        for s in range(SLOTS):
                            ready(s)
                            pe.matmul(bank(s, 0), C("center"), src(s), start=True, stop=True).then_inc(g["centered"], 1)
                        for s in range(SLOTS):
                            pe.wait_ge(g["squared"], nth(n, s))
                            pe.matmul(bank(s, 1), C("mean"), tmp(s, 0), start=True, stop=True).then_inc(g["var"], 1)

                    def normed(name, s):
                        pe.wait_ge(g["normed"], nth(LN[name], s))

                    def kv_tokens(n):
                        for s in range(SLOTS):
                            pe.wait_ge(g["kv_ready"], nth(n, s))
                            for b in range(GB):
                                pe.transpose(ps[s][:, 128 * b:128 * b + 128], kvT[s][:, KEYS * b:KEYS * b + CTX], C("ident"))
                                m = pe.transpose(ps[s][0:64, 2 * BANK + 128 * b:2 * BANK + 128 * b + 128],
                                                 kvT[s][:, KEYS * b + CTX:KEYS * b + KEYS], C("ident"))
                            m.then_inc(g["kvn_ps"], 1)

                    def heads(gi, n, score, value, nh, h0):
                        for r in range(2):
                            for s in range(SLOTS):
                                if r == 0 and h0 == 0:
                                    pe.wait_ge(g["kvn_ready"], nth(n, s))
                                    pe.wait_ge(g["kvl_ready"], nth(n, s))
                                    pe.wait_ge(g["kv_pad"], nth(n, s))
                                elif r == 0:
                                    added(gi - 1, s)
                                else:
                                    pe.wait_ge(g["qp_act"], nth(2 * gi, s))
                                    pe.wait_ge(g["qp_dve"], nth(2 * gi, s))
                                lat = kvT[s][:, :].rearrange("p (b k) -> p b k", k=KEYS)[:, :, CTX:KEYS]
                                for k in range(4):
                                    h = h0 + 4 * r + k
                                    m = pe.matmul(bank(s, k), score[:, 128 * block_of(h, nh):128 * block_of(h, nh) + 128], lat, start=True, stop=True)
                                m.then_inc(g["qp_ps"], 1)
                        def scores(s, b):
                            for p in range(4):
                                at = (p // 2) * BANK + (p % 2) * KEYS
                                m = pe.matmul(ps[s][:, at:at + KEYS], big[s][:, BANK * b + 128 * p:BANK * b + 128 * p + 128],
                                              kvT[s][:, KEYS * b:KEYS * b + KEYS], start=True, stop=True)
                                if p % 2:
                                    m.then_inc(g["scores"], 1)

                        for s in range(SLOTS):
                            pe.wait_ge(g["qp_act"], nth(2 * gi + 1, s))
                            pe.wait_ge(g["qp_dve"], nth(2 * gi + 1, s))
                            scores(s, 0)
                        for b in range(GB):
                            u = gi * GB + b
                            for s in range(SLOTS):
                                pe.wait_ge(g["p_ready"], nth_half(u, s, 1))
                                if b:
                                    pe.wait_ge(g["mix_out"], nth(u - 1, s))
                                for p in range(4):
                                    pe.transpose(ps[s][:, 2 * BANK + 128 * p:2 * BANK + 128 * p + 128],
                                                 P[s][:, KEYS * p:KEYS * p + CTX], C("ident"))
                                    m = pe.transpose(ps[s][0:64, 3 * BANK + 128 * p:3 * BANK + 128 * p + 128],
                                                     P[s][:, KEYS * p + CTX:KEYS * p + KEYS], C("ident"))
                                m.then_inc(g["pT_ps"], 1)
                                if b < GB - 1:
                                    scores(s, b + 1)
                            for s in range(SLOTS):
                                pe.wait_ge(g["pT_act"], nth(u, s))
                                pe.wait_ge(g["pT_dve"], nth(u, s))
                                pe.matmul(bank(s, 2), T[s][:, 128 * b:128 * b + 128], P[s][:, 1024:1536], start=True, stop=False)
                                pe.matmul(bank(s, 2), T[s][:, GC + 128 * b:GC + 128 * b + 128], P[s][:, 1536:2048],
                                          start=False, stop=True).then_inc(g["mixed"], 1)
                        for s in range(SLOTS):
                            pe.wait_ge(g["mix_out"], nth(gi * GB + GB - 1, s))
                            for k in range(8):
                                m = pe.matmul(bank(s, 1), value[:, 128 * block_of(h0 + k, nh):128 * block_of(h0 + k, nh) + 128],
                                              by_head(s, k), start=(k == 0), stop=(k == 7))
                            m.then_inc(g["heads_ps"], 1)

                    pe.wait_ge(w_cst, 16)
                    for k in range(4):
                        pe.wait_ge(w_main[k], 16)
                    norm("ctx0", lambda s: ctxT[s][:, 0:GT], lambda s: pe.wait_ge(ctx_loaded[s], 16 * i + 16))
                    norm("ctx1", lambda s: ctxT[s][:, GT:GC], lambda s: normed("ctx0", s))
                    norm("x0", lambda s: X[s][:, :], lambda s: (normed("ctx1", s), pe.wait_ge(x_loaded[s], 16)))
                    norm("lat0", lambda s: Z[s][:, :], lambda s: normed("x0", s))
                    kv_tokens(0)
                    heads(0, 0, score0, value0, H0, 0)
                    heads(1, 0, score0, value0, H0, 8)

                    norm("rnn", lambda s: X[s][:, :], lambda s: added(1, s))
                    for s in range(SLOTS):
                        normed("rnn", s)
                        for k in (2, 3, 0, 1):
                            m = pe.matmul(bank(s, k), W("hg")[:, 128 * k:128 * k + 128], Z[s][:, :], start=True, stop=True)
                            if k % 2:
                                m.then_inc(g["rnn_gate" if k == 3 else "rnn_in"], 1)
                    for s in range(SLOTS):
                        pe.wait_ge(g["rnn_h"], nth(0, s))
                        for k in range(2):
                            m = pe.matmul(bank(s, 0), W("rnn_out")[:, 128 * k:128 * k + 128],
                                          big[s][:, 2048 + GT * k:2048 + GT * k + GT], start=(k == 0), stop=(k == 1))
                        m.then_inc(g["rnn_out"], 1)

                    def logits(n, src, w, e, bias=None):
                        for s in range(SLOTS):
                            for t in range(TILES):
                                to = ps[s][:, 16 * t:16 * t + e]
                                if bias:
                                    pe.matmul(to, C("ones_row")[0:1, :], bias, start=True, stop=False)
                                m = pe.matmul(to, src(s)[:, 128 * t:128 * t + 128], w, start=not bias, stop=True)
                            m.then_inc(g["logits"], 1)

                    def turn(n, pairs):
                        for s in range(SLOTS):
                            pe.wait_ge(g["comb"], nth(n, s))
                            for at, k in pairs:
                                for t in range(TILES):
                                    m = pe.transpose(ps[s][0:8, k * BANK + 128 * t:k * BANK + 128 * t + 128],
                                                     small[s][:, at + 8 * t:at + 8 * t + 8], C("ident"))
                            m.then_inc(g["combT_ps"], 1)

                    norm("lora", lambda s: X[s][:, :], lambda s: added(2, s))
                    for s in range(SLOTS):
                        normed("lora", s)
                    logits(0, lambda s: Z[s], W("gate0"), 10)
                    for s in range(SLOTS):
                        pe.matmul(bank(s, 1), W("loraA"), Z[s][:, :], start=True, stop=True).then_inc(g["lora_z_ps"], 1)
                        pe.matmul(bank(s, 2), W("base"), Z[s][:, :], start=True, stop=False)
                    turn(0, [(352, 3)])
                    for s in range(SLOTS):
                        pe.wait_ge(g["combT"], nth(0, s))
                        pe.wait_ge(g["lora_z"], nth(0, s))
                        pe.matmul(bank(s, 1), C("lora_sel")[0:8, :], tmp(s, 3)[0:8, :], start=True, stop=True).then_inc(g["lora_b"], 1)
                    for s in range(SLOTS):
                        pe.wait_ge(g["lora_zs"], nth(0, s))
                        pe.matmul(bank(s, 2), W("loraB"), tmp(s, 1), start=False, stop=True).then_inc(g["lora_out"], 1)

                    norm("x1", lambda s: X[s][:, :], lambda s: added(3, s))
                    for s in range(SLOTS):
                        normed("x1", s)
                        pe.matmul(bank(s, 0), W("q1"), Z[s][:, :], start=True, stop=True)
                        pe.matmul(bank(s, 1), W("k1"), ctxT[s][:, 0:GT], start=True, stop=True)
                        pe.matmul(bank(s, 2), W("k1"), ctxT[s][:, GT:GC], start=True, stop=True).then_inc(g["x1_proj"], 1)
                    for s in range(SLOTS):
                        pe.wait_ge(g["x1_q"], nth(0, s))
                        pe.wait_ge(g["x1_k"], nth(0, s))
                        for b in range(GB):
                            p0 = SEQ * (b % 2)
                            m = pe.matmul(ps[s][p0:p0 + SEQ, 128 * (b // 2):128 * (b // 2) + 128], A[s][:, SEQ * b:SEQ * b + SEQ],
                                          kvT[s][:, CTX * b:CTX * b + CTX], start=True, stop=True)
                        m.then_inc(g["x1_s"], 1)
                        for b in range(GB):
                            m = pe.matmul(ps[s][:, BANK + 128 * b:BANK + 128 * b + 128], ctxT[s][:, CTX * b:CTX * b + CTX],
                                          W("v1"), start=True, stop=True)
                        m.then_inc(g["x1_v"], 1)
                    for s in range(SLOTS):
                        pe.wait_ge(g["x1_p"], nth(0, s))
                        for t in range(TILES):
                            m = pe.transpose(ps[s][:, 3 * BANK + 128 * t:3 * BANK + 128 * t + 128], P[s][:, 128 * t:128 * t + 128],
                                             C("ident"))
                        m.then_inc(g["x1_pT"], 1)
                    for s in range(SLOTS):
                        pe.wait_ge(g["x1_pT_sb"], nth(0, s))
                        pe.wait_ge(g["x1_v_sb"], nth(0, s))
                        for b in range(GB):
                            m = pe.matmul(ps[s][:, SEQ * b:SEQ * b + SEQ], big[s][:, CTX * b:CTX * b + CTX],
                                          P[s][:, 512 + SEQ * b:512 + SEQ * b + SEQ], start=True, stop=True)
                        m.then_inc(g["x1_o"], 1)

                    def values(s, k, src, w):
                        wv = w.rearrange("p (j c d) -> p j c d", c=2, d=HD)
                        for b in range(GB):
                            for hh in range(2):
                                m = pe.matmul(ps[s][64 * hh:64 * hh + 64, k * BANK + 64 * b:k * BANK + 64 * b + 64],
                                              src[:, SEQ * b:SEQ * b + SEQ], wv[:, :, hh, :], start=True, stop=True)
                        m.then_inc(g["v_ps"], 1)

                    def project(m_, w):
                        for s in range(SLOTS):
                            for t in range(TILES):
                                m = pe.transpose(ps[s][:, BANK + 128 * t:BANK + 128 * t + 128], kvT[s][:, 128 * t:128 * t + 128],
                                                 C("ident"))
                            m.then_inc(g["n_yT"], 1)
                        for s in range(SLOTS):
                            pe.wait_ge(g["n_yT_sb"], nth(m_, s))
                            pe.matmul(bank(s, 2), w, kvT[s][:, GT:2 * GT], start=True, stop=True).then_inc(g["n_out"], 1)

                    def head_outputs(s, k, t, src):
                        for bb in range(2):
                            b = 2 * t + bb
                            for j in range(8):
                                m = pe.matmul(ps[s][64 * bb:64 * bb + 64, BANK * k + 18 * j:BANK * k + 18 * j + 18], src(bb, j),
                                              Vbd[s][:, 18 * (8 * b + j):18 * (8 * b + j) + 18], start=True, stop=True)
                        m.then_inc(g["n_o"], 1)

                    def softmax_heads(u0, v0, causal):
                        def scores(s, t):
                            pe.wait_ge(g["bd_ready"], nth(u0 + t, s))
                            for half in range(2 if causal else 0):
                                pe.matmul(bank(s, half), ident_b[:, :], over(causal_b[:, :], 1, [128, 8, SEQ]), start=True, stop=False)
                            for half in range(2):
                                for bb in range(2):
                                    b, at = 2 * t + bb, 2048 * (t % 2) + 1024 * bb + 512 * half
                                    m = pe.matmul(bank(s, half, 1, 64 * bb, 64 * bb + 64), tmp(s, 0)[:, SEQ * b:SEQ * b + SEQ],
                                                  big[s][:, at:at + 512], start=not causal, stop=True)
                            m.then_inc(g["n_s"], 1)

                        for s in range(SLOTS):
                            scores(s, 0)
                        for t in range(TILES):
                            u, v = u0 + t, v0 + t
                            for s in range(SLOTS):
                                pe.wait_ge(g["n_exp"], nth(v, s))
                                if t:
                                    pe.wait_ge(g["n_y"], nth(u - 1, s))
                                for j in range(8):
                                    m = pe.transpose(ps[s][:, 2 * BANK + 128 * j:2 * BANK + 128 * j + 128],
                                                     P[s][:, 128 * j:128 * j + 128], C("ident"))
                                m.then_inc(g["n_pT"], 1)
                                if t < TILES - 1:
                                    scores(s, t + 1)
                            for s in range(SLOTS):
                                pe.wait_ge(g["n_pT_act"], nth(v, s))
                                pe.wait_ge(g["n_pT_dve"], nth(v, s))
                                head_outputs(s, 2, t, lambda bb, j: P[s][:, 1024 + 128 * j + 64 * bb:1024 + 128 * j + 64 * bb + 64])
                        for s in range(SLOTS):
                            pe.wait_ge(g["n_y"], nth(u0 + TILES - 1, s))

                    norm("lin", lambda s: X[s][:, :], lambda s: added(4, s))
                    for s in range(SLOTS):
                        normed("lin", s)
                        pe.matmul(bank(s, 0), W("lin_q"), Z[s][:, :], start=True, stop=True)
                        pe.matmul(bank(s, 1), W("lin_k"), Z[s][:, :], start=True, stop=True).then_inc(g["n_proj"], 1)
                        values(s, 2, Z[s], W("lin_v"))

                    def scores(s, t):
                        pe.wait_ge(g["bd_ready"], nth(t, s))
                        for bb in range(2):
                            b, at = 2 * t + bb, 2048 * (t % 2) + 1024 * bb
                            q = big[s][:, at:at + 1024].rearrange("p (j c t) -> p j c t", c=2, t=SEQ)
                            for hh in range(2):
                                m = pe.matmul(bank(s, 2 * (t % 2) + bb, 1, 64 * hh, 64 * hh + 64), tmp(s, 2)[:, SEQ * b:SEQ * b + SEQ],
                                              q[:, :, hh, :], start=True, stop=True)
                        m.then_inc(g["n_s"], 1)

                    for t in range(2):
                        for s in range(SLOTS):
                            pe.wait_ge(g["n_k"], nth(0, s))
                            pe.wait_ge(g["v_sb"], nth(0, s))
                            scores(s, t)
                    for t in range(TILES):
                        for s in range(SLOTS):
                            pe.wait_ge(g["n_sub"], nth(t, s))
                            head_outputs(s, 2 * (t % 2), t, lambda bb, j: P[s][:, 1024 * (t % 2) + 64 * (8 * bb + j):
                                                                            1024 * (t % 2) + 64 * (8 * bb + j) + 64])
                        for s in range(SLOTS if t + 2 < TILES else 0):
                            pe.wait_ge(g["n_y"], nth(t, s))
                            scores(s, t + 2)
                    for s in range(SLOTS):
                        pe.wait_ge(g["n_y"], nth(TILES - 1, s))
                    project(0, W("lin_o"))

                    def rms(n, ready):
                        for s in range(SLOTS):
                            ready(s)
                            pe.wait_ge(g["rms_sq"], nth(n, s))
                            pe.matmul(bank(s, 1), C("mean"), tmp(s, 0), start=True, stop=True).then_inc(g["rms_var"], 1)

                    norm("moe1", lambda s: X[s][:, :], lambda s: added(5, s))
                    rms(0, lambda s: normed("moe1", s))
                    for s in range(SLOTS):
                        pe.wait_ge(g["rms_done"], nth(0, s))
                        for k, name in enumerate(("rq", "rqp", "rk", "rkp")):
                            m = pe.matmul(bank(s, k), W(name), A[s][:, :], start=True, stop=True)
                        m.then_inc(g["n_proj"], 1)
                    for s in range(SLOTS):
                        pe.wait_ge(g["rope_dve"], nth(0, s))
                        values(s, 0, A[s], W("rv"))
                    for s in range(SLOTS):
                        pe.wait_ge(g["v_sb"], nth(1, s))
                    softmax_heads(4, 0, True)
                    project(1, W("ro"))
                    rms(1, lambda s: None)
                    for s in range(SLOTS):
                        pe.wait_ge(g["rms_done"], nth(1, s))
                    logits(1, lambda s: A[s], W("gate1"), MOE1_E)
                    turn(1, [(352, 3)])
                    for s in range(SLOTS):
                        pe.wait_ge(g["combT"], nth(1, s))
                        for e in range(MOE1_E):
                            pe.matmul(bank(s, e), C("ident")[0:8, e:e + 1].to_broadcast([8, 128]), tmp(s, 3)[0:8, :],
                                      start=True, stop=True).then_inc(g["m1_bc"], 1)

                    def gate_half(s, k):
                        pe.matmul(bank(s, H3[2 * k % 3]), W("w1")[:, 128 * k:128 * k + 128], A[s][:, :], start=True, stop=True)\
                            .then_inc(g["m1_a"], 1)

                    def down(s, k):
                        m = pe.matmul(bank(s, 2), W("w2")[:, 128 * k:128 * k + 128], P[s][:, 1024 + 512 * (k % 2):1536 + 512 * (k % 2)],
                                      start=(k == 0), stop=(k == MOE1_K - 1))
                        if k == MOE1_K - 1:
                            m.then_inc(g["m1_out"], 1)

                    for s in range(SLOTS):
                        pe.wait_ge(g["m1_x"], nth(0, s))
                        gate_half(s, 0)
                    for k in range(MOE1_K):
                        for s in range(SLOTS):
                            if k:
                                pe.wait_ge(g["m1_g"], nth(k - 1, s))
                            at = BANK * (k // MOE1_C)
                            pe.matmul(bank(s, H3[(2 * k + 1) % 3]), W("w3")[:, 128 * k:128 * k + 128], big[s][:, at:at + BANK],
                                      start=True, stop=True).then_inc(g["m1_b"], 1)
                            if k < MOE1_K - 1:
                                gate_half(s, k + 1)
                            if k:
                                down(s, k - 1)
                    for s in range(SLOTS):
                        pe.wait_ge(g["m1_g"], nth(MOE1_K - 1, s))
                        down(s, MOE1_K - 1)

                    norm("x2", lambda s: X[s][:, :], lambda s: added(6, s))
                    norm("lat2", lambda s: Z[s][:, :], lambda s: normed("x2", s))
                    kv_tokens(1)
                    heads(2, 1, score2, value2, H2, 0)

                    norm("loc", lambda s: X[s][:, :], lambda s: added(7, s))
                    for s in range(SLOTS):
                        normed("loc", s)
                        pe.matmul(bank(s, 0), W("loc_q"), Z[s][:, :], start=True, stop=True)
                        pe.matmul(bank(s, 1), W("loc_k"), Z[s][:, :], start=True, stop=True).then_inc(g["n_proj"], 1)
                        values(s, 2, Z[s], W("loc_v"))
                    for s in range(SLOTS):
                        pe.wait_ge(g["n_q"], nth(1, s))
                        pe.wait_ge(g["n_k"], nth(1, s))
                        pe.wait_ge(g["v_sb"], nth(2, s))
                    softmax_heads(8, 4, False)
                    project(2, W("loc_o"))

                    def top1_experts(layer, w1, w2, b2):
                        for s in range(SLOTS):
                            pe.matmul(bank(s, 2), b2[0:8, :], tmp(s, 3)[0:8, :], start=True, stop=False)

                        def up(s, e):
                            src = A[s][:, :] if layer == 0 else Z[s][:, :]
                            pe.matmul(bank(s, 3 * (e % 2)), w1[:, 128 * e:128 * e + 128], src, start=True, stop=True).then_inc(g["m2_h"], 1)

                        def mask(s, e):
                            pe.matmul(bank(s, 1), pick_b[0:8, 128 * e:128 * e + 128], mTb[s][0:8, :], start=True, stop=True)\
                                .then_inc(g["m2_mask"], 1)

                        for s in range(SLOTS):
                            up(s, 0)
                            mask(s, 0)
                        for s in range(SLOTS):
                            up(s, 1)
                        for e in range(EXPERTS):
                            for s in range(SLOTS):
                                pe.wait_ge(g["m2_m"], nth(layer * EXPERTS + e, s))
                                if e + 1 < EXPERTS:
                                    mask(s, e + 1)
                                m = pe.matmul(bank(s, 2), w2[:, 128 * e:128 * e + 128], P[s][:, 1024 + 512 * (e % 2):1536 + 512 * (e % 2)],
                                              start=False, stop=(e == EXPERTS - 1))
                                if e == EXPERTS - 1:
                                    m.then_inc(g["m2_out"], 1)
                                if e + 2 < EXPERTS:
                                    up(s, e + 2)

                    norm("moe2", lambda s: X[s][:, :], lambda s: added(8, s))
                    for s in range(SLOTS):
                        normed("moe2", s)
                    at = COL_AT["br"][0]
                    logits(2, lambda s: Z[s], W("moe2_r"), 8, col[0:1, at:at + 8])
                    for s in range(SLOTS):
                        pe.wait_ge(g["onehot"], nth(0, s))
                        for t in range(TILES):
                            for t2 in range(t):
                                pe.matmul(ps[s][:, BANK + 8 * t:BANK + 8 * t + 8], ones_b[:, :], ohb[s][:, 8 * t2:8 * t2 + 8],
                                          start=(t2 == 0), stop=False)
                            pe.matmul(ps[s][:, BANK + 8 * t:BANK + 8 * t + 8], upto_b[:, :], ohb[s][:, 8 * t:8 * t + 8],
                                      start=(t == 0), stop=True)
                        for t in range(TILES):
                            m = pe.matmul(ps[s][:, BANK + 32:BANK + 40], ones_b[:, :], ohb[s][:, 8 * t:8 * t + 8],
                                          start=(t == 0), stop=(t == TILES - 1))
                        m.then_inc(g["cum_ps"], 1)
                    turn(2, [(352, 3), (384, 2)])
                    for s in range(SLOTS):
                        pe.wait_ge(g["combT"], nth(2, s))
                        pe.matmul(bank(s, 0), C("ones_row")[0:8, :], tmp(s, 2)[0:8, :], start=True, stop=True).then_inc(g["g_bc"], 1)
                    for s in range(SLOTS):
                        pe.wait_ge(g["xg"], nth(0, s))
                    top1_experts(0, W("moe2_w1"), W("moe2_w2"), W("moe2_b2"))

                    norm("x3", lambda s: X[s][:, :], lambda s: added(9, s))
                    for s in range(SLOTS):
                        normed("x3", s)
                        pe.wait_ge(g["x3_sum"], nth(0, s))
                        pe.matmul(bank(s, 0), W("x3a"), Z[s][:, :], start=True, stop=True)
                        pe.matmul(ps[s][:, BANK:BANK + GB], W("x3b"), small[s][:, 0:8], start=True, stop=True).then_inc(g["x3_ps"], 1)

                    norm("ssm", lambda s: X[s][:, :], lambda s: added(10, s))
                    for s in range(SLOTS):
                        normed("ssm", s)
                        for k in range(4):
                            m = pe.matmul(bank(s, k), W("ssm_in")[:, 128 * k:128 * k + 128], Z[s][:, :], start=True, stop=True)
                            if k % 2:
                                m.then_inc(g["ssm_in"], 1)
                    for s in range(SLOTS):
                        for k in range(2):
                            pe.wait_ge(g["ssm_x"], nth_half(0, s, k))
                            m = pe.matmul(bank(s, 0, 1, 0, STATE), W("ssm_B")[:, STATE * k:STATE * k + STATE],
                                          P[s][:, 1024 + GT * k:1024 + GT * k + GT], start=(k == 0), stop=(k == 1))
                        m.then_inc(g["ssm_u"], 1)
                    for s in range(SLOTS):
                        pe.wait_ge(g["ssm_h"], nth(0, s))
                        for k in range(2):
                            m = pe.matmul(bank(s, k), W("ssm_C")[0:STATE, 128 * k:128 * k + 128], tmp(s, 1)[0:STATE, :],
                                          start=True, stop=True)
                        m.then_inc(g["ssm_y"], 1)
                    for s in range(SLOTS):
                        pe.wait_ge(g["ssm_g"], nth(0, s))
                        for k in range(2):
                            m = pe.matmul(bank(s, 2), W("ssm_out")[:, 128 * k:128 * k + 128], P[s][:, GT * k:GT * k + GT],
                                          start=(k == 0), stop=(k == 1))
                        m.then_inc(g["ssm_out"], 1)

                    norm("moe3", lambda s: X[s][:, :], lambda s: added(11, s))
                    for s in range(SLOTS):
                        normed("moe3", s)
                    at = COL_AT["bg"][0]
                    logits(3, lambda s: Z[s], W("moe3_r"), 8, col[0:1, at:at + 8])
                    turn(3, [(352, 3)])
                    for s in range(SLOTS):
                        pe.wait_ge(g["combT"], nth(3, s))
                    top1_experts(1, W("moe3_w1"), W("moe3_w2"), W("moe3_b2"))

                @block.scalar
                def _(act):
                    def norm(name):
                        n = LN[name]
                        for s in range(SLOTS):
                            act.wait_ge(g["centered"], nth(n, s))
                            act.activation(tmp(s, 0), bank(s, 0), ACT.Square).then_inc(g["squared"], 1)
                        for s in range(SLOTS):
                            act.wait_ge(g["var"], nth(n, s))
                            act.activation(tmp(s, 0), bank(s, 1), ACT.Ln, bias=eps5[:, 0:1]).then_inc(g["log_var"], 1)
                            act.wait_ge(g["log_var"], nth(n, s))
                            act.activation(tmp(s, 1), tmp(s, 0), ACT.Exp, scale=-0.5).then_inc(g["rstd"], 1)

                    def kv_tokens(n):
                        for s in range(SLOTS):
                            act.wait_ge(g["kvn_ps"], nth(n, s))
                            act.activation(T[s][:, 0:GC], bank(s, 0, 2), ACT.Copy).then_inc(g["kvn_ready"], 1)

                    def heads(gi, scale, bias, h0):
                        for r in range(2):
                            for s in range(SLOTS):
                                act.wait_ge(g["qp_ps"], nth(2 * gi + r, s))
                                for k in (2, 3):
                                    h = 4 * r + k
                                    m = act.activation(by_head(s, h), seqs(bank(s, k)), ACT.Identity,
                                                       bias=qb(h0 + h) if bias else 0.0, scale=scale)
                                m.then_inc(g["qp_act"], 1)
                        def exps(u, s):
                            for p in range(4):
                                if p % 2 == 0:
                                    act.wait_ge(g["maxed"], nth_half(u, s, p // 2))
                                at = (p // 2) * BANK + (p % 2) * KEYS
                                m = act.activation(P[s][:, KEYS * p:KEYS * p + KEYS], ps[s][:, at:at + KEYS], ACT.Exp,
                                                   bias=small[s][:, p:p + 1], accum_out=small[s][:, 8 + p:9 + p])
                                if p % 2:
                                    m.then_inc(g["exped"], 1)

                        for s in range(SLOTS):
                            exps(gi * GB, s)
                        for b in range(GB):
                            u = gi * GB + b
                            for s in range(SLOTS):
                                act.wait_ge(g["pT_ps"], nth(u, s))
                                act.activation(P[s][:, 1024:1536], bank(s, 2), ACT.Copy).then_inc(g["pT_act"], 1)
                                if b < GB - 1:
                                    exps(u + 1, s)

                    act.preload_act_table_set(LN_EXP)
                    norm("ctx0")
                    norm("ctx1")
                    norm("x0")
                    norm("lat0")
                    kv_tokens(0)
                    heads(0, 0.125, True, 0)
                    heads(1, 0.125, True, 8)

                    norm("rnn")
                    for s in range(SLOTS):
                        act.wait_ge(g["rnn_gate"], nth(0, s))
                        act.activation(tmp(s, 0, 2), bank(s, 2, 2), ACT.Tanh, scale=0.5).then_inc(g["rnn_tanh"], 1)
                        act.wait_ge(g["rnn_tanh"], nth(0, s))
                        act.activation(seqs(tmp(s, 3))[:, :, 1:SEQ], seqs(tmp(s, 1))[:, :, 1:SEQ], ACT.Copy, scale=-0.5,
                                       bias=0.5).then_inc(g["rnn_keep1"], 1)
                    act.preload_act_table_set(LN_EXP)

                    def exp_logits(n, e):
                        for s in range(SLOTS):
                            act.wait_ge(g["shifted"], nth(n, s))
                            act.activation(route(s, U, e), route(s, U, e), ACT.Exp).then_inc(g["u_exp"], 1)

                    def turned(n, copies):
                        for s in range(SLOTS):
                            act.wait_ge(g["combT_ps"], nth(n, s))
                            for dst, k in copies:
                                m = act.activation(dst(s), bank(s, k, 1, 0, 8), ACT.Copy)
                            m.then_inc(g["combT"], 1)

                    norm("lora")
                    for s in range(SLOTS):
                        act.wait_ge(g["lora_z_ps"], nth(0, s))
                        act.activation(tmp(s, 0), bank(s, 1), ACT.Copy, scale=2.0).then_inc(g["lora_z"], 1)
                    exp_logits(0, 10)
                    turned(0, [(lambda s: tmp(s, 3)[0:8, :], 3)])

                    norm("x1")
                    for s in range(SLOTS):
                        act.wait_ge(g["x1_proj"], nth(0, s))
                        act.activation(kvT[s][:, 0:GC], bank(s, 1, 2), ACT.Identity, bias=V("bk1")).then_inc(g["x1_k"], 1)
                    for s in range(SLOTS):
                        act.wait_ge(g["x1_v"], nth(0, s))
                        act.activation(big[s][:, 0:GC], bank(s, 1, 2), ACT.Copy).then_inc(g["x1_v_sb"], 1)
                    for s in range(SLOTS):
                        act.wait_ge(g["x1_max"], nth(0, s))
                        for t in range(TILES):
                            m = act.activation(P[s][:, 128 * t:128 * t + 128], ps[s][:, 128 * t:128 * t + 128], ACT.Exp,
                                               bias=small[s][:, 16 + t:17 + t], scale=X1_SCALE, accum_out=small[s][:, 20 + t:21 + t])
                        m.then_inc(g["x1_exp"], 1)

                    def values(m_, k):
                        for s in range(SLOTS):
                            act.wait_ge(g["v_ps"], nth(m_, s))
                            vb = Vbd[s][:, :].rearrange("p (n c) -> p n c", c=18)
                            for hh in range(2):
                                p0 = 64 * hh
                                m = act.activation(vb[p0:p0 + 64, :, 9 * hh:9 * hh + 8],
                                                   bank(s, k, 1, p0, p0 + 64).rearrange("p (n d) -> p n d", d=HD), ACT.Copy)
                            m.then_inc(g["v_sb"], 1)

                    def project(m_, bias):
                        for s in range(SLOTS):
                            act.wait_ge(g["n_yT"], nth(m_, s))
                            act.activation(kvT[s][:, GT:2 * GT], bank(s, 1), ACT.Identity, bias=bias).then_inc(g["n_yT_sb"], 1)

                    def softmax_heads(v0):
                        def exps(v, s):
                            act.wait_ge(g["n_sub"], nth(v + TILES, s))
                            act.activation(P[s][:, 0:1024], P[s][:, 0:1024], ACT.Exp, scale=HD ** -0.5).then_inc(g["n_exp"], 1)

                        for s in range(SLOTS):
                            exps(v0, s)
                        for v in range(v0, v0 + TILES):
                            for s in range(SLOTS):
                                act.wait_ge(g["n_pT"], nth(v, s))
                                act.activation(P[s][:, 1024:1536], bank(s, 2), ACT.Copy).then_inc(g["n_pT_act"], 1)
                                if v < v0 + TILES - 1:
                                    exps(v + 1, s)

                    norm("lin")
                    for s in range(SLOTS):
                        act.wait_ge(g["n_proj"], nth(0, s))
                        act.activation(tmp(s, 2), bank(s, 1), ACT.Relu).then_inc(g["n_k"], 1)
                    values(0, 2)
                    project(0, 0.0)

                    def rms(n, ready):
                        for s in range(SLOTS):
                            ready(s)
                            act.activation(tmp(s, 0), Z[s][:, :], ACT.Square).then_inc(g["rms_sq"], 1)
                        for s in range(SLOTS):
                            act.wait_ge(g["rms_var"], nth(n, s))
                            act.activation(tmp(s, 0), bank(s, 1), ACT.Ln, bias=eps7[:, 0:1]).then_inc(g["rms_log"], 1)
                            act.wait_ge(g["rms_log"], nth(n, s))
                            act.activation(tmp(s, 1), tmp(s, 0), ACT.Exp, scale=-0.5).then_inc(g["rms_rstd"], 1)

                    norm("moe1")
                    rms(0, lambda s: act.wait_ge(g["normed"], nth(LN["moe1"], s)))
                    values(1, 0)
                    softmax_heads(0)
                    project(1, 0.0)
                    rms(1, lambda s: act.wait_ge(g["y_ready"], nth(0, s)))
                    exp_logits(1, MOE1_E)
                    turned(1, [(lambda s: tmp(s, 3)[0:8, :], 3)])
                    for k in range(MOE1_K):
                        for s in range(SLOTS):
                            act.wait_ge(g["m1_a"], nth(k, s))
                            act.activation(P[s][:, 512 * (k % 2):512 * (k % 2) + 512], bank(s, H3[2 * k % 3]), ACT.Tanh, scale=0.5)\
                               .then_inc(g["m1_t"], 1)
                    act.preload_act_table_set(LN_EXP)

                    norm("x2")
                    norm("lat2")
                    kv_tokens(1)
                    heads(2, 8.0, False, 0)

                    norm("loc")
                    for s in range(SLOTS):
                        act.wait_ge(g["n_proj"], nth(2, s))
                        act.activation(tmp(s, 2), bank(s, 1), ACT.Identity, bias=V("bqkv", 1)).then_inc(g["n_k"], 1)
                    values(2, 2)
                    softmax_heads(4)
                    project(2, V("bqkv", 2))

                    def top1_experts(layer, func, b1):
                        for e in range(EXPERTS):
                            n = layer * EXPERTS + e
                            for s in range(SLOTS):
                                act.wait_ge(g["m2_h"], nth(n, s))
                                act.activation(P[s][:, 512 * (e % 2):512 * (e % 2) + 512], bank(s, 3 * (e % 2)), func, bias=V(b1, e))\
                                    .then_inc(g["m2_act"], 1)

                    norm("moe2")
                    exp_logits(2, EXPERTS)
                    turned(2, [(lambda s: tmp(s, 3)[0:8, :], 3), (lambda s: mTb[s][0:8, :], 3), (lambda s: tmp(s, 2)[0:8, :], 2)])
                    for s in range(SLOTS):
                        act.wait_ge(g["g_bc"], nth(0, s))
                        act.activation(tmp(s, 0), bank(s, 0), ACT.Copy).then_inc(g["g_sb"], 1)
                    top1_experts(0, ACT.Relu, "moe2_b1")

                    norm("x3")

                    norm("ssm")
                    for s in range(SLOTS):
                        act.wait_ge(g["ssm_in"], nth_half(0, s, 0))
                        act.wait_ge(g["ssm_pad"], nth(0, s))
                        act.activation(padded(s)[:, :, 3:67], bank(s, 0, 2).rearrange("p (n t) -> p n t", t=SEQ), ACT.Copy)\
                           .then_inc(g["ssm_xp"], 1)
                        for k in range(2):
                            m = act.activation(big[s][:, 2048 + GT * k:2048 + GT * k + GT], bank(s, k), ACT.Identity,
                                               scale=V("conv_w", 4 * k + 3), bias=V("conv_b", k))
                        m.then_inc(g["ssm_tap"], 1)
                    for s in range(SLOTS):
                        for k in range(2):
                            act.wait_ge(g["ssm_conv"], nth_half(0, s, k))
                            act.activation(P[s][:, GT * k:GT * k + GT], big[s][:, 2048 + GT * k:2048 + GT * k + GT], ACT.Tanh,
                                           scale=0.5).then_inc(g["ssm_t"], 1)
                        if s == 0:
                            for z in range(SLOTS):
                                act.wait_ge(g["ssm_in"], nth_half(0, z, 1))
                                act.activation(tmp(z, 2, 2), bank(z, 2, 2), ACT.Tanh, scale=0.5).then_inc(g["ssm_zt"], 1)
                    act.preload_act_table_set(LN_EXP)

                    norm("moe3")
                    turned(3, [(lambda s: tmp(s, 3)[0:8, :], 3), (lambda s: mTb[s][0:8, :], 3)])
                    top1_experts(1, ACT.Gelu, "moe3_b1")

                @block.vector
                def _(dve):
                    links = [0]

                    def link(ins):
                        links[0] += 1
                        ins.then_inc(g["chain"], 1)
                        dve.wait_ge(g["chain"], links[0])

                    def norm(name, dst, eps=1e-5):
                        n = LN[name]
                        for s in range(SLOTS):
                            dve.wait_ge(g["rstd"], nth(n, s))
                            dve.tensor_tensor(dst(s), bank(s, 0), tmp(s, 1), ALU.mult).then_inc(g["normed"], 1)

                    def kv(n, name, wm, bm, wl, bl):
                        for s in range(SLOTS):
                            view = kvT[s][:, :].rearrange("p (b k) -> p b k", k=KEYS)
                            dve.tensor_scalar(view[:, :, 0:CTX], ctxz[s][:, :].rearrange("p (b k) -> p b k", k=CTX),
                                              V(wm), V(bm), ALU.mult, ALU.add)
                            dve.wait_ge(g["normed"], nth(LN[name], s))
                            dve.tensor_scalar(view[:, :, CTX:KEYS], seqs(A[s][:, :]), V(wl), V(bl), ALU.mult, ALU.add)\
                               .then_inc(g["kv_ready"], 1)
                        for s in range(SLOTS):
                            dve.wait_ge(g["kvn_ps"], nth(n, s))
                            dve.tensor_copy(T[s][0:64, GC:2 * GC], bank(s, 2, 2, 0, 64)).then_inc(g["kvl_ready"], 1)

                    def heads(gi, scale, bias, h0):
                        for r in range(2):
                            for s in range(SLOTS):
                                dve.wait_ge(g["qp_ps"], nth(2 * gi + r, s))
                                for k in (0, 1):
                                    h = 4 * r + k
                                    if bias:
                                        m = dve.tensor_scalar(by_head(s, h), seqs(bank(s, k)), scale,
                                                              qb(h0 + h), ALU.mult, ALU.add)
                                    else:
                                        m = dve.tensor_scalar(by_head(s, h), seqs(bank(s, k)), scale, None, ALU.mult)
                                m.then_inc(g["qp_dve"], 1)
                        def negmax(u, s):
                            for hf in range(2):
                                dve.wait_ge(g["scores"], nth_half(u, s, hf))
                                dve.tensor_reduce(small[s][:, 2 * hf:2 * hf + 2],
                                                  ps[s][:, BANK * hf:BANK * hf + 2 * KEYS].rearrange("p (c k) -> p c k", k=KEYS),
                                                  AX.X, ALU.max, negate=True).then_inc(g["maxed"], 1)

                        def inverse(u, s):
                            for hf in range(2):
                                dve.wait_ge(g["exped"], nth_half(u, s, hf))
                                dve.reciprocal(small[s][:, 12 + 2 * hf:14 + 2 * hf], small[s][:, 8 + 2 * hf:10 + 2 * hf])\
                                   .then_inc(g["rsum"], 1)

                        for s in range(SLOTS):
                            negmax(gi * GB, s)
                        for s in range(SLOTS):
                            inverse(gi * GB, s)
                        for b in range(GB):
                            u = gi * GB + b
                            for s in range(SLOTS):
                                dve.wait_ge(g["pT_ps"], nth(u, s))
                                dve.tensor_copy(P[s][0:64, 1536:2048], bank(s, 3, 1, 0, 64)).then_inc(g["pT_dve"], 1)
                                if b < GB - 1:
                                    negmax(u + 1, s)
                            for s in range(SLOTS):
                                if b < GB - 1:
                                    inverse(u + 1, s)
                                dve.wait_ge(g["mixed"], nth(u, s))
                                dve.tensor_copy(big[s][:, BANK * b:BANK * b + BANK], bank(s, 2)).then_inc(g["mix_out"], 1)
                        for s in range(SLOTS):
                            dve.wait_ge(g["heads_ps"], nth(gi, s))
                            if gi == 0:
                                dve.scalar_tensor_tensor(X[s][:, :], bank(s, 1), obias0[:, 0:1], X[s][:, :], ALU.add, ALU.add)\
                                   .then_inc(g["x_added"], 1)
                            else:
                                dve.tensor_tensor(X[s][:, :], bank(s, 1), X[s][:, :], ALU.add).then_inc(g["x_added"], 1)

                    norm("ctx0", lambda s: ctxz[s][:, 0:GT])
                    norm("ctx1", lambda s: ctxz[s][:, GT:GC])
                    norm("x0", lambda s: Z[s][:, :])
                    norm("lat0", lambda s: A[s][:, :])
                    kv(0, "lat0", "lmw", "lmb", "llw", "llb")
                    heads(0, 0.125, True, 0)
                    heads(1, 0.125, True, 8)

                    def add_to_x(done, n, k, bias=None):
                        for s in range(SLOTS):
                            dve.wait_ge(done, nth(n, s))
                            if bias is None:
                                dve.tensor_tensor(X[s][:, :], bank(s, k), X[s][:, :], ALU.add).then_inc(g["x_added"], 1)
                            else:
                                dve.scalar_tensor_tensor(X[s][:, :], bank(s, k), bias, X[s][:, :], ALU.add, ALU.add).then_inc(g["x_added"], 1)

                    def to_z(s):
                        return Z[s][:, :]

                    norm("rnn", to_z)
                    for s in range(SLOTS):
                        dve.wait_ge(g["rnn_in"], nth(0, s))
                        link(dve.tensor_scalar(big[s][:, 0:1024], bank(s, 0, 2), 0.0, 0.5, ALU.max, ALU.add))
                        dve.wait_ge(g["rnn_tanh"], nth(0, s))
                        link(dve.scalar_tensor_tensor(big[s][:, 1024:2048], tmp(s, 0, 2), 1.0, big[s][:, 0:1024], ALU.add, ALU.mult))
                        for k in range(2):
                            dve.wait_ge(g[f"rnn_keep{k}"], nth(0, s))
                            m = dve.tensor_tensor_scan(big[s][:, 2048 + GT * k:2048 + GT * k + GT], tmp(s, 2 + k),
                                                       big[s][:, 1024 + GT * k:1024 + GT * k + GT], 0.0, ALU.mult, ALU.add)
                        m.then_inc(g["rnn_h"], 1)
                    for s in range(SLOTS):
                        dve.wait_ge(g["rnn_out"], nth(0, s))
                        dve.scalar_tensor_tensor(X[s][:, :], bank(s, 0), 0.5, X[s][:, :], ALU.mult, ALU.add).then_inc(g["x_added"], 1)

                    def each(op):
                        for s in range(SLOTS):
                            m = op(s)
                        link(m)

                    def router(n, e, top):
                        wide = max(e, 8)
                        if wide > e:
                            each(lambda s: dve.memset(route(s, L, wide), NEG))
                        for s in range(SLOTS):
                            dve.wait_ge(g["logits"], nth(n, s))
                        each(lambda s: dve.tensor_copy(route(s, L, e), ps[s][:, 0:64].rearrange("p (t e) -> p t e", e=16)[:, :, 0:e]))
                        for s in range(SLOTS):
                            for t in range(TILES):
                                m = dve.max(small[s][:, M8 + 8 * t:M8 + 8 * t + 8], small[s][:, L + 16 * t:L + 16 * t + wide])
                        link(m)
                        if n != 3:
                            for s in range(SLOTS):
                                dve.tensor_tensor(route(s, U, e), route(s, L, e), over_e(s, M8, 0, e), ALU.subtract).then_inc(g["shifted"], 1)
                        for s in range(SLOTS):
                            for t in range(TILES):
                                m = dve.max_index(idx[s][:, 8 * t:8 * t + 8], small[s][:, M8 + 8 * t:M8 + 8 * t + 8],
                                                  small[s][:, L + 16 * t:L + 16 * t + wide])
                        link(m)
                        each(lambda s: dve.tensor_copy(small[s][:, IXF:IXF + 32], idx[s][:, :]))
                        iota = over(C("iota")[:, 0:e], 1, [128, TILES, e])
                        each(lambda s: dve.tensor_tensor(route(s, OH, e), iota, over_e(s, IXF, 0, e), ALU.is_equal))
                        if top == 2:
                            each(lambda s: dve.tensor_tensor(route(s, OH1, e), iota, over_e(s, IXF, 1, e), ALU.is_equal))
                            each(lambda s: dve.tensor_tensor(route(s, OH, e), route(s, OH, e), route(s, OH1, e), ALU.add))

                    def top2_weights(n, e):
                        for s in range(SLOTS):
                            dve.wait_ge(g["u_exp"], nth(n, s))
                        if e < 8:
                            each(lambda s: dve.memset(comb(s, CW), 0.0))
                        k = min(e, 8)
                        each(lambda s: dve.tensor_tensor(comb(s, CW)[:, :, 0:k], route(s, U, k), route(s, OH, k), ALU.mult))
                        each(lambda s: dve.tensor_reduce(small[s][:, DN:DN + 4], comb(s, CW), AX.X, ALU.add))
                        if e > 8:
                            each(lambda s: dve.tensor_scalar(small[s][:, DN + 4:DN + 8], small[s][:, DN:DN + 4], 0.0, None, ALU.is_equal))
                            each(lambda s: dve.tensor_tensor(small[s][:, DN:DN + 4], small[s][:, DN:DN + 4], small[s][:, DN + 4:DN + 8], ALU.add))
                        each(lambda s: dve.reciprocal(small[s][:, DN + 8:DN + 12], small[s][:, DN:DN + 4]))
                        for s in range(SLOTS):
                            dve.tensor_tensor(comb(s, CW), comb(s, CW), over(small[s][:, DN + 8:DN + 12], 2, [128, TILES, 8]), ALU.mult)\
                               .then_inc(g["comb"], 1)

                    norm("lora", to_z)
                    router(0, 10, 2)
                    top2_weights(0, 10)
                    for s in range(SLOTS):
                        dve.wait_ge(g["lora_b"], nth(0, s))
                        dve.tensor_tensor(tmp(s, 1), tmp(s, 0), bank(s, 1), ALU.mult).then_inc(g["lora_zs"], 1)
                    add_to_x(g["lora_out"], 0, 2, V("base_b"))

                    norm("x1", to_z)
                    for s in range(SLOTS):
                        dve.wait_ge(g["x1_proj"], nth(0, s))
                        dve.tensor_scalar(A[s][:, :], bank(s, 0), V("bq1"), None, ALU.add).then_inc(g["x1_q"], 1)
                    for s in range(SLOTS):
                        dve.wait_ge(g["x1_s"], nth(0, s))
                        m = dve.tensor_reduce(small[s][:, 12:16], bank(s, 0).rearrange("p (t k) -> p t k", k=CTX), AX.X, ALU.max,
                                              negate=True)
                    link(m)
                    for s in range(SLOTS):
                        dve.tensor_scalar(small[s][:, 16:20], small[s][:, 12:16], X1_SCALE, None, ALU.mult).then_inc(g["x1_max"], 1)
                    for s in range(SLOTS):
                        dve.wait_ge(g["x1_exp"], nth(0, s))
                        dve.reciprocal(small[s][:, 24:28], small[s][:, 20:24]).then_inc(g["x1_sum"], 1)
                    for s in range(SLOTS):
                        dve.wait_ge(g["x1_pT"], nth(0, s))
                        dve.tensor_copy(P[s][:, 512:1024], bank(s, 3)).then_inc(g["x1_pT_sb"], 1)
                    add_to_x(g["x1_o"], 0, 0, V("bv1"))

                    def head_out(u, t, k, eps):
                        for s in range(SLOTS):
                            dve.wait_ge(g["n_o"], nth(u, s))
                            both = ps[s][:, BANK * k:BANK * k + 9 * NH].rearrange("p (h c) -> p h c", c=9)
                            rec = small[s][:, 16:16 + NH].unsqueeze(2)
                            if eps:
                                link(dve.tensor_scalar(rec, both[:, :, 8:9], eps, None, ALU.add))
                                link(dve.reciprocal(rec, rec))
                            else:
                                link(dve.reciprocal(rec, both[:, :, 8:9]))
                            dve.tensor_tensor(kvT[s][:, 128 * t:128 * t + 128].rearrange("p (h d) -> p h d", d=HD), both[:, :, 0:8],
                                              over(small[s][:, 16:16 + NH], 2, [128, NH, HD]), ALU.mult).then_inc(g["n_y"], 1)

                    def softmax_heads(u0, v0):
                        def minus_max(u, s):
                            dve.wait_ge(g["n_s"], nth(u, s))
                            sc = bank(s, 0, 2).rearrange("p (h k) -> p h k", k=SEQ)
                            link(dve.tensor_reduce(small[s][:, 0:16], sc, AX.X, ALU.max))
                            dve.tensor_tensor(P[s][:, 0:1024].rearrange("p (h k) -> p h k", k=SEQ), sc,
                                              over(small[s][:, 0:16], 2, [128, NH, SEQ]), ALU.subtract).then_inc(g["n_sub"], 1)

                        for s in range(SLOTS):
                            minus_max(u0, s)
                        for t in range(TILES):
                            for s in range(SLOTS):
                                dve.wait_ge(g["n_pT"], nth(v0 + t, s))
                                dve.tensor_copy(P[s][:, 1536:2048], bank(s, 3)).then_inc(g["n_pT_dve"], 1)
                                if t < TILES - 1:
                                    minus_max(u0 + t + 1, s)
                            head_out(u0 + t, t, 2, 0.0)

                    norm("lin", to_z)
                    for s in range(SLOTS):
                        dve.wait_ge(g["n_proj"], nth(0, s))
                        dve.tensor_scalar(A[s][:, :], bank(s, 0), 0.0, None, ALU.max).then_inc(g["n_q"], 1)

                    def masked(t):
                        for s in range(SLOTS):
                            dve.wait_ge(g["n_s"], nth(t, s))
                            dve.tensor_tensor(P[s][:, 1024 * (t % 2):1024 * (t % 2) + 1024].rearrange("p (n t) -> p n t", t=SEQ),
                                              bank(s, 2 * (t % 2), 2).rearrange("p (n t) -> p n t", t=SEQ),
                                              over(C("causal_T"), 1, [128, 16, SEQ]), ALU.mult).then_inc(g["n_sub"], 1)

                    masked(0)
                    masked(1)
                    for t in range(TILES):
                        head_out(t, t, 2 * (t % 2), 1e-5)
                        if t + 2 < TILES:
                            masked(t + 2)
                    add_to_x(g["n_out"], 0, 2)

                    def rms(n, gain):
                        for s in range(SLOTS):
                            dve.wait_ge(g["rms_rstd"], nth(n, s))
                            dve.scalar_tensor_tensor(A[s][:, :], Z[s][:, :], gain, tmp(s, 1), ALU.mult, ALU.mult).then_inc(g["rms_done"], 1)

                    norm("moe1", to_z)
                    rms(0, V("g1"))
                    for s in range(SLOTS):
                        dve.wait_ge(g["n_proj"], nth(1, s))
                        for k in range(4):
                            m = dve.tensor_tensor(seqs(tmp(s, k)), seqs(bank(s, k)),
                                                  over(C("sin" if k % 2 else "cos"), 1, [128, GB, SEQ]), ALU.mult)
                        m.then_inc(g["rope_dve"], 1)
                    softmax_heads(4, 0)
                    for s in range(SLOTS):
                        dve.wait_ge(g["n_out"], nth(1, s))
                        dve.tensor_tensor(Z[s][:, :], bank(s, 2), Z[s][:, :], ALU.add).then_inc(g["y_ready"], 1)
                    rms(1, V("g2"))
                    router(1, MOE1_E, 2)
                    top2_weights(1, MOE1_E)
                    for s in range(SLOTS):
                        for e in range(MOE1_E):
                            dve.wait_ge(g["m1_bc"], MOE1_E * s + e + 1)
                            m = dve.tensor_tensor(big[s][:, BANK * e:BANK * e + BANK], A[s][:, :], bank(s, e), ALU.mult)
                        m.then_inc(g["m1_x"], 1)
                    for k in range(MOE1_K):
                        for s in range(SLOTS):
                            dve.wait_ge(g["m1_t"], nth(k, s))
                            m = dve.scalar_tensor_tensor(tmp(s, k % 2), P[s][:, 512 * (k % 2):512 * (k % 2) + 512], 1.0,
                                                         bank(s, H3[2 * k % 3]), ALU.add, ALU.mult)
                        link(m)
                        for s in range(SLOTS):
                            dve.wait_ge(g["m1_b"], nth(k, s))
                            dve.scalar_tensor_tensor(P[s][:, 1024 + 512 * (k % 2):1536 + 512 * (k % 2)], tmp(s, k % 2), 0.5,
                                                     bank(s, H3[(2 * k + 1) % 3]), ALU.mult, ALU.mult).then_inc(g["m1_g"], 1)
                    for s in range(SLOTS):
                        dve.wait_ge(g["m1_out"], nth(0, s))
                        m = dve.tensor_tensor(Z[s][:, :], bank(s, 2), Z[s][:, :], ALU.add)
                    link(m)
                    for s in range(SLOTS):
                        dve.tensor_tensor(X[s][:, :], Z[s][:, :], X[s][:, :], ALU.add).then_inc(g["x_added"], 1)

                    norm("x2", to_z)
                    norm("lat2", lambda s: A[s][:, :])
                    kv(1, "lat2", "gm", "bm", "gl", "bl")
                    heads(2, 8.0, False, 0)

                    norm("loc", to_z)
                    for s in range(SLOTS):
                        dve.wait_ge(g["n_proj"], nth(2, s))
                        dve.tensor_scalar(tmp(s, 0), bank(s, 0), V("bqkv", 0), None, ALU.add).then_inc(g["n_q"], 1)
                    softmax_heads(8, 4)
                    add_to_x(g["n_out"], 2, 2, V("bo2"))

                    def top1_experts(layer):
                        for e in range(EXPERTS):
                            n = layer * EXPERTS + e
                            for s in range(SLOTS):
                                dve.wait_ge(g["m2_act"], nth(n, s))
                                dve.wait_ge(g["m2_mask"], nth(n, s))
                                dve.tensor_tensor(P[s][:, 1024 + 512 * (e % 2):1536 + 512 * (e % 2)],
                                                  P[s][:, 512 * (e % 2):512 * (e % 2) + 512], bank(s, 1), ALU.mult).then_inc(g["m2_m"], 1)

                    norm("moe2", to_z)
                    router(2, EXPERTS, 1)
                    for s in range(SLOTS):
                        dve.tensor_copy(ohb[s][:, :].rearrange("p (t e) -> p t e", e=8), route(s, OH, 8)).then_inc(g["onehot"], 1)
                    for s in range(SLOTS):
                        dve.wait_ge(g["u_exp"], nth(2, s))
                    each(lambda s: dve.tensor_reduce(small[s][:, DN:DN + 4], route(s, U, 8), AX.X, ALU.add))
                    each(lambda s: dve.reciprocal(small[s][:, DN + 8:DN + 12], small[s][:, DN:DN + 4]))
                    for s in range(SLOTS):
                        dve.wait_ge(g["cum_ps"], nth(0, s))
                        link(dve.tensor_tensor(comb(s, G8), ps[s][:, BANK:BANK + 32].rearrange("p (t e) -> p t e", e=8),
                                               over(count[:, :], 1, [128, TILES, 8]), ALU.add))
                        link(dve.tensor_tensor(count[:, :], count[:, :], ps[s][:, BANK + 32:BANK + 40], ALU.add))
                        link(dve.scalar_tensor_tensor(comb(s, CW), comb(s, G8), float(CAPACITY), route(s, OH, 8), ALU.is_lt, ALU.mult))
                        dve.tensor_tensor(comb(s, G8), comb(s, CW), over(small[s][:, DN + 8:DN + 12], 2, [128, TILES, 8]), ALU.mult)\
                           .then_inc(g["comb"], 1)
                    for s in range(SLOTS):
                        dve.wait_ge(g["g_sb"], nth(0, s))
                        dve.tensor_tensor(A[s][:, :], Z[s][:, :], tmp(s, 0), ALU.mult).then_inc(g["xg"], 1)
                    top1_experts(0)
                    for s in range(SLOTS):
                        dve.wait_ge(g["m2_out"], nth(0, s))
                        m = dve.tensor_tensor(A[s][:, :], tmp(s, 0), bank(s, 2), ALU.mult)
                    link(m)
                    for s in range(SLOTS):
                        dve.tensor_tensor(X[s][:, :], X[s][:, :], A[s][:, :], ALU.add).then_inc(g["x_added"], 1)

                    for s in range(SLOTS):
                        dve.tensor_reduce(small[s][:, 0:8], ctxT[s][:, :].rearrange("p (b k) -> p b k", k=CTX), AX.X, ALU.add)\
                           .then_inc(g["x3_sum"], 1)
                    norm("x3", to_z)
                    for s in range(SLOTS):
                        dve.wait_ge(g["x3_ps"], nth(0, s))
                        dve.tensor_scalar(small[s][:, 8:16], ps[s][:, BANK:BANK + GB], 1.0 / CTX, V("b3"), ALU.mult, ALU.add)
                        m = dve.tensor_tensor(X[s][:, :], X[s][:, :], bank(s, 0), ALU.add)
                    link(m)
                    for s in range(SLOTS):
                        dve.tensor_tensor(seqs(X[s][:, :]), seqs(X[s][:, :]), over(small[s][:, 8:16], 2, [128, GB, SEQ]), ALU.add)\
                           .then_inc(g["x_added"], 1)

                    norm("ssm", to_z)

                    def silu(s, k):
                        dve.wait_ge(g["ssm_t"], nth_half(0, s, k))
                        dve.scalar_tensor_tensor(P[s][:, 1024 + GT * k:1024 + GT * k + GT], P[s][:, GT * k:GT * k + GT], 1.0,
                                                 big[s][:, 2048 + GT * k:2048 + GT * k + GT], ALU.add, ALU.mult)\
                           .then_inc(g["ssm_x"], 1)

                    def state(s):
                        dve.wait_ge(g["ssm_u"], nth(0, s))
                        link(dve.tensor_scalar(tmp(s, 0)[0:STATE, :], bank(s, 0, 1, 0, STATE), 0.05, None, ALU.mult))
                        dve.tensor_tensor_scan(tmp(s, 1)[0:STATE, :], C("decay")[0:STATE, :], tmp(s, 0)[0:STATE, :], 0.0,
                                               ALU.mult, ALU.add).then_inc(g["ssm_h"], 1)

                    for s in range(SLOTS):
                        dve.wait_ge(g["ssm_xp"], nth(0, s))
                        dve.wait_ge(g["ssm_tap"], nth(0, s))
                        for tap in range(3):
                            for k in range(2):
                                acc = seqs(big[s][:, 2048 + GT * k:2048 + GT * k + GT])
                                m = dve.scalar_tensor_tensor(acc, padded(s)[:, GB * k:GB * k + GB, tap:tap + SEQ],
                                                             V("conv_w", 4 * k + tap), acc, ALU.mult, ALU.add)
                                if tap == 2:
                                    m.then_inc(g["ssm_conv"], 1)
                            if tap < 2:
                                link(m)
                    for k in range(2):
                        silu(0, k)
                    silu(1, 0)
                    state(0)
                    silu(1, 1)
                    for s in range(SLOTS):
                        dve.wait_ge(g["ssm_zt"], nth(0, s))
                        m = dve.scalar_tensor_tensor(tmp(s, 2, 2), tmp(s, 2, 2), 1.0, bank(s, 2, 2), ALU.add, ALU.mult)
                        if s == 0:
                            state(1)
                    link(m)
                    for s in range(SLOTS):
                        dve.wait_ge(g["ssm_y"], nth(0, s))
                        dve.scalar_tensor_tensor(P[s][:, 0:1024], tmp(s, 2, 2), 0.5, bank(s, 0, 2), ALU.mult, ALU.mult)\
                           .then_inc(g["ssm_g"], 1)
                    add_to_x(g["ssm_out"], 0, 2)

                    norm("moe3", to_z)
                    router(3, EXPERTS, 1)
                    for s in range(SLOTS):
                        dve.tensor_copy(comb(s, CW), route(s, OH, 8)).then_inc(g["comb"], 1)
                    top1_experts(1)
                    add_to_x(g["m2_out"], 1, 2)

                @block.gpsimd
                def _(pool):
                    def heads(gi):
                        for b in range(GB):
                            u = gi * GB + b
                            for s in range(SLOTS):
                                for hf in range(2):
                                    pool.wait_ge(g["rsum"], nth_half(u, s, hf))
                                    view = P[s][:, 2 * KEYS * hf:2 * KEYS * hf + 2 * KEYS].rearrange("p (a k) -> p a k", k=KEYS)
                                    pool.tensor_tensor(view, view, over(small[s][:, 12 + 2 * hf:14 + 2 * hf], 2, [128, 2, KEYS]),
                                                       ALU.mult).then_inc(g["p_ready"], 1)

                    def pad(n, name):
                        for s in range(SLOTS):
                            pool.wait_ge(g["normed"], nth(LN[name], s))
                            pool.memset(T[s][64:128, GC:2 * GC], 0.0)
                            pool.memset(P[s][64:128, 1536:2048], 0.0).then_inc(g["kv_pad"], 1)

                    pad(0, "lat0")
                    heads(0)
                    heads(1)

                    links = [0]

                    def link(ins):
                        links[0] += 1
                        ins.then_inc(g["pool_chain"], 1)
                        pool.wait_ge(g["pool_chain"], links[0])

                    for s in range(SLOTS):
                        pool.wait_ge(g["rnn_tanh"], nth(0, s))
                        pool.memset(tmp(s, 2, 2).rearrange("p (n t) -> p n t", t=SEQ)[:, :, 0:1], 0.0)
                        pool.tensor_scalar(seqs(tmp(s, 2))[:, :, 1:SEQ], seqs(tmp(s, 0))[:, :, 1:SEQ], -0.5, 0.5,
                                           ALU.mult, ALU.add).then_inc(g["rnn_keep0"], 1)

                    for s in range(SLOTS):
                        pool.wait_ge(g["x1_sum"], nth(0, s))
                        view = P[s][:, 0:512].rearrange("p (t k) -> p t k", k=CTX)
                        pool.tensor_tensor(view, view, over(small[s][:, 24:28], 2, [128, TILES, CTX]), ALU.mult).then_inc(g["x1_p"], 1)

                    def spread(s, b, src, at):
                        return pool.tensor_tensor(big[s][:, at:at + 1024].rearrange("p (h t) -> p h t", t=SEQ),
                                                  over(src[:, SEQ * b:SEQ * b + SEQ], 1, [128, NH, SEQ]),
                                                  over(C("hmask"), 2, [128, NH, SEQ]), ALU.mult)

                    def spread_tiles(u0, src):
                        for t in range(TILES):
                            for s in range(SLOTS):
                                if t >= 2:
                                    pool.wait_ge(g["n_s"], nth(u0 + t - 2, s))
                                for bb in range(2):
                                    m = spread(s, 2 * t + bb, src(s), 2048 * (t % 2) + 1024 * bb)
                                m.then_inc(g["bd_ready"], 1)

                    for s in range(SLOTS):
                        pool.wait_ge(g["n_q"], nth(0, s))
                    spread_tiles(0, lambda s: A[s])

                    for s in range(SLOTS):
                        pool.wait_ge(g["rope_dve"], nth(0, s))
                        pool.tensor_tensor(tmp(s, 0), tmp(s, 0), tmp(s, 1), ALU.add)
                        link(pool.tensor_tensor(tmp(s, 2), tmp(s, 2), tmp(s, 3), ALU.add))
                    spread_tiles(4, lambda s: tmp(s, 2))

                    pad(1, "lat2")
                    heads(2)

                    for s in range(SLOTS):
                        pool.wait_ge(g["n_k"], nth(1, s))
                    spread_tiles(8, lambda s: tmp(s, 2))

                    for s in range(SLOTS):
                        pool.wait_ge(g["normed"], nth(LN["ssm"], s))
                        pool.memset(padded(s)[:, :, 0:3], 0.0).then_inc(g["ssm_pad"], 1)

            nc.all_engine_barrier(sems_to_clear=clear)

        with nc.Block() as block:
            @block.sync
            def _(sp):
                sp.wait_ge(x_free, 16 * SLOTS * PASSES + 16)
                for s in range(SLOTS):
                    sp.wait_ge(ctx_loaded[s], 16 * (PASSES + 1))


def pack(i):
    def heads_T(w):
        return w.T.reshape(-1, 128, 128).transpose(1, 0, 2).reshape(128, -1)

    def rows_of(w, n):
        return w.reshape(n, 128, -1).transpose(1, 0, 2).reshape(128, -1)

    def at(p, a):
        out = np.zeros((128, a.shape[-1]), np.float32)
        out[:p] = a
        return out

    def per_partition(v, n):
        return v.reshape(n, 128).T

    half = HD // 2
    swap = np.arange(D).reshape(-1, HD)
    swap = np.concatenate([swap[:, half:], swap[:, :half]], axis=1).ravel()
    kv_rep = np.arange(32).reshape(4, 1, HD).repeat(4, axis=1).ravel()
    wkv0, wkv2, wqkv = i["L0_xattn_Wkv"], i["L2_xattn_Wkv"], i["L1_attn_wqkv"]
    lq, bqkv = i["L2_attn_w_qkv"], i["L2_attn_b_qkv"]
    wk_rep = i["L1_ffn_wk"][:, kv_rep]
    fold = dict(q0T=heads_T(i["L0_xattn_Wq"]), k0T=heads_T(wkv0[:, :1024]), v0T=heads_T(wkv0[:, 1024:]),
                o0=rows_of(i["L0_xattn_Wout"], 8), q2T=heads_T(i["L2_xattn_Wq"]), k2T=heads_T(wkv2[:, :512]),
                v2T=heads_T(wkv2[:, 512:]), o2=rows_of(i["L2_xattn_Wout"], 4))
    one = lambda n: i[n].reshape(128, 1)
    cols = dict(lmw=one("L0_xattn_ln_media_w"), lmb=one("L0_xattn_ln_media_b"), llw=one("L0_xattn_ln_lat_w"),
                llb=one("L0_xattn_ln_lat_b"), bout0=one("L0_xattn_bout"), bq0=per_partition(i["L0_xattn_bq"], 8),
                bv0=per_partition(i["L0_xattn_bkv"][1024:], 8), base_b=one("L0_ffn_base_b"), bq1=one("L1_xattn_bq"),
                bk1=one("L1_xattn_bk"), bv1=one("L1_xattn_bv"), g1=one("L1_ffn_g1"), g2=one("L1_ffn_g2"),
                gm=one("L2_xattn_gm"), bm=one("L2_xattn_bm"), gl=one("L2_xattn_gl"), bl=one("L2_xattn_bl"),
                bqkv=per_partition(bqkv, 3), bo2=one("L2_attn_b_out"), moe2_b1=i["L2_ffn_b1"].T, b3=one("L3_xattn_b"),
                conv_w=i["L3_attn_conv_w"].reshape(2, 128, 4).transpose(1, 0, 2).reshape(128, 8),
                conv_b=per_partition(i["L3_attn_conv_b"], 2), moe3_b1=i["L3_ffn_b1"].T,
                br=at(1, i["L2_ffn_br"]), bg=at(1, i["L3_ffn_bg"]))
    experts = lambda w: w.transpose(1, 0, 2).reshape(128, -1)
    wts = dict(hg=i["L0_attn_W_hg"], rnn_out=rows_of(i["L0_attn_W_out"], 2), base=i["L0_ffn_base_w"].T,
               gate0=i["L0_ffn_gate_w"].T, loraA=i["L0_ffn_lora_A"].reshape(128, 128).T,
               loraB=i["L0_ffn_lora_B"].transpose(0, 2, 1).reshape(128, 128),
               q1=i["L1_xattn_Wq"], k1=i["L1_xattn_Wk"], v1=i["L1_xattn_Wv"],
               lin_q=wqkv[:, :128], lin_k=wqkv[:, 128:256], lin_v=wqkv[:, 256:], lin_o=i["L1_attn_wo"],
               rq=i["L1_ffn_wq"], rqp=i["L1_ffn_wq"][:, swap], rk=wk_rep, rkp=wk_rep[:, swap],
               rv=i["L1_ffn_wv"][:, kv_rep], ro=i["L1_ffn_wo"], gate1=i["L1_ffn_gate"],
               w1=experts(i["L1_ffn_w1"]), w3=experts(i["L1_ffn_w3"]), w2=rows_of(i["L1_ffn_w2"].reshape(-1, 128), 12),
               loc_q=lq[:, :128], loc_k=lq[:, 128:256], loc_v=lq[:, 256:], loc_o=i["L2_attn_w_out"],
               moe2_r=i["L2_ffn_Wr"], moe2_w1=experts(i["L2_ffn_W1"]), moe2_w2=experts(i["L2_ffn_W2"]),
               moe2_b2=at(8, i["L2_ffn_b2"]), x3a=i["L3_xattn_W"][:, :128].T, x3b=i["L3_xattn_W"][:, 128:].T,
               ssm_in=i["L3_attn_w_in"], ssm_B=rows_of(i["L3_attn_w_B"], 2), ssm_C=at(16, i["L3_attn_w_C"]),
               ssm_out=rows_of(i["L3_attn_w_out"], 2), moe3_r=i["L3_ffn_Wg"], moe3_w1=experts(i["L3_ffn_W1"]),
               moe3_w2=experts(i["L3_ffn_W2"]), moe3_b2=at(8, i["L3_ffn_b2"]))
    return [np.concatenate([parts[n] for n, _ in table], axis=1)
            for table, parts in ((FOLD, fold), (COLUMNS, cols), (WEIGHTS, wts))]


def shape_constants():
    p = np.arange(128)
    half = HD // 2
    inv = (np.float32(1.0) / np.float32(10000.0) ** (np.arange(0, HD, 2, dtype=np.float32) / np.float32(HD))).astype(np.float32)
    angle = np.arange(SEQ, dtype=np.float32)[None, :] * inv[p % half][:, None]
    sign = np.where(p % HD < half, -1.0, 1.0)[:, None]
    q, k = p[:, None] % SEQ, np.arange(SEQ)[None, :]
    decay = np.full((128, GT), 0.9)
    decay[:, ::SEQ] = 0.0
    c = dict(ident=np.eye(128), center=np.eye(128) - 1.0 / 128, mean=np.full((128, 128), 1.0 / 128),
             hmask=(p[:, None] // HD == np.arange(NH)[None, :]), cos=np.cos(angle), sin=np.sin(angle) * sign,
             causal_add=np.where(k <= q, 0.0, NEG), causal_T=(k >= q), upto=(p[:, None] <= p[None, :]),
             iota=np.broadcast_to(np.arange(16), (128, 16)), lora_sel=(p[:, None] == p[None, :] // LORA_R),
             decay=decay, ones_row=np.ones((128, 128)))
    return np.concatenate([np.asarray(c[n], np.float32) for n, _ in CONSTS], axis=1)


def kernel(**inputs):
    import concourse.bacc as bacc
    from concourse.bass_utils import run_bass_kernel_spmd

    i = {k: np.asarray(v) for k, v in inputs.items()}
    fold, cols, wts = pack(i)
    ctx = np.pad(i["ctx_1024"].reshape(BATCH * CTX, D).T, ((0, 0), (0, SLOTS * GC)))
    arrays = {"x_dram": i["x"].reshape(BATCH * SEQ, D).T, "ctx_dram": ctx,
              "fold_dram": fold, "cols_dram": cols, "weights_dram": wts, "consts_dram": shape_constants()}
    arrays = {k: np.ascontiguousarray(v) for k, v in arrays.items()}
    nc = bacc.Bacc("TRN2", target_bir_lowering=False, num_devices=1)
    f32 = mybir.dt.float32
    args = [nc.dram_tensor(k, v.shape, f32, kind="ExternalInput").ap() for k, v in arrays.items()]
    out = nc.dram_tensor("out_dram", (D, BATCH * SEQ), f32, kind="ExternalOutput").ap()
    build(nc, *args, out)
    r = run_bass_kernel_spmd(nc, [arrays], core_ids=[0])
    return np.ascontiguousarray(r.results[0]["out_dram"].T).reshape(BATCH, SEQ, D)
```

```python
import numpy as np
from contextlib import ExitStack

import concourse.bass as bass
from concourse import mybir

D = 128
BATCH, SEQ, CTX = 64, 64, 128
SLOTS = 2
GB = 8
GT = GB * SEQ
GC = GB * CTX
TILES = GT // 128
PASSES = BATCH // (GB * SLOTS)
BANK = 512
KEYS = CTX + SEQ
H0, H2, DH = 16, 8, 64
NH, HD = 16, 8
LORA_E, LORA_R = 8, 16
MOE1_E, MOE1_C = 4, 3
MOE1_K = MOE1_E * MOE1_C
H3 = (0, 1, 3)
EXPERTS = 8
CAPACITY = BATCH * SEQ // EXPERTS
NEG = -1.0e30

FOLD = [("q0T", 1024), ("k0T", 1024), ("v0T", 1024), ("o0", 1024), ("q2T", 512), ("k2T", 512), ("v2T", 512), ("o2", 512)]
COLUMNS = [("lmw", 1), ("lmb", 1), ("llw", 1), ("llb", 1), ("bout0", 1), ("bq0", 8), ("bv0", 8), ("base_b", 1),
           ("bq1", 1), ("bk1", 1), ("bv1", 1), ("g1", 1), ("g2", 1), ("gm", 1), ("bm", 1), ("gl", 1), ("bl", 1),
           ("bqkv", 3), ("bqk_turned", 2), ("bo2", 1), ("moe2_b1", 8), ("b3", 1), ("conv_w", 8), ("conv_b", 2), ("moe3_b1", 8),
           ("br", 8), ("bg", 8)]
WEIGHTS = [("hg", 512), ("rnn_out", 256), ("base", 128), ("gate0", 10), ("loraA", 128), ("loraB", 128),
           ("q1", 128), ("k1", 128), ("v1", 128), ("lin_q", 128), ("lin_k", 128), ("lin_v", 128), ("lin_o", 128),
           ("rq", 192), ("rqp", 192), ("rk", 192), ("rkp", 192), ("rv", 128), ("ro", 128), ("gate1", 4),
           ("w1", 1536), ("w3", 1536), ("w2", 1536),
           ("loc_q", 192), ("loc_k", 192), ("loc_v", 128), ("loc_o", 128),
           ("moe2_r", 8), ("moe2_w1", 1024), ("moe2_w2", 1024), ("moe2_b2", 128),
           ("x3a", 128), ("x3b", 128), ("ssm_in", 512), ("ssm_B", 256), ("ssm_C", 256), ("ssm_out", 256),
           ("moe3_r", 8), ("moe3_w1", 1024), ("moe3_w2", 1024), ("moe3_b2", 128)]
CONSTS = [("ident", 128), ("center", 128), ("mean", 128), ("hmask", NH), ("hmask8", NH // 2), ("cos", SEQ), ("sin", SEQ),
          ("causal_add", SEQ), ("causal_T", SEQ), ("upto", 128), ("iota", 16), ("lora_sel", 128),
          ("ones8", 128)]


def offsets(table):
    at, out = 0, {}
    for name, n in table:
        out[name] = (at, n)
        at += n
    return out, at


FOLD_AT, FOLD_N = offsets(FOLD)
COL_AT, COL_N = offsets(COLUMNS)
W_AT, W_N = offsets(WEIGHTS)
C_AT, C_N = offsets(CONSTS)


def build(nc, x, ctxin, fold, cols, weights, consts, out):
    f32, bf16, u32 = mybir.dt.float32, mybir.dt.bfloat16, mybir.dt.uint32
    ALU, ACT, AX = mybir.AluOpType, mybir.ActivationFunctionType, mybir.AxisListType

    stack = ExitStack()
    with stack:
        def sb(name, cols_, dt=f32):
            return stack.enter_context(nc.sbuf_tensor(name, [128, cols_], dt))

        def sem(name):
            return stack.enter_context(nc.semaphore(name))

        cst = sb("cst", C_N)
        col = sb("col", COL_N)
        wts = sb("wts", W_N)
        score0 = sb("score0", H0 * D)
        value0 = sb("value0", H0 * D)
        score2 = sb("score2", H2 * D)
        value2 = sb("value2", H2 * D)
        qbias0 = sb("qbias0", H0)
        obias0 = sb("obias0", 1)
        ident_b = sb("ident_b", 128, bf16)
        causal_b = sb("causal_b", SEQ, bf16)
        upto_b = sb("upto_b", 128, bf16)
        ones_b = sb("ones_b", 128, bf16)
        pick_b = sb("pick_b", EXPERTS * 128, bf16)
        eps5 = sb("eps5", 1)
        eps7 = sb("eps7", 1)
        count = sb("count", EXPERTS)

        def C(name):
            at, n = C_AT[name]
            return cst[:, at:at + n]

        def W(name):
            at, n = W_AT[name]
            return wts[:, at:at + n]

        def V(name, k=0):
            at = COL_AT[name][0] + k
            return col[:, at:at + 1]

        def per_slot(name, n, dt=f32):
            return [sb(f"{name}_{s}", n, dt) for s in range(SLOTS)]

        X = per_slot("X", GT)
        Z = per_slot("Z", GT)
        A = per_slot("A", GT)
        ctxT = per_slot("ctxT", GC)
        ctxz = per_slot("ctxz", GC)
        kvT = per_slot("kvT", GB * KEYS)
        T = per_slot("T", 4 * GT)
        big = per_slot("big", 4096)
        P = per_slot("P", 2048)
        Vbd = per_slot("Vbd", GB * 8 * 18)
        small = per_slot("small", 448)
        idx = per_slot("idx", TILES * 8, u32)
        ohb = per_slot("ohb", TILES * 8, bf16)
        mTb = per_slot("mTb", GT, bf16)

        ps = [stack.enter_context(nc.psum_tensor(f"ps_{s}", [128, 4 * BANK], f32)) for s in range(SLOTS)]

        def bank(s, k, n=1, p0=0, p1=128):
            return ps[s][p0:p1, k * BANK:(k + n) * BANK]

        def tmp(s, k, n=1):
            return T[s][:, k * GT:(k + n) * GT]

        def seqs(ap):
            return ap.rearrange("p (b t) -> p b t", t=SEQ)

        def by_head(s, h):
            return big[s][:, :].rearrange("p (b h t) -> p b h t", h=8, t=SEQ)[:, :, h, :]

        def block_of(h, n):
            return (h % 2) * (n // 2) + h // 2

        def qb(h):
            return qbias0[:, block_of(h, H0):block_of(h, H0) + 1]

        def over(ap, axis, shape):
            return ap.unsqueeze(axis).to_broadcast(shape)

        L, M8, OH, OH1, U, CW, G8, DN = 32, 96, 160, 224, 288, 352, 384, 416

        def route(s, at, e):
            return small[s][:, at:at + 64].rearrange("p (t e) -> p t e", e=16)[:, :, 0:e]

        def comb(s, at):
            return small[s][:, at:at + 32].rearrange("p (t e) -> p t e", e=8)

        L_BANK = (0, 0, 0, 1)

        CW16, G16 = 3584, 3072

        def rep16(s, at):
            return big[s][:, at:at + 512].rearrange("p (t n e) -> p t n e", n=16, e=8)

        def times16(ap):
            return ap.unsqueeze(2).to_broadcast([128, TILES, 16, 8])

        def over_e(s, at, k, e):
            return comb(s, at)[:, :, k:k + 1].to_broadcast([128, TILES, e])

        def padded(s):
            return big[s][:, 0:2 * GB * (SEQ + 3)].rearrange("p (n t) -> p n t", t=SEQ + 3)

        LN_EXP = "natural_log_exp_and_others"
        X1_SCALE = float(D) ** -0.5

        w_fold_qk = sem("w_fold_qk")
        w_fold, w_col, w_cst, w_main = sem("w_fold"), sem("w_col"), sem("w_cst"), [sem(f"w_main{k}") for k in range(4)]
        prep = sem("prep")
        folded, fold_out = sem("folded"), sem("fold_out")
        ctx_loaded, x_free = (sem("ctx_loaded0"), sem("ctx_loaded1")), sem("x_free")
        NAMES = ["x_loaded0", "x_loaded1",
                 "centered", "squared", "var", "log_var", "rstd", "normed", "rms_sq", "rms_var", "rms_rstd", "rms_done",
                 "kv_ctx", "kv_ready", "kvn_ps", "kvl_ps", "kvn_ready", "kvl_ready",
                 "qp_ps", "qp_act", "qp_dve", "scores", "maxed", "exped", "rsum", "p_ready", "pT_ps", "pT_act", "pT_dve",
                 "mixed", "mix_out", "heads_ps",
                 "rnn_gate", "rnn_in", "rnn_tanh", "rnn_keep0", "rnn_keep1", "rnn_h", "rnn_out",
                 "logits", "shifted", "u_exp", "comb", "combT_ps", "combT", "lora_z_ps", "lora_z", "lora_b", "lora_zs", "lora_out",
                 "x1_proj", "x1_q", "x1_k", "x1_s", "x1_v", "x1_max", "x1_exp", "x1_sum", "x1_p", "x1_pT", "x1_pT_sb", "x1_o",
                 "n_proj", "q_zero", "q_rope", "n_q", "n_k", "v_ps", "v_sb", "bd_ready", "bd_dve", "n_s", "n_sub", "n_exp",
                 "n_pT", "n_pT_act", "n_pT_dve", "n_o", "n_y", "n_yT", "n_yT_sb", "n_out",
                 "rope_dve", "rope", "y_ready", 
                 "m1_bc", "m1_x", "m1_a", "m1_b", "m1_t", "m1_g", "m1_xz", "m1_out",
                 "cum_ps", "g_bc", "g_sb", "xg", "m2_h", "m2_m", "m2_out", 
                 "onehot", "m2_mask", "m2_act", "x1_v_sb", "rms_log", "pool_chain", "kv_pad", "ssm_pad", "ssm_decay", "x3_sum", "x3_ctx", "x3_ps", "ssm_in", "ssm_xp", "ssm_tap", "ssm_conv", "ssm_t", "ssm_x", "ssm_u", "ssm_h", "ssm_y",
                 "ssm_zt", "ssm_g", "ssm_out", "chain", "x_added"]
        g = {n: sem(n) for n in NAMES}
        x_loaded = (g["x_loaded0"], g["x_loaded1"])
        clear = range(g["x_loaded0"].num, g["x_added"].num + 1)
        assert len(clear) == len(NAMES)

        def nth(n, s):
            return n * SLOTS + s + 1

        def nth_half(n, s, hf):
            return 2 * (n * SLOTS + s) + hf + 1

        with nc.Block() as block:
            @block.sync
            def _(sp):
                sp.dma_start(big[0][:, 0:2048], fold[:, 0:2048]).then_inc(w_fold_qk, 16)
                sp.dma_start(big[0][:, 2048:4096], fold[:, 2048:4096]).then_inc(w_fold, 16)
                sp.dma_start(big[1][:, 0:2048], fold[:, 4096:6144]).then_inc(w_fold, 16)
                sp.dma_start(col[:, :], cols[:, :]).then_inc(w_col, 16)
                sp.dma_start(cst[:, :], consts[:, :]).then_inc(w_cst, 16)
                cut = [0, W_AT["lin_q"][0], W_AT["w1"][0], W_AT["loc_q"][0], W_N]
                for s in range(SLOTS):
                    sp.dma_start(ctxT[s][:, :], ctxin[:, s * GC:s * GC + GC]).then_inc(ctx_loaded[s], 16)
                for k in range(4):
                    sp.dma_start(wts[:, cut[k]:cut[k + 1]], weights[:, cut[k]:cut[k + 1]]).then_inc(w_main[k], 16)

            @block.gpsimd
            def _(pool):
                pool.memset(count[:, :], 0.0).then_inc(prep, 1)
                pool.memset(eps7[:, :], 1.1920928955078125e-07).then_inc(x_free, 16)
                for s in range(SLOTS):
                    pool.wait_ge(prep, 3 * s + 1)
                    pool.memset(Vbd[s][:, :], 0.0).then_inc(prep, 1)
                    pool.wait_ge(prep, 3 * s + 2)
                    vb = Vbd[s][:, :].rearrange("p (n c) -> p n c", c=18)
                    pool.memset(vb[0:64, :, 8:9], 1.0).then_inc(prep, 1)
                    pool.wait_ge(prep, 3 * s + 3)
                    pool.memset(vb[64:128, :, 17:18], 1.0).then_inc(prep, 1)

            def rows(s, name, j, hh):
                at = FOLD_AT[name][0] - (4096 if s else 0)
                return big[s][64 * hh:64 * hh + 64, at + 128 * j:at + 128 * j + 128]

            @block.tensor
            def _(pe):
                pe.wait_ge(w_fold_qk, 16)
                for h in range(H0):
                    j, hh, at = h // 2, h % 2, 128 * block_of(h, H0)
                    m = pe.matmul(ps[0][:, at:at + 128], rows(0, "q0T", j, hh), rows(0, "k0T", j, hh), start=True, stop=True)
                m.then_inc(folded, 1)
                pe.wait_ge(w_fold, 32)
                pe.wait_ge(w_col, 16)
                for h in range(H0):
                    j, hh, at = h // 2, h % 2, 128 * block_of(h, H0)
                    m = pe.matmul(ps[1][:, at:at + 128], rows(0, "v0T", j, hh), rows(0, "o0", j, hh), start=True, stop=True)
                m.then_inc(folded, 1)
                pe.wait_ge(fold_out, 2)
                for h in range(H2):
                    j, hh, at = h // 2, h % 2, 128 * block_of(h, H2)
                    pe.matmul(ps[0][:, at:at + 128], rows(1, "q2T", j, hh), rows(1, "k2T", j, hh), start=True, stop=True)
                    m = pe.matmul(ps[1][:, at:at + 128], rows(1, "v2T", j, hh), rows(1, "o2", j, hh), start=True, stop=True)
                for h in range(H0):
                    j, hh = h // 2, h % 2
                    at, to = COL_AT["bq0"][0] + j, (2 + hh) * BANK + j
                    pe.matmul(ps[0][:, to:to + 1], rows(0, "k0T", j, hh), col[64 * hh:64 * hh + 64, at:at + 1],
                              start=True, stop=True)
                for j in range(H0 // 2):
                    at = FOLD_AT["o0"][0] + 128 * j
                    m = pe.matmul(ps[1][:, 2 * BANK:2 * BANK + 1], big[0][:, at:at + 128], V("bv0", j), start=(j == 0), stop=(j == 7))
                m.then_inc(folded, 1)

            @block.scalar
            def _(act):
                act.wait_ge(folded, 1)
                act.activation(score0[:, :], ps[0][:, :], ACT.Copy).then_inc(fold_out, 1)
                act.wait_ge(folded, 3)
                act.activation(score2[:, :], ps[0][:, 0:1024], ACT.Copy).then_inc(fold_out, 1)
                for hh in range(2):
                    act.activation(qbias0[:, 8 * hh:8 * hh + 8], ps[0][:, (2 + hh) * BANK:(2 + hh) * BANK + 8], ACT.Copy,
                                   scale=0.125).then_inc(fold_out, 1)

            @block.vector
            def _(dve):
                dve.wait_ge(w_cst, 16)
                dve.tensor_copy(ident_b[:, :], C("ident"))
                dve.tensor_copy(causal_b[:, :], C("causal_add"))
                dve.tensor_copy(upto_b[:, :], C("upto"))
                dve.tensor_copy(pick_b[:, :].rearrange("p (e m) -> p e m", m=128),
                                over(C("ident")[:, 0:EXPERTS], 2, [128, EXPERTS, 128]))
                dve.memset(ones_b[:, :], 1.0)
                dve.memset(eps5[:, :], 1e-5)
                dve.wait_ge(folded, 2)
                dve.tensor_copy(value0[:, :], ps[1][:, :]).then_inc(fold_out, 1)
                dve.wait_ge(folded, 3)
                dve.tensor_copy(value2[:, :], ps[1][:, 0:1024])
                dve.tensor_tensor(obias0[:, :], ps[1][:, 2 * BANK:2 * BANK + 1], V("bout0"), ALU.add)

        LAST = 12
        LN = dict(ctx0=0, ctx1=1, x0=2, lat0=3, rnn=4, lora=5, x1=6, lin=7, moe1=8, x2=9, lat2=10, loc=11, moe2=12, x3=13,
                  ssm=14, moe3=15)
        LN_PLACE = dict(ctx1=(2, 2), lat0=(0, 2), lat2=(0, 2))

        def spread(engine, s, b, src, at):
            return engine.tensor_tensor(big[s][:, at:at + 1024].rearrange("p (h t) -> p h t", t=SEQ),
                                        over(src[:, SEQ * b:SEQ * b + SEQ], 1, [128, NH, SEQ]),
                                        over(C("hmask"), 2, [128, NH, SEQ]), ALU.mult)

        QUADRANTS = ((0, 64, 0, 0), (0, 64, 1, 1), (64, 128, 0, 1), (64, 128, 1, 0))

        def parity(ap, c):
            return ap.rearrange("p (t c j) -> p t c j", c=2, j=SEQ)[:, :, c, :]

        def q_pairs(s):
            return big[s][:, 2048:3072]

        def k_pairs(s):
            return big[s][:, 3072:3584]

        def q_part(s, p0, p1, c, hf):
            return q_pairs(s)[p0:p1, :].rearrange("p (t h c j) -> p t h c j", h=2, c=2, j=SEQ)[:, :, hf, c, :]

        def k_part(s, p0, p1, hf):
            return k_pairs(s)[p0:p1, :].rearrange("p (t h j) -> p t h j", h=2, j=SEQ)[:, :, hf, :]

        def pair_tile(call, t):
            return TILES + (TILES - 1) * (call - 1) + t - 1

        def spread_pair(engine, s, t):
            return engine.tensor_tensor(
                big[s][:, 1024 * (t % 2):1024 * (t % 2) + 1024].rearrange("p (f h j) -> p f h j", f=2, j=SEQ),
                k_pairs(s)[:, 128 * t:128 * t + 128].rearrange("p (f j) -> p f j", f=2).unsqueeze(2).to_broadcast([128, 2, 8, SEQ]),
                C("hmask8").unsqueeze(1).unsqueeze(3).to_broadcast([128, 2, 8, SEQ]), ALU.mult)

        with nc.Fori(0, PASSES) as i:
            with nc.Block() as block:
                @block.sync
                def _(sp):
                    for s in range(SLOTS):
                        at = i * (SLOTS * GT) + s * GT
                        sp.wait_ge(x_free, 16 * SLOTS * i + 16)
                        sp.dma_start(X[s][:, :], x[:, bass.ds(at, GT)]).then_inc(x_loaded[s], 16)
                    for s in range(SLOTS):
                        atc = (i + 1) * (SLOTS * GC) + s * GC
                        sp.wait_ge(g["x3_sum"], nth(0, s))
                        sp.dma_start(ctxT[s][:, :], ctxin[:, bass.ds(atc, GC)]).then_inc(ctx_loaded[s], 16)
                    for s in range(SLOTS):
                        at = i * (SLOTS * GT) + s * GT
                        sp.wait_ge(g["x_added"], nth(LAST, s))
                        sp.dma_start(out[:, bass.ds(at, GT)], X[s][:, :]).then_inc(x_free, 16)

                @block.tensor
                def _(pe):
                    def added(n, s):
                        if n >= 0:
                            pe.wait_ge(g["x_added"], nth(n, s))

                    def norm(name, src, ready):
                        n, (kb, kt) = LN[name], LN_PLACE.get(name, (0, 0))
                        for s in range(SLOTS):
                            ready(s)
                            pe.matmul(bank(s, kb), C("center"), src(s), start=True, stop=True).then_inc(g["centered"], 1)
                        for s in range(SLOTS):
                            pe.wait_ge(g["squared"], nth(n, s))
                            pe.matmul(bank(s, kb + 1), C("mean"), tmp(s, kt), start=True, stop=True).then_inc(g["var"], 1)

                    def normed(name, s):
                        pe.wait_ge(g["normed"], nth(LN[name], s))

                    def kv_tokens(n):
                        for s in range(SLOTS):
                            pe.wait_ge(g["kv_ctx"], nth(n, s))
                            for b in range(GB):
                                m = pe.transpose(ps[s][:, 2 * BANK + 128 * b:2 * BANK + 128 * b + 128],
                                                 kvT[s][:, KEYS * b:KEYS * b + CTX], C("ident"))
                            m.then_inc(g["kvn_ps"], 1)
                        for s in range(SLOTS):
                            pe.wait_ge(g["kv_ready"], nth(n, s))
                            for b in range(GB):
                                m = pe.transpose(ps[s][0:64, 128 * b:128 * b + 128],
                                                 kvT[s][:, KEYS * b + CTX:KEYS * b + KEYS], C("ident"))
                            m.then_inc(g["kvl_ps"], 1)

                    def heads(gi, n, score, value, nh, h0):
                        for r in range(2):
                            for s in range(SLOTS):
                                if r == 0 and h0 == 0:
                                    pe.wait_ge(g["kvn_ready"], nth(n, s))
                                    pe.wait_ge(g["kvl_ready"], nth(n, s))
                                    pe.wait_ge(g["kv_pad"], nth(n, s))
                                elif r == 0:
                                    added(gi - 1, s)
                                else:
                                    pe.wait_ge(g["qp_act"], nth(2 * gi, s))
                                    pe.wait_ge(g["qp_dve"], nth(2 * gi, s))
                                lat = kvT[s][:, :].rearrange("p (b k) -> p b k", k=KEYS)[:, :, CTX:KEYS]
                                for k in range(4):
                                    h = h0 + 4 * r + k
                                    m = pe.matmul(bank(s, k), score[:, 128 * block_of(h, nh):128 * block_of(h, nh) + 128], lat, start=True, stop=True)
                                m.then_inc(g["qp_ps"], 1)
                        def scores(s, b):
                            for p in range(4):
                                at = (p // 2) * BANK + (p % 2) * KEYS
                                m = pe.matmul(ps[s][:, at:at + KEYS], big[s][:, BANK * b + 128 * p:BANK * b + 128 * p + 128],
                                              kvT[s][:, KEYS * b:KEYS * b + KEYS], start=True, stop=True)
                                if p % 2:
                                    m.then_inc(g["scores"], 1)

                        for s in range(SLOTS):
                            pe.wait_ge(g["qp_act"], nth(2 * gi + 1, s))
                            pe.wait_ge(g["qp_dve"], nth(2 * gi + 1, s))
                            scores(s, 0)
                        for b in range(GB):
                            u = gi * GB + b
                            for s in range(SLOTS):
                                pe.wait_ge(g["p_ready"], nth_half(u, s, 1))
                                if b:
                                    pe.wait_ge(g["mix_out"], nth(u - 1, s))
                                for p in range(4):
                                    pe.transpose(ps[s][:, 2 * BANK + 128 * p:2 * BANK + 128 * p + 128],
                                                 P[s][:, KEYS * p:KEYS * p + CTX], C("ident"))
                                    m = pe.transpose(ps[s][0:64, 3 * BANK + 128 * p:3 * BANK + 128 * p + 128],
                                                     P[s][:, KEYS * p + CTX:KEYS * p + KEYS], C("ident"))
                                m.then_inc(g["pT_ps"], 1)
                                if b < GB - 1:
                                    scores(s, b + 1)
                            for s in range(SLOTS):
                                pe.wait_ge(g["pT_act"], nth(u, s))
                                pe.wait_ge(g["pT_dve"], nth(u, s))
                                pe.matmul(bank(s, 2), T[s][:, 128 * b:128 * b + 128], P[s][:, 1024:1536], start=True, stop=False)
                                pe.matmul(bank(s, 2), T[s][:, GC + 128 * b:GC + 128 * b + 128], P[s][:, 1536:2048],
                                          start=False, stop=True).then_inc(g["mixed"], 1)
                        for s in range(SLOTS):
                            pe.wait_ge(g["mix_out"], nth(gi * GB + GB - 1, s))
                            for k in range(8):
                                m = pe.matmul(bank(s, 1), value[:, 128 * block_of(h0 + k, nh):128 * block_of(h0 + k, nh) + 128],
                                              by_head(s, k), start=(k == 0), stop=(k == 7))
                            m.then_inc(g["heads_ps"], 1)

                    pe.wait_ge(w_cst, 16)
                    for k in range(4):
                        pe.wait_ge(w_main[k], 16)
                    norm("ctx0", lambda s: ctxT[s][:, 0:GT], lambda s: pe.wait_ge(ctx_loaded[s], 16 * i + 16))
                    norm("ctx1", lambda s: ctxT[s][:, GT:GC], lambda s: None)
                    norm("x0", lambda s: X[s][:, :], lambda s: (normed("ctx0", s), pe.wait_ge(x_loaded[s], 16)))
                    norm("lat0", lambda s: Z[s][:, :], lambda s: normed("x0", s))
                    kv_tokens(0)
                    heads(0, 0, score0, value0, H0, 0)
                    heads(1, 0, score0, value0, H0, 8)

                    norm("rnn", lambda s: X[s][:, :], lambda s: added(1, s))
                    for s in range(SLOTS):
                        normed("rnn", s)
                        for k in (2, 3, 0, 1):
                            m = pe.matmul(bank(s, k), W("hg")[:, 128 * k:128 * k + 128], Z[s][:, :], start=True, stop=True)
                            if k % 2:
                                m.then_inc(g["rnn_gate" if k == 3 else "rnn_in"], 1)
                    for s in range(SLOTS):
                        pe.wait_ge(g["rnn_h"], nth(0, s))
                        for k in range(2):
                            m = pe.matmul(bank(s, 0), W("rnn_out")[:, 128 * k:128 * k + 128],
                                          big[s][:, 2048 + GT * k:2048 + GT * k + GT], start=(k == 0), stop=(k == 1))
                        m.then_inc(g["rnn_out"], 1)

                    def logits(n, ready, src, w, e, bias=None):
                        for s in range(SLOTS):
                            ready(s)
                            for t in range(TILES):
                                to = ps[s][:, BANK * L_BANK[n] + 16 * t:BANK * L_BANK[n] + 16 * t + e]
                                if bias:
                                    pe.matmul(to, C("ones8")[0:1, :], bias, start=True, stop=False)
                                m = pe.matmul(to, src(s)[:, 128 * t:128 * t + 128], w, start=not bias, stop=True)
                            m.then_inc(g["logits"], 1)

                    def turn(n, pairs):
                        for s in range(SLOTS):
                            pe.wait_ge(g["comb"], nth(n, s))
                            for at, k in pairs:
                                for t in range(TILES):
                                    m = pe.transpose(ps[s][:, k * BANK + 128 * t:k * BANK + 128 * t + 128],
                                                     big[s][:, at + 128 * t:at + 128 * t + 128], C("ident"))
                            m.then_inc(g["combT_ps"], 1)

                    norm("lora", lambda s: X[s][:, :], lambda s: added(2, s))
                    logits(0, lambda s: normed("lora", s), lambda s: Z[s], W("gate0"), 10)
                    for s in range(SLOTS):
                        pe.matmul(bank(s, 1), W("loraA"), Z[s][:, :], start=True, stop=True).then_inc(g["lora_z_ps"], 1)
                        pe.matmul(bank(s, 2), W("base"), Z[s][:, :], start=True, stop=False)
                    turn(0, [(CW16, 3)])
                    for s in range(SLOTS):
                        pe.wait_ge(g["combT"], nth(0, s))
                        pe.wait_ge(g["lora_z"], nth(0, s))
                        pe.matmul(bank(s, 1), C("lora_sel"), tmp(s, 3), start=True, stop=True).then_inc(g["lora_b"], 1)
                    for s in range(SLOTS):
                        pe.wait_ge(g["lora_zs"], nth(0, s))
                        pe.matmul(bank(s, 2), W("loraB"), tmp(s, 1), start=False, stop=True).then_inc(g["lora_out"], 1)

                    norm("x1", lambda s: X[s][:, :], lambda s: added(3, s))
                    for s in range(SLOTS):
                        normed("x1", s)
                        pe.matmul(bank(s, 0), W("q1"), Z[s][:, :], start=True, stop=True)
                        pe.matmul(bank(s, 1), W("k1"), ctxT[s][:, 0:GT], start=True, stop=True)
                        pe.matmul(bank(s, 2), W("k1"), ctxT[s][:, GT:GC], start=True, stop=True).then_inc(g["x1_proj"], 1)
                    for s in range(SLOTS):
                        pe.wait_ge(g["x1_q"], nth(0, s))
                        pe.wait_ge(g["x1_k"], nth(0, s))
                        for b in range(GB):
                            p0 = SEQ * (b % 2)
                            m = pe.matmul(ps[s][p0:p0 + SEQ, 128 * (b // 2):128 * (b // 2) + 128], A[s][:, SEQ * b:SEQ * b + SEQ],
                                          kvT[s][:, CTX * b:CTX * b + CTX], start=True, stop=True)
                        m.then_inc(g["x1_s"], 1)
                        for b in range(GB):
                            m = pe.matmul(ps[s][:, BANK + 128 * b:BANK + 128 * b + 128], ctxT[s][:, CTX * b:CTX * b + CTX],
                                          W("v1"), start=True, stop=True)
                        m.then_inc(g["x1_v"], 1)
                    for s in range(SLOTS):
                        pe.wait_ge(g["x1_p"], nth(0, s))
                        for t in range(TILES):
                            m = pe.transpose(ps[s][:, 3 * BANK + 128 * t:3 * BANK + 128 * t + 128], P[s][:, 128 * t:128 * t + 128],
                                             C("ident"))
                        m.then_inc(g["x1_pT"], 1)
                    for s in range(SLOTS):
                        pe.wait_ge(g["x1_pT_sb"], nth(0, s))
                        pe.wait_ge(g["x1_v_sb"], nth(0, s))
                        for b in range(GB):
                            m = pe.matmul(ps[s][:, SEQ * b:SEQ * b + SEQ], big[s][:, CTX * b:CTX * b + CTX],
                                          P[s][:, 512 + SEQ * b:512 + SEQ * b + SEQ], start=True, stop=True)
                        m.then_inc(g["x1_o"], 1)

                    def values(s, k, src, w):
                        wv = w.rearrange("p (j c d) -> p j c d", c=2, d=HD)
                        for b in range(GB):
                            for hh in range(2):
                                m = pe.matmul(ps[s][64 * hh:64 * hh + 64, k * BANK + 64 * b:k * BANK + 64 * b + 64],
                                              src[:, SEQ * b:SEQ * b + SEQ], wv[:, :, hh, :], start=True, stop=True)
                        m.then_inc(g["v_ps"], 1)

                    def project(m_, w):
                        for s in range(SLOTS):
                            for t in range(TILES):
                                m = pe.transpose(ps[s][:, BANK + 128 * t:BANK + 128 * t + 128], kvT[s][:, 128 * t:128 * t + 128],
                                                 C("ident"))
                            m.then_inc(g["n_yT"], 1)
                        for s in range(SLOTS):
                            pe.wait_ge(g["n_yT_sb"], nth(m_, s))
                            pe.matmul(bank(s, 2), w, kvT[s][:, GT:2 * GT], start=True, stop=True).then_inc(g["n_out"], 1)

                    def head_outputs(s, k, t, src):
                        for bb in range(2):
                            b = 2 * t + bb
                            for j in range(8):
                                m = pe.matmul(ps[s][64 * bb:64 * bb + 64, BANK * k + 18 * j:BANK * k + 18 * j + 18], src(bb, j),
                                              Vbd[s][:, 18 * (8 * b + j):18 * (8 * b + j) + 18], start=True, stop=True)
                        m.then_inc(g["n_o"], 1)

                    def project_turned(s, k, w, src):
                        for c in range(2):
                            m = pe.matmul(parity(bank(s, k), c), w[:, 64 * c:64 * c + 128], parity(src[:, :], c), start=True, stop=True)
                        return m

                    def softmax_heads(call, u0, v0, causal, q_ready, nq):
                        def scores(s, t):
                            if t == 0:
                                pe.wait_ge(q_ready, nq(s))
                                pe.wait_ge(g["bd_dve"], nth(call, s))
                            else:
                                pe.wait_ge(g["bd_ready"], nth(pair_tile(call, t), s))
                            for half in range(2 if causal else 0):
                                pe.matmul(bank(s, half), ident_b[:, :], over(causal_b[:, :], 1, [128, 8, SEQ]), start=True, stop=False)
                            for half in range(2):
                                q_at, k_at = 256 * t + 128 * half, 1024 * (t % 2) + 512 * half
                                m = pe.matmul(bank(s, half), q_pairs(s)[:, q_at:q_at + 128], big[s][:, k_at:k_at + 512],
                                              start=not causal, stop=True)
                            m.then_inc(g["n_s"], 1)

                        for s in range(SLOTS):
                            scores(s, 0)
                        for t in range(TILES):
                            u, v = u0 + t, v0 + t
                            for s in range(SLOTS):
                                pe.wait_ge(g["n_exp"], nth(v, s))
                                if t:
                                    pe.wait_ge(g["n_y"], nth(u - 1, s))
                                else:
                                    pe.wait_ge(g["v_sb"], nth(call, s))
                                for j in range(8):
                                    m = pe.transpose(ps[s][:, 2 * BANK + 128 * j:2 * BANK + 128 * j + 128],
                                                     P[s][:, 128 * j:128 * j + 128], C("ident"))
                                m.then_inc(g["n_pT"], 1)
                                if t < TILES - 1:
                                    scores(s, t + 1)
                            for s in range(SLOTS):
                                pe.wait_ge(g["n_pT_act"], nth(v, s))
                                pe.wait_ge(g["n_pT_dve"], nth(v, s))
                                head_outputs(s, 2, t, lambda bb, j: P[s][:, 1024 + 128 * j + 64 * bb:1024 + 128 * j + 64 * bb + 64])
                        for s in range(SLOTS):
                            pe.wait_ge(g["n_y"], nth(u0 + TILES - 1, s))

                    norm("lin", lambda s: X[s][:, :], lambda s: added(4, s))
                    for s in range(SLOTS):
                        normed("lin", s)
                        pe.matmul(bank(s, 0), W("lin_q"), Z[s][:, :], start=True, stop=True)
                        pe.matmul(bank(s, 1), W("lin_k"), Z[s][:, :], start=True, stop=True).then_inc(g["n_proj"], 1)
                        values(s, 2, Z[s], W("lin_v"))

                    def scores(s, t):
                        pe.wait_ge(g["bd_ready"], nth(t, s))
                        if t == 0:
                            pe.wait_ge(g["bd_dve"], nth(0, s))
                        for bb in range(2):
                            b, at = 2 * t + bb, 2048 * (t % 2) + 1024 * bb
                            q = big[s][:, at:at + 1024].rearrange("p (j c t) -> p j c t", c=2, t=SEQ)
                            for hh in range(2):
                                m = pe.matmul(bank(s, 2 * (t % 2) + bb, 1, 64 * hh, 64 * hh + 64), tmp(s, 2)[:, SEQ * b:SEQ * b + SEQ],
                                              q[:, :, hh, :], start=True, stop=True)
                        m.then_inc(g["n_s"], 1)

                    for t in range(2):
                        for s in range(SLOTS):
                            pe.wait_ge(g["n_k"], nth(0, s))
                            pe.wait_ge(g["v_sb"], nth(0, s))
                            scores(s, t)
                    for t in range(TILES):
                        for s in range(SLOTS):
                            pe.wait_ge(g["n_sub"], nth(t, s))
                            head_outputs(s, 2 * (t % 2), t, lambda bb, j: P[s][:, 1024 * (t % 2) + 64 * (8 * bb + j):
                                                                            1024 * (t % 2) + 64 * (8 * bb + j) + 64])
                        for s in range(SLOTS if t + 2 < TILES else 0):
                            pe.wait_ge(g["n_y"], nth(t, s))
                            scores(s, t + 2)
                    for s in range(SLOTS):
                        pe.wait_ge(g["n_y"], nth(TILES - 1, s))
                    project(0, W("lin_o"))

                    def rms(n, ready):
                        for s in range(SLOTS):
                            ready(s)
                            pe.wait_ge(g["rms_sq"], nth(n, s))
                            pe.matmul(bank(s, 1), C("mean"), tmp(s, 0), start=True, stop=True).then_inc(g["rms_var"], 1)

                    norm("moe1", lambda s: X[s][:, :], lambda s: added(5, s))
                    rms(0, lambda s: normed("moe1", s))
                    for s in range(SLOTS):
                        pe.wait_ge(g["rms_done"], nth(0, s))
                        for k, name in enumerate(("rq", "rqp", "rk", "rkp")):
                            m = project_turned(s, k, W(name), A[s])
                        m.then_inc(g["n_proj"], 1)
                    for s in range(SLOTS):
                        pe.wait_ge(g["rope_dve"], nth(0, s))
                        values(s, 2, A[s], W("rv"))
                    softmax_heads(1, 4, 0, True, g["q_rope"], lambda s: len(QUADRANTS) * (s + 1))
                    project(1, W("ro"))
                    rms(1, lambda s: None)
                    logits(1, lambda s: pe.wait_ge(g["rms_done"], nth(1, s)), lambda s: A[s], W("gate1"), MOE1_E)
                    turn(1, [(CW16, 3)])
                    for s in range(SLOTS):
                        pe.wait_ge(g["combT"], nth(1, s))
                        for e in range(MOE1_E):
                            pe.matmul(bank(s, e), C("ident")[:, e:e + 1].to_broadcast([128, 128]), tmp(s, 3),
                                      start=True, stop=True).then_inc(g["m1_bc"], 1)

                    def gate_half(s, k):
                        pe.matmul(bank(s, H3[2 * k % 3]), W("w1")[:, 128 * k:128 * k + 128], A[s][:, :], start=True, stop=True)\
                            .then_inc(g["m1_a"], 1)

                    def down(s, k):
                        m = pe.matmul(bank(s, 2), W("w2")[:, 128 * k:128 * k + 128], P[s][:, 1024 + 512 * (k % 2):1536 + 512 * (k % 2)],
                                      start=(k == 0), stop=(k == MOE1_K - 1))
                        if k == MOE1_K - 1:
                            m.then_inc(g["m1_out"], 1)

                    for s in range(SLOTS):
                        pe.wait_ge(g["m1_x"], nth(0, s))
                        gate_half(s, 0)
                    for k in range(MOE1_K):
                        for s in range(SLOTS):
                            if k:
                                pe.wait_ge(g["m1_g"], nth(k - 1, s))
                            at = BANK * (k // MOE1_C)
                            pe.matmul(bank(s, H3[(2 * k + 1) % 3]), W("w3")[:, 128 * k:128 * k + 128], big[s][:, at:at + BANK],
                                      start=True, stop=True).then_inc(g["m1_b"], 1)
                            if k < MOE1_K - 1:
                                gate_half(s, k + 1)
                            if k:
                                down(s, k - 1)
                    for s in range(SLOTS):
                        pe.wait_ge(g["m1_g"], nth(MOE1_K - 1, s))
                        down(s, MOE1_K - 1)

                    norm("x2", lambda s: X[s][:, :], lambda s: added(6, s))
                    norm("lat2", lambda s: Z[s][:, :], lambda s: normed("x2", s))
                    kv_tokens(1)
                    heads(2, 1, score2, value2, H2, 0)

                    norm("loc", lambda s: X[s][:, :], lambda s: added(7, s))
                    for s in range(SLOTS):
                        normed("loc", s)
                        project_turned(s, 0, W("loc_q"), Z[s])
                        project_turned(s, 1, W("loc_k"), Z[s]).then_inc(g["n_proj"], 1)
                        values(s, 2, Z[s], W("loc_v"))
                    for s in range(SLOTS):
                        pe.wait_ge(g["n_k"], nth(1, s))
                    softmax_heads(2, 8, 4, False, g["n_q"], lambda s: nth(1, s))
                    project(2, W("loc_o"))

                    def up(layer, w1, s, e):
                        src = A[s][:, :] if layer == 0 else Z[s][:, :]
                        pe.matmul(bank(s, 3 * (e % 2)), w1[:, 128 * e:128 * e + 128], src, start=True, stop=True).then_inc(g["m2_h"], 1)

                    def first_up(layer, w1):
                        for e in range(2):
                            for s in range(SLOTS):
                                up(layer, w1, s, e)

                    def top1_experts(layer, w1, w2, b2):
                        for s in range(SLOTS):
                            pe.matmul(bank(s, 2), b2, tmp(s, 3), start=True, stop=False)

                        def mask(s, e):
                            pe.matmul(bank(s, 1), pick_b[:, 128 * e:128 * e + 128], mTb[s][:, :], start=True, stop=True)\
                                .then_inc(g["m2_mask"], 1)

                        for s in range(SLOTS):
                            mask(s, 0)
                        for e in range(EXPERTS):
                            for s in range(SLOTS):
                                pe.wait_ge(g["m2_m"], nth(layer * EXPERTS + e, s))
                                if e + 1 < EXPERTS:
                                    mask(s, e + 1)
                                m = pe.matmul(bank(s, 2), w2[:, 128 * e:128 * e + 128], P[s][:, 1024 + 512 * (e % 2):1536 + 512 * (e % 2)],
                                              start=False, stop=(e == EXPERTS - 1))
                                if e == EXPERTS - 1:
                                    m.then_inc(g["m2_out"], 1)
                                if e + 2 < EXPERTS:
                                    up(layer, w1, s, e + 2)

                    norm("moe2", lambda s: X[s][:, :], lambda s: added(8, s))
                    at = COL_AT["br"][0]
                    logits(2, lambda s: normed("moe2", s), lambda s: Z[s], W("moe2_r"), 8, col[0:1, at:at + 8])
                    for s in range(SLOTS):
                        pe.wait_ge(g["onehot"], nth(0, s))
                        for t in range(TILES):
                            for t2 in range(t):
                                pe.matmul(ps[s][:, BANK + 8 * t:BANK + 8 * t + 8], ones_b[:, :], ohb[s][:, 8 * t2:8 * t2 + 8],
                                          start=(t2 == 0), stop=False)
                            pe.matmul(ps[s][:, BANK + 8 * t:BANK + 8 * t + 8], upto_b[:, :], ohb[s][:, 8 * t:8 * t + 8],
                                      start=(t == 0), stop=True)
                        for t in range(TILES):
                            m = pe.matmul(ps[s][:, BANK + 32:BANK + 40], ones_b[:, :], ohb[s][:, 8 * t:8 * t + 8],
                                          start=(t == 0), stop=(t == TILES - 1))
                        m.then_inc(g["cum_ps"], 1)
                    turn(2, [(CW16, 3), (G16, 2)])
                    for s in range(SLOTS):
                        pe.wait_ge(g["combT"], nth(2, s))
                        pe.matmul(bank(s, 0), C("ones8"), tmp(s, 2), start=True, stop=True).then_inc(g["g_bc"], 1)
                    for s in range(SLOTS):
                        pe.wait_ge(g["xg"], nth(0, s))
                    first_up(0, W("moe2_w1"))
                    top1_experts(0, W("moe2_w1"), W("moe2_w2"), W("moe2_b2"))

                    norm("x3", lambda s: X[s][:, :], lambda s: added(9, s))
                    for s in range(SLOTS):
                        normed("x3", s)
                        pe.wait_ge(g["x3_sum"], nth(0, s))
                        pe.matmul(ps[s][:, BANK:BANK + GB], W("x3b"), small[s][:, 0:8], start=True, stop=True).then_inc(g["x3_ctx"], 1)
                        pe.matmul(bank(s, 0), W("x3a"), Z[s][:, :], start=True, stop=True).then_inc(g["x3_ps"], 1)

                    norm("ssm", lambda s: X[s][:, :], lambda s: added(10, s))
                    for s in range(SLOTS):
                        normed("ssm", s)
                        for k in range(4):
                            m = pe.matmul(bank(s, k), W("ssm_in")[:, 128 * k:128 * k + 128], Z[s][:, :], start=True, stop=True)
                            if k % 2:
                                m.then_inc(g["ssm_in"], 1)
                    for s in range(SLOTS):
                        for k in range(2):
                            pe.wait_ge(g["ssm_x"], nth_half(0, s, k))
                            m = pe.matmul(bank(s, 0), W("ssm_B")[:, 128 * k:128 * k + 128],
                                          P[s][:, 1024 + GT * k:1024 + GT * k + GT], start=(k == 0), stop=(k == 1))
                        m.then_inc(g["ssm_u"], 1)
                    for s in range(SLOTS):
                        pe.wait_ge(g["ssm_h"], nth(0, s))
                        for k in range(2):
                            m = pe.matmul(bank(s, k), W("ssm_C")[:, 128 * k:128 * k + 128], tmp(s, 1),
                                          start=True, stop=True)
                        m.then_inc(g["ssm_y"], 1)
                    for s in range(SLOTS):
                        pe.wait_ge(g["ssm_g"], nth(0, s))
                        for k in range(2):
                            m = pe.matmul(bank(s, 2), W("ssm_out")[:, 128 * k:128 * k + 128], P[s][:, GT * k:GT * k + GT],
                                          start=(k == 0), stop=(k == 1))
                        m.then_inc(g["ssm_out"], 1)

                    norm("moe3", lambda s: X[s][:, :], lambda s: added(11, s))
                    at = COL_AT["bg"][0]
                    logits(3, lambda s: normed("moe3", s), lambda s: Z[s], W("moe3_r"), 8, col[0:1, at:at + 8])
                    first_up(1, W("moe3_w1"))
                    turn(3, [(CW16, 2)])
                    for s in range(SLOTS):
                        pe.wait_ge(g["combT"], nth(3, s))
                    top1_experts(1, W("moe3_w1"), W("moe3_w2"), W("moe3_b2"))

                @block.scalar
                def _(act):
                    def norm(name):
                        n, (kb, kt) = LN[name], LN_PLACE.get(name, (0, 0))
                        for s in range(SLOTS):
                            act.wait_ge(g["centered"], nth(n, s))
                            act.activation(tmp(s, kt), bank(s, kb), ACT.Square).then_inc(g["squared"], 1)
                        for s in range(SLOTS):
                            act.wait_ge(g["var"], nth(n, s))
                            act.activation(tmp(s, kt), bank(s, kb + 1), ACT.Ln, bias=eps5[:, 0:1]).then_inc(g["log_var"], 1)
                            act.wait_ge(g["log_var"], nth(n, s))
                            act.activation(tmp(s, kt + 1), tmp(s, kt), ACT.Exp, scale=-0.5).then_inc(g["rstd"], 1)

                    def kv_tokens(n):
                        for s in range(SLOTS):
                            act.wait_ge(g["kvn_ps"], nth(n, s))
                            act.activation(T[s][:, 0:GC], bank(s, 2, 2), ACT.Copy).then_inc(g["kvn_ready"], 1)

                    def heads(gi, scale, bias, h0):
                        for r in range(2):
                            for s in range(SLOTS):
                                act.wait_ge(g["qp_ps"], nth(2 * gi + r, s))
                                for k in (2, 3):
                                    h = 4 * r + k
                                    m = act.activation(by_head(s, h), seqs(bank(s, k)), ACT.Identity,
                                                       bias=qb(h0 + h) if bias else 0.0, scale=scale)
                                m.then_inc(g["qp_act"], 1)
                        def exps(u, s):
                            for p in range(4):
                                if p % 2 == 0:
                                    act.wait_ge(g["maxed"], nth_half(u, s, p // 2))
                                at = (p // 2) * BANK + (p % 2) * KEYS
                                m = act.activation(P[s][:, KEYS * p:KEYS * p + KEYS], ps[s][:, at:at + KEYS], ACT.Exp,
                                                   bias=small[s][:, p:p + 1], accum_out=small[s][:, 8 + p:9 + p])
                                if p % 2:
                                    m.then_inc(g["exped"], 1)

                        for s in range(SLOTS):
                            exps(gi * GB, s)
                        for b in range(GB):
                            u = gi * GB + b
                            for s in range(SLOTS):
                                act.wait_ge(g["pT_ps"], nth(u, s))
                                act.activation(P[s][:, 1024:1536], bank(s, 2), ACT.Copy).then_inc(g["pT_act"], 1)
                                if b < GB - 1:
                                    exps(u + 1, s)

                    act.preload_act_table_set(LN_EXP)
                    norm("ctx0")
                    norm("ctx1")
                    norm("x0")
                    norm("lat0")
                    kv_tokens(0)
                    heads(0, 0.125, True, 0)
                    heads(1, 0.125, True, 8)

                    norm("rnn")
                    for s in range(SLOTS):
                        act.wait_ge(g["rnn_gate"], nth(0, s))
                        act.activation(tmp(s, 0, 2), bank(s, 2, 2), ACT.Tanh, scale=0.5).then_inc(g["rnn_tanh"], 1)
                        act.wait_ge(g["rnn_tanh"], nth(0, s))
                        act.activation(seqs(tmp(s, 3))[:, :, 1:SEQ], seqs(tmp(s, 1))[:, :, 1:SEQ], ACT.Copy, scale=-0.5,
                                       bias=0.5).then_inc(g["rnn_keep1"], 1)
                    act.preload_act_table_set(LN_EXP)

                    def exp_logits(n, e):
                        for s in range(SLOTS):
                            act.wait_ge(g["shifted"], nth(n, s))
                            act.activation(route(s, U, e), route(s, U, e), ACT.Exp).then_inc(g["u_exp"], 1)

                    def turned(n, copies):
                        for s in range(SLOTS):
                            act.wait_ge(g["combT_ps"], nth(n, s))
                            for dst, k in copies:
                                m = act.activation(dst(s), bank(s, k), ACT.Copy)
                            m.then_inc(g["combT"], 1)

                    norm("lora")
                    for s in range(SLOTS):
                        act.wait_ge(g["lora_z_ps"], nth(0, s))
                        act.activation(tmp(s, 0), bank(s, 1), ACT.Copy, scale=2.0).then_inc(g["lora_z"], 1)
                    exp_logits(0, 10)
                    turned(0, [(lambda s: tmp(s, 3), 3)])

                    norm("x1")
                    for s in range(SLOTS):
                        act.wait_ge(g["x1_proj"], nth(0, s))
                        act.activation(kvT[s][:, 0:GC], bank(s, 1, 2), ACT.Identity, bias=V("bk1")).then_inc(g["x1_k"], 1)
                    for s in range(SLOTS):
                        act.wait_ge(g["x1_max"], nth(0, s))
                        for t in range(TILES):
                            m = act.activation(P[s][:, 128 * t:128 * t + 128], ps[s][:, 128 * t:128 * t + 128], ACT.Exp,
                                               bias=small[s][:, 16 + t:17 + t], scale=X1_SCALE, accum_out=small[s][:, 20 + t:21 + t])
                        m.then_inc(g["x1_exp"], 1)
                    for s in range(SLOTS):
                        act.wait_ge(g["x1_v"], nth(0, s))
                        act.activation(big[s][:, 0:GC], bank(s, 1, 2), ACT.Copy).then_inc(g["x1_v_sb"], 1)

                    def values(m_, k):
                        for s in range(SLOTS):
                            act.wait_ge(g["v_ps"], nth(m_, s))
                            vb = Vbd[s][:, :].rearrange("p (n c) -> p n c", c=18)
                            for hh in range(2):
                                p0 = 64 * hh
                                m = act.activation(vb[p0:p0 + 64, :, 9 * hh:9 * hh + 8],
                                                   bank(s, k, 1, p0, p0 + 64).rearrange("p (n d) -> p n d", d=HD), ACT.Copy)
                            m.then_inc(g["v_sb"], 1)

                    def project(m_, bias):
                        for s in range(SLOTS):
                            act.wait_ge(g["n_yT"], nth(m_, s))
                            act.activation(kvT[s][:, GT:2 * GT], bank(s, 1), ACT.Identity, bias=bias).then_inc(g["n_yT_sb"], 1)

                    def softmax_heads(v0):
                        def exps(v, s):
                            act.wait_ge(g["n_sub"], nth(v + TILES, s))
                            act.activation(P[s][:, 0:1024], P[s][:, 0:1024], ACT.Exp, scale=HD ** -0.5).then_inc(g["n_exp"], 1)

                        for s in range(SLOTS):
                            exps(v0, s)
                        for v in range(v0, v0 + TILES):
                            for s in range(SLOTS):
                                act.wait_ge(g["n_pT"], nth(v, s))
                                act.activation(P[s][:, 1024:1536], bank(s, 2), ACT.Copy).then_inc(g["n_pT_act"], 1)
                                if v < v0 + TILES - 1:
                                    exps(v + 1, s)

                    norm("lin")
                    for s in range(SLOTS):
                        act.wait_ge(g["n_proj"], nth(0, s))
                        act.activation(tmp(s, 2), bank(s, 1), ACT.Relu).then_inc(g["n_k"], 1)
                    values(0, 2)
                    project(0, 0.0)

                    def rms(n, ready):
                        for s in range(SLOTS):
                            ready(s)
                            act.activation(tmp(s, 0), Z[s][:, :], ACT.Square).then_inc(g["rms_sq"], 1)
                        for s in range(SLOTS):
                            act.wait_ge(g["rms_var"], nth(n, s))
                            act.activation(tmp(s, 0), bank(s, 1), ACT.Ln, bias=eps7[:, 0:1]).then_inc(g["rms_log"], 1)
                            act.wait_ge(g["rms_log"], nth(n, s))
                            act.activation(tmp(s, 1), tmp(s, 0), ACT.Exp, scale=-0.5).then_inc(g["rms_rstd"], 1)

                    norm("moe1")
                    rms(0, lambda s: act.wait_ge(g["normed"], nth(LN["moe1"], s)))
                    values(1, 2)
                    softmax_heads(0)
                    project(1, 0.0)
                    rms(1, lambda s: act.wait_ge(g["y_ready"], nth(0, s)))
                    exp_logits(1, MOE1_E)
                    turned(1, [(lambda s: tmp(s, 3), 3)])
                    for k in range(MOE1_K):
                        for s in range(SLOTS):
                            act.wait_ge(g["m1_a"], nth(k, s))
                            act.activation(P[s][:, 512 * (k % 2):512 * (k % 2) + 512], bank(s, H3[2 * k % 3]), ACT.Tanh, scale=0.5)\
                               .then_inc(g["m1_t"], 1)
                    act.preload_act_table_set(LN_EXP)

                    norm("x2")
                    norm("lat2")
                    kv_tokens(1)
                    heads(2, 8.0, False, 0)

                    norm("loc")
                    for s in range(SLOTS):
                        act.wait_ge(g["n_proj"], nth(2, s))
                        for p0, p1, c, hf in QUADRANTS:
                            m = act.activation(k_part(s, p0, p1, hf), parity(bank(s, 1, 1, p0, p1), c), ACT.Identity,
                                               bias=V("bqk_turned" if c else "bqkv", 1)[p0:p1, :])
                        m.then_inc(g["n_k"], 1)
                    values(2, 2)
                    softmax_heads(4)
                    project(2, V("bqkv", 2))

                    def top1_experts(layer, func, b1):
                        for e in range(EXPERTS):
                            n = layer * EXPERTS + e
                            for s in range(SLOTS):
                                act.wait_ge(g["m2_h"], nth(n, s))
                                act.activation(P[s][:, 512 * (e % 2):512 * (e % 2) + 512], bank(s, 3 * (e % 2)), func, bias=V(b1, e))\
                                    .then_inc(g["m2_act"], 1)

                    norm("moe2")
                    exp_logits(2, EXPERTS)
                    turned(2, [(lambda s: tmp(s, 3), 3), (lambda s: mTb[s][:, :], 3), (lambda s: tmp(s, 2), 2)])
                    for s in range(SLOTS):
                        act.wait_ge(g["g_bc"], nth(0, s))
                        act.activation(tmp(s, 0), bank(s, 0), ACT.Copy).then_inc(g["g_sb"], 1)
                    top1_experts(0, ACT.Relu, "moe2_b1")

                    norm("x3")

                    norm("ssm")
                    for s in range(SLOTS):
                        act.wait_ge(g["ssm_in"], nth_half(0, s, 0))
                        act.wait_ge(g["ssm_pad"], nth(0, s))
                        act.activation(padded(s)[:, :, 3:67], bank(s, 0, 2).rearrange("p (n t) -> p n t", t=SEQ), ACT.Copy)\
                           .then_inc(g["ssm_xp"], 1)
                        for k in range(2):
                            m = act.activation(big[s][:, 2048 + GT * k:2048 + GT * k + GT], bank(s, k), ACT.Identity,
                                               scale=V("conv_w", 4 * k + 3), bias=V("conv_b", k))
                        m.then_inc(g["ssm_tap"], 1)
                    for s in range(SLOTS):
                        for k in range(2):
                            act.wait_ge(g["ssm_conv"], nth_half(0, s, k))
                            act.activation(P[s][:, GT * k:GT * k + GT], big[s][:, 2048 + GT * k:2048 + GT * k + GT], ACT.Tanh,
                                           scale=0.5).then_inc(g["ssm_t"], 1)
                        if s == 0:
                            for z in range(SLOTS):
                                act.wait_ge(g["ssm_in"], nth_half(0, z, 1))
                                act.activation(tmp(z, 2, 2), bank(z, 2, 2), ACT.Tanh, scale=0.5).then_inc(g["ssm_zt"], 1)
                    act.preload_act_table_set(LN_EXP)

                    norm("moe3")
                    turned(3, [(lambda s: tmp(s, 3), 2), (lambda s: mTb[s][:, :], 2)])
                    top1_experts(1, ACT.Gelu, "moe3_b1")

                @block.vector
                def _(dve):
                    links = [0]

                    def link(ins):
                        links[0] += 1
                        ins.then_inc(g["chain"], 1)
                        dve.wait_ge(g["chain"], links[0])

                    def norm(name, dst):
                        n, (kb, kt) = LN[name], LN_PLACE.get(name, (0, 0))
                        for s in range(SLOTS):
                            dve.wait_ge(g["rstd"], nth(n, s))
                            dve.tensor_tensor(dst(s), bank(s, kb), tmp(s, kt + 1), ALU.mult).then_inc(g["normed"], 1)

                    def kv_context(name, w, b):
                        for s in range(SLOTS):
                            dve.wait_ge(g["normed"], nth(LN[name], s))
                            dve.tensor_scalar(kvT[s][:, :].rearrange("p (b k) -> p b k", k=KEYS)[:, :, 0:CTX],
                                              ctxz[s][:, :].rearrange("p (b k) -> p b k", k=CTX), V(w), V(b), ALU.mult, ALU.add)\
                               .then_inc(g["kv_ctx"], 1)

                    def kv_latents(n, name, w, b):
                        for s in range(SLOTS):
                            dve.wait_ge(g["normed"], nth(LN[name], s))
                            dve.tensor_scalar(kvT[s][:, :].rearrange("p (b k) -> p b k", k=KEYS)[:, :, CTX:KEYS], seqs(A[s][:, :]),
                                              V(w), V(b), ALU.mult, ALU.add).then_inc(g["kv_ready"], 1)
                        for s in range(SLOTS):
                            dve.wait_ge(g["kvl_ps"], nth(n, s))
                            dve.tensor_copy(T[s][0:64, GC:2 * GC], bank(s, 0, 2, 0, 64)).then_inc(g["kvl_ready"], 1)

                    def heads(gi, scale, bias, h0):
                        for r in range(2):
                            for s in range(SLOTS):
                                dve.wait_ge(g["qp_ps"], nth(2 * gi + r, s))
                                for k in (0, 1):
                                    h = 4 * r + k
                                    if bias:
                                        m = dve.tensor_scalar(by_head(s, h), seqs(bank(s, k)), scale,
                                                              qb(h0 + h), ALU.mult, ALU.add)
                                    else:
                                        m = dve.tensor_scalar(by_head(s, h), seqs(bank(s, k)), scale, None, ALU.mult)
                                m.then_inc(g["qp_dve"], 1)
                        def negmax(u, s):
                            for hf in range(2):
                                dve.wait_ge(g["scores"], nth_half(u, s, hf))
                                dve.tensor_reduce(small[s][:, 2 * hf:2 * hf + 2],
                                                  ps[s][:, BANK * hf:BANK * hf + 2 * KEYS].rearrange("p (c k) -> p c k", k=KEYS),
                                                  AX.X, ALU.max, negate=True).then_inc(g["maxed"], 1)

                        def inverse(u, s):
                            for hf in range(2):
                                dve.wait_ge(g["exped"], nth_half(u, s, hf))
                                dve.reciprocal(small[s][:, 12 + 2 * hf:14 + 2 * hf], small[s][:, 8 + 2 * hf:10 + 2 * hf])\
                                   .then_inc(g["rsum"], 1)

                        for s in range(SLOTS):
                            negmax(gi * GB, s)
                        for s in range(SLOTS):
                            inverse(gi * GB, s)
                        for b in range(GB):
                            u = gi * GB + b
                            for s in range(SLOTS):
                                dve.wait_ge(g["pT_ps"], nth(u, s))
                                dve.tensor_copy(P[s][0:64, 1536:2048], bank(s, 3, 1, 0, 64)).then_inc(g["pT_dve"], 1)
                                if b < GB - 1:
                                    negmax(u + 1, s)
                            for s in range(SLOTS):
                                if b < GB - 1:
                                    inverse(u + 1, s)
                                dve.wait_ge(g["mixed"], nth(u, s))
                                dve.tensor_copy(big[s][:, BANK * b:BANK * b + BANK], bank(s, 2)).then_inc(g["mix_out"], 1)
                        for s in range(SLOTS):
                            dve.wait_ge(g["heads_ps"], nth(gi, s))
                            if gi == 0:
                                dve.scalar_tensor_tensor(X[s][:, :], bank(s, 1), obias0[:, 0:1], X[s][:, :], ALU.add, ALU.add)\
                                   .then_inc(g["x_added"], 1)
                            else:
                                dve.tensor_tensor(X[s][:, :], bank(s, 1), X[s][:, :], ALU.add).then_inc(g["x_added"], 1)

                    norm("ctx0", lambda s: ctxz[s][:, 0:GT])
                    norm("ctx1", lambda s: ctxz[s][:, GT:GC])
                    norm("x0", lambda s: Z[s][:, :])
                    kv_context("ctx1", "lmw", "lmb")
                    norm("lat0", lambda s: A[s][:, :])
                    kv_latents(0, "lat0", "llw", "llb")
                    heads(0, 0.125, True, 0)
                    heads(1, 0.125, True, 8)

                    def add_to_x(done, n, k, bias=None):
                        for s in range(SLOTS):
                            dve.wait_ge(done, nth(n, s))
                            if bias is None:
                                dve.tensor_tensor(X[s][:, :], bank(s, k), X[s][:, :], ALU.add).then_inc(g["x_added"], 1)
                            else:
                                dve.scalar_tensor_tensor(X[s][:, :], bank(s, k), bias, X[s][:, :], ALU.add, ALU.add).then_inc(g["x_added"], 1)

                    def to_z(s):
                        return Z[s][:, :]

                    norm("rnn", to_z)
                    for s in range(SLOTS):
                        dve.wait_ge(g["rnn_in"], nth(0, s))
                        link(dve.tensor_scalar(big[s][:, 0:1024], bank(s, 0, 2), 0.0, 0.5, ALU.max, ALU.add))
                        dve.wait_ge(g["rnn_tanh"], nth(0, s))
                        link(dve.scalar_tensor_tensor(big[s][:, 1024:2048], tmp(s, 0, 2), 1.0, big[s][:, 0:1024], ALU.add, ALU.mult))
                        for k in range(2):
                            dve.wait_ge(g[f"rnn_keep{k}"], nth(0, s))
                            m = dve.tensor_tensor_scan(big[s][:, 2048 + GT * k:2048 + GT * k + GT], tmp(s, 2 + k),
                                                       big[s][:, 1024 + GT * k:1024 + GT * k + GT], 0.0, ALU.mult, ALU.add)
                        m.then_inc(g["rnn_h"], 1)
                    for s in range(SLOTS):
                        dve.wait_ge(g["rnn_out"], nth(0, s))
                        dve.scalar_tensor_tensor(X[s][:, :], bank(s, 0), 0.5, X[s][:, :], ALU.mult, ALU.add).then_inc(g["x_added"], 1)

                    def each(op):
                        for s in range(SLOTS):
                            m = op(s)
                        link(m)

                    def router(n, e, top):
                        wide = max(e, 8)
                        in_bank = [ps[s][:, BANK * L_BANK[n]:BANK * L_BANK[n] + 64] for s in range(SLOTS)]
                        if wide > e:
                            each(lambda s: dve.memset(route(s, L, wide), NEG))
                        for s in range(SLOTS):
                            dve.wait_ge(g["logits"], nth(n, s))
                        if wide > e:
                            each(lambda s: dve.tensor_copy(route(s, L, e), in_bank[s].rearrange("p (t e) -> p t e", e=16)[:, :, 0:e]))
                        at = [small[s][:, L:L + 64] for s in range(SLOTS)] if wide > e else in_bank
                        for s in range(SLOTS):
                            for t in range(TILES):
                                m = dve.max(small[s][:, M8 + 8 * t:M8 + 8 * t + 8], at[s][:, 16 * t:16 * t + wide])
                        link(m)
                        if n != 3:
                            for s in range(SLOTS):
                                dve.tensor_tensor(route(s, U, e), at[s].rearrange("p (t e) -> p t e", e=16)[:, :, 0:e],
                                                  over_e(s, M8, 0, e), ALU.subtract).then_inc(g["shifted"], 1)
                        for s in range(SLOTS):
                            for t in range(TILES):
                                m = dve.max_index(idx[s][:, 8 * t:8 * t + 8], small[s][:, M8 + 8 * t:M8 + 8 * t + 8],
                                                  at[s][:, 16 * t:16 * t + wide])
                        link(m)
                        iota = over(C("iota")[:, 0:e], 1, [128, TILES, e])
                        for s in range(SLOTS):
                            for k, to in ((0, OH), (1, OH1))[0:top]:
                                chosen = idx[s][:, :].rearrange("p (t e) -> p t e", e=8)[:, :, k:k + 1].to_broadcast([128, TILES, e])
                                m = dve.tensor_tensor(route(s, to, e), iota, chosen, ALU.is_equal)
                        link(m)
                        if top == 2:
                            each(lambda s: dve.tensor_tensor(route(s, OH, e), route(s, OH, e), route(s, OH1, e), ALU.add))

                    def top2_weights(n, e):
                        for s in range(SLOTS):
                            dve.wait_ge(g["u_exp"], nth(n, s))
                        if e < 8:
                            each(lambda s: dve.memset(comb(s, CW), 0.0))
                        k = min(e, 8)
                        each(lambda s: dve.tensor_tensor(comb(s, CW)[:, :, 0:k], route(s, U, k), route(s, OH, k), ALU.mult))
                        each(lambda s: dve.tensor_reduce(small[s][:, DN:DN + 4], comb(s, CW), AX.X, ALU.add))
                        if e > 8:
                            each(lambda s: dve.tensor_scalar(small[s][:, DN + 4:DN + 8], small[s][:, DN:DN + 4], 0.0, None, ALU.is_equal))
                            each(lambda s: dve.tensor_tensor(small[s][:, DN:DN + 4], small[s][:, DN:DN + 4], small[s][:, DN + 4:DN + 8], ALU.add))
                        each(lambda s: dve.reciprocal(small[s][:, DN + 8:DN + 12], small[s][:, DN:DN + 4]))
                        for s in range(SLOTS):
                            dve.tensor_tensor(rep16(s, CW16), times16(comb(s, CW)), times16(over(small[s][:, DN + 8:DN + 12], 2, [128, TILES, 8])), ALU.mult)\
                               .then_inc(g["comb"], 1)

                    norm("lora", to_z)
                    router(0, 10, 2)
                    top2_weights(0, 10)
                    for s in range(SLOTS):
                        dve.wait_ge(g["lora_b"], nth(0, s))
                        dve.tensor_tensor(tmp(s, 1), tmp(s, 0), bank(s, 1), ALU.mult).then_inc(g["lora_zs"], 1)
                    add_to_x(g["lora_out"], 0, 2, V("base_b"))

                    norm("x1", to_z)
                    for s in range(SLOTS):
                        dve.wait_ge(g["x1_proj"], nth(0, s))
                        dve.tensor_scalar(A[s][:, :], bank(s, 0), V("bq1"), None, ALU.add).then_inc(g["x1_q"], 1)
                    for s in range(SLOTS):
                        dve.wait_ge(g["x1_s"], nth(0, s))
                        link(dve.tensor_reduce(small[s][:, 12:16], bank(s, 0).rearrange("p (t k) -> p t k", k=CTX), AX.X, ALU.max,
                                               negate=True))
                        dve.tensor_scalar(small[s][:, 16:20], small[s][:, 12:16], X1_SCALE, None, ALU.mult).then_inc(g["x1_max"], 1)
                    for s in range(SLOTS):
                        dve.wait_ge(g["x1_exp"], nth(0, s))
                        dve.reciprocal(small[s][:, 24:28], small[s][:, 20:24]).then_inc(g["x1_sum"], 1)
                    for s in range(SLOTS):
                        dve.wait_ge(g["x1_pT"], nth(0, s))
                        dve.tensor_copy(P[s][:, 512:1024], bank(s, 3)).then_inc(g["x1_pT_sb"], 1)
                    add_to_x(g["x1_o"], 0, 0, V("bv1"))

                    def head_out(u, t, k, eps):
                        for s in range(SLOTS):
                            dve.wait_ge(g["n_o"], nth(u, s))
                            both = ps[s][:, BANK * k:BANK * k + 9 * NH].rearrange("p (h c) -> p h c", c=9)
                            rec = small[s][:, 16:16 + NH].unsqueeze(2)
                            if eps:
                                link(dve.tensor_scalar(rec, both[:, :, 8:9], eps, None, ALU.add))
                                link(dve.reciprocal(rec, rec))
                            else:
                                link(dve.reciprocal(rec, both[:, :, 8:9]))
                            dve.tensor_tensor(kvT[s][:, 128 * t:128 * t + 128].rearrange("p (h d) -> p h d", d=HD), both[:, :, 0:8],
                                              over(small[s][:, 16:16 + NH], 2, [128, NH, HD]), ALU.mult).then_inc(g["n_y"], 1)

                    def softmax_heads(u0, v0):
                        def minus_max(u, s):
                            dve.wait_ge(g["n_s"], nth(u, s))
                            sc = bank(s, 0, 2).rearrange("p (h k) -> p h k", k=SEQ)
                            link(dve.tensor_reduce(small[s][:, 0:16], sc, AX.X, ALU.max))
                            dve.tensor_tensor(P[s][:, 0:1024].rearrange("p (h k) -> p h k", k=SEQ), sc,
                                              over(small[s][:, 0:16], 2, [128, NH, SEQ]), ALU.subtract).then_inc(g["n_sub"], 1)

                        for s in range(SLOTS):
                            minus_max(u0, s)
                        for t in range(TILES):
                            for s in range(SLOTS):
                                dve.wait_ge(g["n_pT"], nth(v0 + t, s))
                                dve.tensor_copy(P[s][:, 1536:2048], bank(s, 3)).then_inc(g["n_pT_dve"], 1)
                                if t < TILES - 1:
                                    minus_max(u0 + t + 1, s)
                            head_out(u0 + t, t, 2, 0.0)

                    norm("lin", to_z)
                    for s in range(SLOTS):
                        dve.wait_ge(g["n_proj"], nth(0, s))
                        dve.tensor_scalar(A[s][:, :], bank(s, 0), 0.0, None, ALU.max).then_inc(g["n_q"], 1)
                        dve.wait_ge(g["n_q"], nth(0, s))
                        spread(dve, s, 1, A[s], 1024).then_inc(g["bd_dve"], 1)

                    def masked(t):
                        for s in range(SLOTS):
                            dve.wait_ge(g["n_s"], nth(t, s))
                            dve.tensor_tensor(P[s][:, 1024 * (t % 2):1024 * (t % 2) + 1024].rearrange("p (n t) -> p n t", t=SEQ),
                                              bank(s, 2 * (t % 2), 2).rearrange("p (n t) -> p n t", t=SEQ),
                                              over(C("causal_T"), 1, [128, 16, SEQ]), ALU.mult).then_inc(g["n_sub"], 1)

                    masked(0)
                    masked(1)
                    for t in range(TILES):
                        head_out(t, t, 2 * (t % 2), 1e-5)
                        if t + 2 < TILES:
                            masked(t + 2)
                    add_to_x(g["n_out"], 0, 2)

                    def rms(n, gain):
                        for s in range(SLOTS):
                            dve.wait_ge(g["rms_rstd"], nth(n, s))
                            dve.scalar_tensor_tensor(A[s][:, :], Z[s][:, :], gain, tmp(s, 1), ALU.mult, ALU.mult).then_inc(g["rms_done"], 1)

                    norm("moe1", to_z)
                    rms(0, V("g1"))
                    for s in range(SLOTS):
                        dve.wait_ge(g["n_proj"], nth(1, s))
                        for k in range(4):
                            m = dve.tensor_tensor(seqs(tmp(s, k)), seqs(bank(s, k)),
                                                  over(C("sin" if k % 2 else "cos"), 1, [128, GB, SEQ]), ALU.mult)
                        m.then_inc(g["rope_dve"], 1)
                        dve.wait_ge(g["rope_dve"], nth(0, s))
                        for p0, p1, c, hf in QUADRANTS:
                            m = dve.tensor_tensor(k_part(s, p0, p1, hf), parity(tmp(s, 2)[p0:p1, :], c),
                                                  parity(tmp(s, 3)[p0:p1, :], c), ALU.add)
                        m.then_inc(g["rope"], 1)
                        dve.wait_ge(g["rope"], nth(0, s))
                        spread_pair(dve, s, 0).then_inc(g["bd_dve"], 1)
                    softmax_heads(4, 0)
                    for s in range(SLOTS):
                        dve.wait_ge(g["n_out"], nth(1, s))
                        dve.tensor_tensor(Z[s][:, :], bank(s, 2), Z[s][:, :], ALU.add).then_inc(g["y_ready"], 1)
                    rms(1, V("g2"))
                    router(1, MOE1_E, 2)
                    top2_weights(1, MOE1_E)
                    for s in range(SLOTS):
                        for e in range(MOE1_E):
                            dve.wait_ge(g["m1_bc"], MOE1_E * s + e + 1)
                            m = dve.tensor_tensor(big[s][:, BANK * e:BANK * e + BANK], A[s][:, :], bank(s, e), ALU.mult)
                        m.then_inc(g["m1_x"], 1)
                    for k in range(MOE1_K):
                        for s in range(SLOTS):
                            dve.wait_ge(g["m1_t"], nth(k, s))
                            m = dve.scalar_tensor_tensor(tmp(s, k % 2), P[s][:, 512 * (k % 2):512 * (k % 2) + 512], 1.0,
                                                         bank(s, H3[2 * k % 3]), ALU.add, ALU.mult)
                        link(m)
                        for s in range(SLOTS):
                            dve.wait_ge(g["m1_b"], nth(k, s))
                            dve.scalar_tensor_tensor(P[s][:, 1024 + 512 * (k % 2):1536 + 512 * (k % 2)], tmp(s, k % 2), 0.5,
                                                     bank(s, H3[(2 * k + 1) % 3]), ALU.mult, ALU.mult).then_inc(g["m1_g"], 1)
                    for s in range(SLOTS):
                        dve.wait_ge(g["m1_out"], nth(0, s))
                        dve.wait_ge(g["m1_xz"], nth(0, s))
                        dve.tensor_tensor(X[s][:, :], bank(s, 2), X[s][:, :], ALU.add).then_inc(g["x_added"], 1)

                    norm("x2", to_z)
                    kv_context("x2", "gm", "bm")
                    norm("lat2", lambda s: A[s][:, :])
                    kv_latents(1, "lat2", "gl", "bl")
                    heads(2, 8.0, False, 0)

                    norm("loc", to_z)
                    for s in range(SLOTS):
                        dve.wait_ge(g["n_proj"], nth(2, s))
                        dve.wait_ge(g["q_zero"], nth(1, s))
                        for p0, p1, c, hf in QUADRANTS:
                            m = dve.tensor_scalar(q_part(s, p0, p1, c, hf), parity(bank(s, 0, 1, p0, p1), c),
                                                  V("bqk_turned" if c else "bqkv", 0)[p0:p1, :], None, ALU.add)
                        m.then_inc(g["n_q"], 1)
                        dve.wait_ge(g["n_k"], nth(1, s))
                        spread_pair(dve, s, 0).then_inc(g["bd_dve"], 1)
                    softmax_heads(8, 4)
                    add_to_x(g["n_out"], 2, 2, V("bo2"))

                    def top1_experts(layer):
                        for e in range(EXPERTS):
                            n = layer * EXPERTS + e
                            for s in range(SLOTS):
                                dve.wait_ge(g["m2_act"], nth(n, s))
                                dve.wait_ge(g["m2_mask"], nth(n, s))
                                dve.tensor_tensor(P[s][:, 1024 + 512 * (e % 2):1536 + 512 * (e % 2)],
                                                  P[s][:, 512 * (e % 2):512 * (e % 2) + 512], bank(s, 1), ALU.mult).then_inc(g["m2_m"], 1)

                    norm("moe2", to_z)
                    router(2, EXPERTS, 1)
                    for s in range(SLOTS):
                        dve.tensor_copy(ohb[s][:, :].rearrange("p (t e) -> p t e", e=8), route(s, OH, 8)).then_inc(g["onehot"], 1)
                    for s in range(SLOTS):
                        dve.wait_ge(g["u_exp"], nth(2, s))
                    each(lambda s: dve.tensor_reduce(small[s][:, DN:DN + 4], route(s, U, 8), AX.X, ALU.add))
                    each(lambda s: dve.reciprocal(small[s][:, DN + 8:DN + 12], small[s][:, DN:DN + 4]))
                    for s in range(SLOTS):
                        dve.wait_ge(g["cum_ps"], nth(0, s))
                        link(dve.tensor_tensor(comb(s, G8), ps[s][:, BANK:BANK + 32].rearrange("p (t e) -> p t e", e=8),
                                               over(count[:, :], 1, [128, TILES, 8]), ALU.add))
                        link(dve.tensor_tensor(count[:, :], count[:, :], ps[s][:, BANK + 32:BANK + 40], ALU.add))
                        link(dve.scalar_tensor_tensor(comb(s, CW), comb(s, G8), float(CAPACITY), route(s, OH, 8), ALU.is_lt, ALU.mult))
                        dve.tensor_copy(rep16(s, CW16), times16(comb(s, CW)))
                        dve.tensor_tensor(rep16(s, G16), times16(comb(s, CW)), times16(over(small[s][:, DN + 8:DN + 12], 2, [128, TILES, 8])), ALU.mult)\
                           .then_inc(g["comb"], 1)
                    for s in range(SLOTS):
                        dve.wait_ge(g["g_sb"], nth(0, s))
                        dve.tensor_tensor(A[s][:, :], Z[s][:, :], tmp(s, 0), ALU.mult).then_inc(g["xg"], 1)
                    top1_experts(0)
                    for s in range(SLOTS):
                        dve.wait_ge(g["m2_out"], nth(0, s))
                        m = dve.tensor_tensor(A[s][:, :], tmp(s, 0), bank(s, 2), ALU.mult)
                    link(m)
                    for s in range(SLOTS):
                        dve.tensor_tensor(X[s][:, :], X[s][:, :], A[s][:, :], ALU.add).then_inc(g["x_added"], 1)

                    for s in range(SLOTS):
                        dve.tensor_reduce(small[s][:, 0:8], ctxT[s][:, :].rearrange("p (b k) -> p b k", k=CTX), AX.X, ALU.add)\
                           .then_inc(g["x3_sum"], 1)
                    norm("x3", to_z)
                    for s in range(SLOTS):
                        dve.wait_ge(g["x3_ctx"], nth(0, s))
                        link(dve.tensor_scalar(small[s][:, 8:16], ps[s][:, BANK:BANK + GB], 1.0 / CTX, V("b3"), ALU.mult, ALU.add))
                        link(dve.tensor_tensor(seqs(X[s][:, :]), seqs(X[s][:, :]), over(small[s][:, 8:16], 2, [128, GB, SEQ]), ALU.add))
                        dve.wait_ge(g["x3_ps"], nth(0, s))
                        dve.tensor_tensor(X[s][:, :], X[s][:, :], bank(s, 0), ALU.add).then_inc(g["x_added"], 1)

                    norm("ssm", to_z)

                    def silu(s, k):
                        dve.wait_ge(g["ssm_t"], nth_half(0, s, k))
                        dve.scalar_tensor_tensor(P[s][:, 1024 + GT * k:1024 + GT * k + GT], P[s][:, GT * k:GT * k + GT], 1.0,
                                                 big[s][:, 2048 + GT * k:2048 + GT * k + GT], ALU.add, ALU.mult)\
                           .then_inc(g["ssm_x"], 1)

                    def state(s):
                        dve.wait_ge(g["ssm_u"], nth(0, s))
                        link(dve.tensor_scalar(tmp(s, 0), bank(s, 0), 0.05, None, ALU.mult))
                        dve.wait_ge(g["ssm_decay"], nth(0, s))
                        dve.tensor_tensor_scan(tmp(s, 1), A[s][:, :], tmp(s, 0), 0.0,
                                               ALU.mult, ALU.add).then_inc(g["ssm_h"], 1)

                    for s in range(SLOTS):
                        dve.wait_ge(g["ssm_xp"], nth(0, s))
                        dve.wait_ge(g["ssm_tap"], nth(0, s))
                        for tap in range(3):
                            for k in range(2):
                                acc = seqs(big[s][:, 2048 + GT * k:2048 + GT * k + GT])
                                m = dve.scalar_tensor_tensor(acc, padded(s)[:, GB * k:GB * k + GB, tap:tap + SEQ],
                                                             V("conv_w", 4 * k + tap), acc, ALU.mult, ALU.add)
                                if tap == 2:
                                    m.then_inc(g["ssm_conv"], 1)
                            if tap < 2:
                                link(m)
                    for k in range(2):
                        silu(0, k)
                    silu(1, 0)
                    state(0)
                    silu(1, 1)
                    for s in range(SLOTS):
                        dve.wait_ge(g["ssm_zt"], nth(0, s))
                        m = dve.scalar_tensor_tensor(tmp(s, 2, 2), tmp(s, 2, 2), 1.0, bank(s, 2, 2), ALU.add, ALU.mult)
                        if s == 0:
                            state(1)
                    link(m)
                    for s in range(SLOTS):
                        dve.wait_ge(g["ssm_y"], nth(0, s))
                        dve.scalar_tensor_tensor(P[s][:, 0:1024], tmp(s, 2, 2), 0.5, bank(s, 0, 2), ALU.mult, ALU.mult)\
                           .then_inc(g["ssm_g"], 1)
                    add_to_x(g["ssm_out"], 0, 2)

                    norm("moe3", to_z)
                    router(3, EXPERTS, 1)
                    for s in range(SLOTS):
                        dve.tensor_copy(rep16(s, CW16), times16(route(s, OH, 8))).then_inc(g["comb"], 1)
                    top1_experts(1)
                    add_to_x(g["m2_out"], 1, 2)

                @block.gpsimd
                def _(pool):
                    def heads(gi):
                        for b in range(GB):
                            u = gi * GB + b
                            for s in range(SLOTS):
                                for hf in range(2):
                                    pool.wait_ge(g["rsum"], nth_half(u, s, hf))
                                    view = P[s][:, 2 * KEYS * hf:2 * KEYS * hf + 2 * KEYS].rearrange("p (a k) -> p a k", k=KEYS)
                                    pool.tensor_tensor(view, view, over(small[s][:, 12 + 2 * hf:14 + 2 * hf], 2, [128, 2, KEYS]),
                                                       ALU.mult).then_inc(g["p_ready"], 1)

                    def pad(n, name):
                        for s in range(SLOTS):
                            pool.wait_ge(g["normed"], nth(LN[name], s))
                            pool.memset(T[s][64:128, GC:2 * GC], 0.0)
                            pool.memset(P[s][64:128, 1536:2048], 0.0).then_inc(g["kv_pad"], 1)

                    pad(0, "lat0")
                    heads(0)
                    heads(1)

                    links = [0]

                    def link(ins):
                        links[0] += 1
                        ins.then_inc(g["pool_chain"], 1)
                        pool.wait_ge(g["pool_chain"], links[0])

                    for s in range(SLOTS):
                        pool.wait_ge(g["rnn_tanh"], nth(0, s))
                        pool.memset(tmp(s, 2, 2).rearrange("p (n t) -> p n t", t=SEQ)[:, :, 0:1], 0.0)
                        pool.tensor_scalar(seqs(tmp(s, 2))[:, :, 1:SEQ], seqs(tmp(s, 0))[:, :, 1:SEQ], -0.5, 0.5,
                                           ALU.mult, ALU.add).then_inc(g["rnn_keep0"], 1)

                    for s in range(SLOTS):
                        pool.wait_ge(g["x1_sum"], nth(0, s))
                        view = P[s][:, 0:512].rearrange("p (t k) -> p t k", k=CTX)
                        pool.tensor_tensor(view, view, over(small[s][:, 24:28], 2, [128, TILES, CTX]), ALU.mult).then_inc(g["x1_p"], 1)

                    def spread_tiles(u0, src):
                        for t in range(TILES):
                            for s in range(SLOTS):
                                if t >= 2:
                                    pool.wait_ge(g["n_s"], nth(u0 + t - 2, s))
                                for bb in range(2 if t else 1):
                                    m = spread(pool, s, 2 * t + bb, src(s), 2048 * (t % 2) + 1024 * bb)
                                m.then_inc(g["bd_ready"], 1)

                    def zero_queries(s):
                        pool.memset(q_pairs(s), 0.0).then_inc(g["q_zero"], 1)

                    def spread_pairs(u0, k_ready, nk):
                        for t in range(1, TILES):
                            for s in range(SLOTS):
                                if t == 1:
                                    pool.wait_ge(k_ready, nth(nk, s))
                                else:
                                    pool.wait_ge(g["n_s"], nth(u0 + t - 2, s))
                                spread_pair(pool, s, t).then_inc(g["bd_ready"], 1)

                    for s in range(SLOTS):
                        pool.wait_ge(g["n_q"], nth(0, s))
                    spread_tiles(0, lambda s: A[s])

                    for s in range(SLOTS):
                        pool.wait_ge(g["n_s"], nth(TILES - 1, s))
                        zero_queries(s)
                    pool.wait_ge(g["q_zero"], nth(0, SLOTS - 1))
                    for s in range(SLOTS):
                        pool.wait_ge(g["rope_dve"], nth(0, s))
                        for n, (p0, p1, c, hf) in enumerate(QUADRANTS):
                            pool.tensor_tensor(q_part(s, p0, p1, c, hf), parity(tmp(s, 0)[p0:p1, :], c),
                                               parity(tmp(s, 1)[p0:p1, :], c), ALU.add).then_inc(g["q_rope"], 1)
                            pool.wait_ge(g["q_rope"], len(QUADRANTS) * s + n + 1)
                    spread_pairs(4, g["rope"], 0)
                    for s in range(SLOTS):
                        pool.wait_ge(g["y_ready"], nth(0, s))
                        pool.tensor_tensor(X[s][:, :], X[s][:, :], Z[s][:, :], ALU.add).then_inc(g["m1_xz"], 1)

                    pad(1, "lat2")
                    heads(2)

                    for s in range(SLOTS):
                        pool.wait_ge(g["x_added"], nth(7, s))
                        zero_queries(s)
                    spread_pairs(8, g["n_k"], 1)

                    for s in range(SLOTS):
                        pool.wait_ge(g["normed"], nth(LN["ssm"], s))
                        pool.memset(padded(s)[:, :, 0:3], 0.0).then_inc(g["ssm_pad"], 1)
                    pool.wait_ge(g["ssm_pad"], nth(0, SLOTS - 1))
                    for s in range(SLOTS):
                        pool.memset(seqs(A[s][:, :])[:, :, 1:SEQ], 0.9)
                        pool.memset(seqs(A[s][:, :])[:, :, 0:1], 0.0).then_inc(g["ssm_decay"], 1)

            nc.all_engine_barrier(sems_to_clear=clear)

        with nc.Block() as block:
            @block.sync
            def _(sp):
                sp.wait_ge(x_free, 16 * SLOTS * PASSES + 16)
                for s in range(SLOTS):
                    sp.wait_ge(ctx_loaded[s], 16 * (PASSES + 1))


def pack(i):
    def heads_T(w):
        return w.T.reshape(-1, 128, 128).transpose(1, 0, 2).reshape(128, -1)

    def rows_of(w, n):
        return w.reshape(n, 128, -1).transpose(1, 0, 2).reshape(128, -1)

    def at(p, a):
        out = np.zeros((128, a.shape[-1]), np.float32)
        out[:p] = a
        return out

    def per_partition(v, n):
        return v.reshape(n, 128).T

    half = HD // 2
    swap = np.arange(D).reshape(-1, HD)
    swap = np.concatenate([swap[:, half:], swap[:, :half]], axis=1).ravel()
    kv_rep = np.arange(32).reshape(4, 1, HD).repeat(4, axis=1).ravel()
    wkv0, wkv2, wqkv = i["L0_xattn_Wkv"], i["L2_xattn_Wkv"], i["L1_attn_wqkv"]
    lq, bqkv = i["L2_attn_w_qkv"], i["L2_attn_b_qkv"]
    wk_rep = i["L1_ffn_wk"][:, kv_rep]
    fold = dict(q0T=heads_T(i["L0_xattn_Wq"]), k0T=heads_T(wkv0[:, :1024]), v0T=heads_T(wkv0[:, 1024:]),
                o0=rows_of(i["L0_xattn_Wout"], 8), q2T=heads_T(i["L2_xattn_Wq"]), k2T=heads_T(wkv2[:, :512]),
                v2T=heads_T(wkv2[:, 512:]), o2=rows_of(i["L2_xattn_Wout"], 4))
    one = lambda n: i[n].reshape(128, 1)
    cols = dict(lmw=one("L0_xattn_ln_media_w"), lmb=one("L0_xattn_ln_media_b"), llw=one("L0_xattn_ln_lat_w"),
                llb=one("L0_xattn_ln_lat_b"), bout0=one("L0_xattn_bout"), bq0=per_partition(i["L0_xattn_bq"], 8),
                bv0=per_partition(i["L0_xattn_bkv"][1024:], 8), base_b=one("L0_ffn_base_b"), bq1=one("L1_xattn_bq"),
                bk1=one("L1_xattn_bk"), bv1=one("L1_xattn_bv"), g1=one("L1_ffn_g1"), g2=one("L1_ffn_g2"),
                gm=one("L2_xattn_gm"), bm=one("L2_xattn_bm"), gl=one("L2_xattn_gl"), bl=one("L2_xattn_bl"),
                bqkv=per_partition(bqkv, 3), bqk_turned=np.roll(per_partition(bqkv, 3)[:, 0:2], 64, axis=0), bo2=one("L2_attn_b_out"), moe2_b1=i["L2_ffn_b1"].T, b3=one("L3_xattn_b"),
                conv_w=i["L3_attn_conv_w"].reshape(2, 128, 4).transpose(1, 0, 2).reshape(128, 8),
                conv_b=per_partition(i["L3_attn_conv_b"], 2), moe3_b1=i["L3_ffn_b1"].T,
                br=at(1, i["L2_ffn_br"]), bg=at(1, i["L3_ffn_bg"]))
    wide = lambda w: np.concatenate([w, w[:, :64]], axis=1)
    experts = lambda w: w.transpose(1, 0, 2).reshape(128, -1)
    wts = dict(hg=i["L0_attn_W_hg"], rnn_out=rows_of(i["L0_attn_W_out"], 2), base=i["L0_ffn_base_w"].T,
               gate0=i["L0_ffn_gate_w"].T, loraA=i["L0_ffn_lora_A"].reshape(128, 128).T,
               loraB=i["L0_ffn_lora_B"].transpose(0, 2, 1).reshape(128, 128),
               q1=i["L1_xattn_Wq"], k1=i["L1_xattn_Wk"], v1=i["L1_xattn_Wv"],
               lin_q=wqkv[:, :128], lin_k=wqkv[:, 128:256], lin_v=wqkv[:, 256:], lin_o=i["L1_attn_wo"],
               rq=wide(i["L1_ffn_wq"]), rqp=wide(i["L1_ffn_wq"][:, swap]), rk=wide(wk_rep), rkp=wide(wk_rep[:, swap]),
               rv=i["L1_ffn_wv"][:, kv_rep], ro=i["L1_ffn_wo"], gate1=i["L1_ffn_gate"],
               w1=experts(i["L1_ffn_w1"]), w3=experts(i["L1_ffn_w3"]), w2=rows_of(i["L1_ffn_w2"].reshape(-1, 128), 12),
               loc_q=wide(lq[:, :128]), loc_k=wide(lq[:, 128:256]), loc_v=lq[:, 256:], loc_o=i["L2_attn_w_out"],
               moe2_r=i["L2_ffn_Wr"], moe2_w1=experts(i["L2_ffn_W1"]), moe2_w2=experts(i["L2_ffn_W2"]),
               moe2_b2=at(8, i["L2_ffn_b2"]), x3a=i["L3_xattn_W"][:, :128].T, x3b=i["L3_xattn_W"][:, 128:].T,
               ssm_in=i["L3_attn_w_in"], ssm_B=rows_of(np.tile(i["L3_attn_w_B"], 8), 2), ssm_C=at(16, i["L3_attn_w_C"]),
               ssm_out=rows_of(i["L3_attn_w_out"], 2), moe3_r=i["L3_ffn_Wg"], moe3_w1=experts(i["L3_ffn_W1"]),
               moe3_w2=experts(i["L3_ffn_W2"]), moe3_b2=at(8, i["L3_ffn_b2"]))
    return [np.concatenate([parts[n] for n, _ in table], axis=1)
            for table, parts in ((FOLD, fold), (COLUMNS, cols), (WEIGHTS, wts))]


def shape_constants():
    p = np.arange(128)
    half = HD // 2
    inv = (np.float32(1.0) / np.float32(10000.0) ** (np.arange(0, HD, 2, dtype=np.float32) / np.float32(HD))).astype(np.float32)
    angle = np.arange(SEQ, dtype=np.float32)[None, :] * inv[p % half][:, None]
    sign = np.where(p % HD < half, -1.0, 1.0)[:, None]
    q, k = p[:, None] % SEQ, np.arange(SEQ)[None, :]
    c = dict(ident=np.eye(128), center=np.eye(128) - 1.0 / 128, mean=np.full((128, 128), 1.0 / 128),
             hmask=(p[:, None] // HD == np.arange(NH)[None, :]), hmask8=(p[:, None] % 64 // HD == np.arange(NH // 2)[None, :]), cos=np.cos(angle), sin=np.sin(angle) * sign,
             causal_add=np.where(k <= q, 0.0, NEG), causal_T=(k >= q), upto=(p[:, None] <= p[None, :]),
             iota=np.broadcast_to(np.arange(16), (128, 16)), lora_sel=(p[:, None] == p[None, :] // LORA_R),
             ones8=np.broadcast_to(p[:, None] < 8, (128, 128)))
    return np.concatenate([np.asarray(c[n], np.float32) for n, _ in CONSTS], axis=1)


def kernel(**inputs):
    import concourse.bacc as bacc
    from concourse.bass_utils import run_bass_kernel_spmd

    i = {k: np.asarray(v) for k, v in inputs.items()}
    fold, cols, wts = pack(i)
    ctx = np.pad(i["ctx_1024"].reshape(BATCH * CTX, D).T, ((0, 0), (0, SLOTS * GC)))
    arrays = {"x_dram": i["x"].reshape(BATCH * SEQ, D).T, "ctx_dram": ctx,
              "fold_dram": fold, "cols_dram": cols, "weights_dram": wts, "consts_dram": shape_constants()}
    arrays = {k: np.ascontiguousarray(v) for k, v in arrays.items()}
    nc = bacc.Bacc("TRN2", target_bir_lowering=False, num_devices=1)
    f32 = mybir.dt.float32
    args = [nc.dram_tensor(k, v.shape, f32, kind="ExternalInput").ap() for k, v in arrays.items()]
    out = nc.dram_tensor("out_dram", (D, BATCH * SEQ), f32, kind="ExternalOutput").ap()
    build(nc, *args, out)
    r = run_bass_kernel_spmd(nc, [arrays], core_ids=[0])
    return np.ascontiguousarray(r.results[0]["out_dram"].T).reshape(BATCH, SEQ, D)
```
